# Optimizing a Trainium2 kernel written in Bass

```python
import numpy as np
import jax
import jax.numpy as jnp

def _softmax(x, axis=-1):
    return jax.nn.softmax(x, axis=axis)

def _gelu(x):
    return jax.nn.gelu(x, approximate=True)

def _silu(x):
    return jax.nn.silu(x)

def _sigmoid(x):
    return jax.nn.sigmoid(x)

def _layernorm(x, axis=-1, eps=1e-05):
    m = jnp.mean(x, axis=axis, keepdims=True)
    v = jnp.var(x, axis=axis, keepdims=True)
    return (x - m) / jnp.sqrt(v + eps)

def _scatter_add(tgt, idx, src, axis=0):
    return tgt.at[idx].add(src)

def _segment_sum(src, seg, n):
    return jax.ops.segment_sum(src, seg, n)
kernel_name = 'mk_vit_tower_d1_tok_img768_r4_225d26'

def setup_inputs(seed: int=0):
    np.random.seed(seed)
    _w = jnp.asarray

    def _rec_inputs():
        import jax
        import jax.numpy as jnp
        _rk = jax.random.key(seed)
        x = -0.00016672 + 0.999947 * jax.random.normal(jax.random.fold_in(_rk, 1), (64, 3, 224, 224), jnp.float32)
        return x
    x = _rec_inputs()

    def _L0_tok_setup():
        import jax, jax.numpy as jnp
        import numpy as np
        P = 16
        EMBED = 192
        EPS = 1e-05

        def _patchify(x):
            N, C, H, W = x.shape
            x = x.reshape(N, C, H // P, P, W // P, P)
            x = x.transpose(0, 2, 4, 1, 3, 5)
            return x.reshape(N, H // P * (W // P), C * P * P)
        key = jax.random.key(seed)
        k1, k2, k3 = jax.random.split(key, 3)
        in_dim = P * P * 3
        x = jax.random.normal(k1, (64, 3, 96, 96), dtype=jnp.float32)
        bound = 1.0 / np.sqrt(in_dim)
        W = jax.random.uniform(k2, (EMBED, in_dim), dtype=jnp.float32, minval=-bound, maxval=bound)
        b = jax.random.uniform(k3, (EMBED,), dtype=jnp.float32, minval=-bound, maxval=bound)
        ln_w = jnp.ones((EMBED,), dtype=jnp.float32)
        ln_b = jnp.zeros((EMBED,), dtype=jnp.float32)
        return {'x': x, 'W': W, 'b': b, 'ln_w': ln_w, 'ln_b': ln_b}
    _L0_tok_all = _L0_tok_setup()
    _L0_tok_in = {k: v for k, v in _L0_tok_all.items() if k in ('W', 'b', 'ln_w', 'ln_b')}
    del _L0_tok_all

    def _L0_attn_setup():
        import jax, jax.numpy as jnp
        import numpy as np
        LEVEL = 8
        NUM_HEADS = 12
        QN_SYM = float(-(LEVEL // 2))
        QP_SYM = float(LEVEL // 2 - 1)
        QN_ASYM = 0.0
        QP_ASYM = float(LEVEL - 1)

        def fake_quant(x, s, qn, qp):
            xc = jnp.clip(x / s, qn, qp)
            xr = xc + jax.lax.stop_gradient(jnp.round(xc) - xc)
            return s * xr
        key = jax.random.key(seed)
        k0, k1, k2 = jax.random.split(key, 3)
        B, N, C = (4, 512, 192)
        x = jax.random.normal(k0, (B, N, C), dtype=jnp.float32)
        Wqkv = jax.random.normal(k1, (3 * C, C), dtype=jnp.float32) * C ** (-0.5)
        Wproj = jax.random.normal(k2, (C, C), dtype=jnp.float32) * C ** (-0.5)
        bproj = jnp.zeros((C,), dtype=jnp.float32)
        s_q = jnp.asarray(1.0, dtype=jnp.float32)
        s_k = jnp.asarray(1.0, dtype=jnp.float32)
        s_v = jnp.asarray(1.0, dtype=jnp.float32)
        s_attn = jnp.asarray(1.0 / QP_ASYM, dtype=jnp.float32)
        s_after = jnp.asarray(1.0, dtype=jnp.float32)
        return {'x': x, 'Wqkv': Wqkv, 'Wproj': Wproj, 'bproj': bproj, 's_q': s_q, 's_k': s_k, 's_v': s_v, 's_attn': s_attn, 's_after': s_after}
    _L0_attn_all = _L0_attn_setup()
    _L0_attn_in = {k: v for k, v in _L0_attn_all.items() if k in ('Wqkv', 'Wproj', 'bproj', 's_q', 's_k', 's_v', 's_attn', 's_after')}
    del _L0_attn_all

    def _L0_ffn_setup():
        import jax, jax.numpy as jnp
        import numpy as np
        H = 192
        R = 64
        E = 8
        B, S = (8, 512)
        key = jax.random.key(seed)
        ks = jax.random.split(key, 10)
        s_in = 1.0 / np.sqrt(H)
        s_r = 1.0 / np.sqrt(R)
        return {'x': jax.random.normal(ks[0], (B, S, H), dtype=jnp.float32), 'enc_w': jax.random.uniform(ks[1], (H, R), jnp.float32, -s_in, s_in), 'enc_b': jax.random.uniform(ks[2], (R,), jnp.float32, -s_in, s_in), 'sw_w': jax.random.uniform(ks[3], (R, E), jnp.float32, -s_r, s_r), 'sw_b': jax.random.uniform(ks[4], (E,), jnp.float32, -s_r, s_r), 'w1': jax.random.uniform(ks[5], (E, H, R), jnp.float32, -s_in, s_in), 'b1': jax.random.uniform(ks[6], (E, R), jnp.float32, -s_in, s_in), 'w2': jax.random.uniform(ks[7], (E, R, H), jnp.float32, -s_r, s_r), 'b2': jax.random.uniform(ks[8], (E, H), jnp.float32, -s_r, s_r)}
    _L0_ffn_all = _L0_ffn_setup()
    _L0_ffn_in = {k: v for k, v in _L0_ffn_all.items() if k in ('enc_w', 'enc_b', 'sw_w', 'sw_b', 'w1', 'b1', 'w2', 'b2')}
    del _L0_ffn_all
    return {'x': x, 'L0_tok_W': _L0_tok_in['W'], 'L0_tok_b': _L0_tok_in['b'], 'L0_tok_ln_w': _L0_tok_in['ln_w'], 'L0_tok_ln_b': _L0_tok_in['ln_b'], 'L0_attn_Wqkv': _L0_attn_in['Wqkv'], 'L0_attn_Wproj': _L0_attn_in['Wproj'], 'L0_attn_bproj': _L0_attn_in['bproj'], 'L0_attn_s_q': _L0_attn_in['s_q'], 'L0_attn_s_k': _L0_attn_in['s_k'], 'L0_attn_s_v': _L0_attn_in['s_v'], 'L0_attn_s_attn': _L0_attn_in['s_attn'], 'L0_attn_s_after': _L0_attn_in['s_after'], 'L0_ffn_enc_w': _L0_ffn_in['enc_w'], 'L0_ffn_enc_b': _L0_ffn_in['enc_b'], 'L0_ffn_sw_w': _L0_ffn_in['sw_w'], 'L0_ffn_sw_b': _L0_ffn_in['sw_b'], 'L0_ffn_w1': _L0_ffn_in['w1'], 'L0_ffn_b1': _L0_ffn_in['b1'], 'L0_ffn_w2': _L0_ffn_in['w2'], 'L0_ffn_b2': _L0_ffn_in['b2']}

def reference(x, L0_tok_W, L0_tok_b, L0_tok_ln_w, L0_tok_ln_b, L0_attn_Wqkv, L0_attn_Wproj, L0_attn_bproj, L0_attn_s_q, L0_attn_s_k, L0_attn_s_v, L0_attn_s_attn, L0_attn_s_after, L0_ffn_enc_w, L0_ffn_enc_b, L0_ffn_sw_w, L0_ffn_sw_b, L0_ffn_w1, L0_ffn_b1, L0_ffn_w2, L0_ffn_b2):
    import jax
    import jax.numpy as jnp

    def _L0_tok_ref(x, W, b, ln_w, ln_b):
        import jax, jax.numpy as jnp
        import numpy as np
        P = 16
        EMBED = 192
        EPS = 1e-05

        def _patchify(x):
            N, C, H, W = x.shape
            x = x.reshape(N, C, H // P, P, W // P, P)
            x = x.transpose(0, 2, 4, 1, 3, 5)
            return x.reshape(N, H // P * (W // P), C * P * P)
        patches = _patchify(x)
        y = jnp.einsum('nsi,oi->nso', patches, W) + b
        mu = jnp.mean(y, axis=-1, keepdims=True)
        var = jnp.mean(jnp.square(y - mu), axis=-1, keepdims=True)
        return (y - mu) / jnp.sqrt(var + EPS) * ln_w + ln_b

    def _L0_attn_ref(x, Wqkv, Wproj, bproj, s_q, s_k, s_v, s_attn, s_after):
        import jax, jax.numpy as jnp
        import numpy as np
        LEVEL = 8
        NUM_HEADS = 12
        QN_SYM = float(-(LEVEL // 2))
        QP_SYM = float(LEVEL // 2 - 1)
        QN_ASYM = 0.0
        QP_ASYM = float(LEVEL - 1)

        def fake_quant(x, s, qn, qp):
            xc = jnp.clip(x / s, qn, qp)
            xr = xc + jax.lax.stop_gradient(jnp.round(xc) - xc)
            return s * xr
        B, N, C = x.shape
        H = NUM_HEADS
        D = C // H
        scale = D ** (-0.5)
        qkv = jnp.einsum('bnc,dc->bnd', x, Wqkv).reshape(B, N, 3, H, D).transpose(2, 0, 3, 1, 4)
        q, k, v = (qkv[0], qkv[1], qkv[2])
        q = fake_quant(q, s_q, QN_SYM, QP_SYM) * scale
        k = fake_quant(k, s_k, QN_SYM, QP_SYM)
        v = fake_quant(v, s_v, QN_SYM, QP_SYM)
        attn = jnp.einsum('bhnd,bhmd->bhnm', q, k)
        attn = fake_quant(attn / N, s_attn, QN_ASYM, QP_ASYM)
        out = jnp.einsum('bhnm,bhmd->bhnd', attn, v)
        out = fake_quant(out, s_after, QN_SYM, QP_SYM)
        out = out.transpose(0, 2, 1, 3).reshape(B, N, C)
        return out @ Wproj.T + bproj

    def _L0_ffn_ref(x, enc_w, enc_b, sw_w, sw_b, w1, b1, w2, b2):
        import jax, jax.numpy as jnp
        import numpy as np
        H = 192
        R = 64
        E = 8
        B, S = (8, 512)
        b, s, d = x.shape
        xt = x.reshape(-1, d)
        x_enc = xt @ enc_w + enc_b
        route_prob = jax.nn.softmax(x_enc @ sw_w + sw_b, axis=-1)
        route_prob_max = jnp.max(route_prob, axis=-1)
        routes = jnp.argmax(route_prob, axis=-1)
        onehot = jax.nn.one_hot(routes, E, dtype=xt.dtype)
        h = jnp.einsum('td,edr->ter', xt, w1) + b1[None]
        h = jax.nn.gelu(h, approximate=False)
        h = h * onehot[..., None]
        out = jnp.einsum('ter,erd->td', h, w2) + onehot @ b2
        out = out * route_prob_max[:, None]
        return out.reshape(b, s, d)
    h = _L0_tok_ref(x, L0_tok_W, L0_tok_b, L0_tok_ln_w, L0_tok_ln_b)
    h = h + _L0_attn_ref(_layernorm(h, axis=-1), L0_attn_Wqkv, L0_attn_Wproj, L0_attn_bproj, L0_attn_s_q, L0_attn_s_k, L0_attn_s_v, L0_attn_s_attn, L0_attn_s_after)
    h = h + _L0_ffn_ref(_layernorm(h, axis=-1), L0_ffn_enc_w, L0_ffn_enc_b, L0_ffn_sw_w, L0_ffn_sw_b, L0_ffn_w1, L0_ffn_b1, L0_ffn_w2, L0_ffn_b2)
    return h

_drawn_inputs = setup_inputs


def setup_inputs(seed=0):
    import zlib

    import numpy as np

    out = dict(_drawn_inputs(seed))
    spreads = {'L0_tok_ln_w': (1.0, 0.2), 'L0_tok_ln_b': (0.0, 0.1), 'L0_attn_bproj': (0.0, 0.1)}
    factors = {'L0_ffn_enc_b': 8.0, 'L0_ffn_b1': 8.0, 'L0_ffn_b2': 4.28}
    for name, (base, spread) in spreads.items():
        noise = np.random.default_rng([zlib.crc32(name.encode()), seed]).standard_normal(out[name].shape)
        drawn = base * np.exp(spread * noise) if base else spread * noise
        out[name] = jnp.asarray(drawn.astype(out[name].dtype))
    for name, factor in factors.items():
        out[name] = (out[name] * factor).astype(out[name].dtype)
    return out
```

```python
import numpy as np
import concourse.bass as bass
import concourse.mybir as mybir
from contextlib import ExitStack

IMAGES, PATCH, GRID, EMBED, HEADS, EXPERTS, HIDDEN = 64, 16, 14, 192, 12, 8, 64
SEQ = GRID * GRID
FAN_IN = 3 * PATCH * PATCH
KC = FAN_IN // 128
GI = 4
GROUPS = IMAGES // GI
TOK = GI * SEQ
TT = 112
NT = TOK // TT
HALF = TOK // 2
KEYS = SEQ // 2
DH = EMBED // HEADS
PAIRS = HEADS // 2
SLOTS = GI * PAIRS
LO = EMBED - 128
FF = EXPERTS * HIDDEN
FC = FF // 128
EPS = 1e-5
MASKED = 2.0 ** 60
E4_STEP = 512.0

C_IDENT, C_RAMP, C_SEL = 0, TT, TT + EXPERTS
C_BOUND = C_SEL + FF
C_PART = C_BOUND + 4
C_FIRST = C_PART + 3
C_HALFNEG, C_E, C_EPS = (C_FIRST + TT + n for n in range(3))
C_ALL = C_EPS + 1


def constants():
    c = np.zeros((128, C_ALL), np.float32)
    c[:TT, C_IDENT:C_IDENT + TT] = np.eye(TT)
    c[:, C_RAMP:C_RAMP + EXPERTS] = EXPERTS - np.arange(EXPERTS)
    for e in range(EXPERTS):
        c[e, C_SEL + HIDDEN * e:C_SEL + HIDDEN * (e + 1)] = MASKED
    odd = (np.arange(128) // DH) % 2
    for n, (head, bound) in enumerate(((0, -4), (0, 3), (1, -4), (1, 3))):
        c[:, C_BOUND + n] = np.where(odd == head, bound, 0)
    for j in range(3):
        c[8 * j:8 * j + 8, C_PART + j] = 1
        c[8 * j, C_FIRST:C_FIRST + TT] = 1
    c[:, C_HALFNEG] = -0.5
    c[:, C_E] = np.e
    c[:, C_EPS] = EPS
    return c


class Group:

    def __init__(self, loop, offset, parity):
        self.loop, self.offset, self.parity = loop, offset, parity

    def count(self, per_group, k):
        return self.loop * per_group + (self.offset * per_group + k)


def stages(loop, offset, parity):
    found = []
    for back in range(3):
        n = offset - back
        there = not isinstance(loop, int) or 0 <= n < GROUPS
        found.append(Group(loop, n, (parity + back) % 2) if there else None)
    return found


def wait(eng, sem, value):
    if not isinstance(value, int) or value > 0:
        eng.wait_ge(sem, value)


LOOP_FROM, LOOP_TO = 4, 14


def passes(eng, body):
    for i in range(LOOP_FROM):
        body(*stages(0, i, i % 2))
    with eng.Fori(LOOP_FROM, LOOP_TO, 2) as i:
        body(*stages(i, 0, 0))
        body(*stages(i, 1, 1))
    for i in range(LOOP_TO, GROUPS + 2):
        body(*stages(0, i, i % 2))


EMBED_SPAN = [3, 3, 2, 3, 3, 2, 2]
EMBED_END = [sum(EMBED_SPAN[:t + 1]) - 1 for t in range(NT)]


def embeds_of(slot):
    for t, (span, end) in enumerate(zip(EMBED_SPAN, EMBED_END)):
        step = slot - (end + 1 - span)
        if 0 <= step < span:
            return [(t, j) for j in range(KC) if j * span // KC == step]
    return []


def at(slots, slot):
    return [t for t, s in enumerate(slots) if s == slot]


STATS1 = [s + 1 for s in EMBED_END]
NORM1 = [s + 2 for s in EMBED_END]
STATS2 = [s + 3 for s in EMBED_END]
NORM2 = [s + 4 for s in EMBED_END]
TURN2 = [s + 5 for s in EMBED_END]
ROWS_AT = {-1: [(0, 0), (1, 0)], 1: [(2, 0)], 4: [(0, 1)], 5: [(1, 1)], 6: [(2, 1)]}
VALUES_AT = {-1: [0], 2: [1], 7: [2], 8: [3]}
PROJ = [8, 14, 15, 20, 21, 26, 27]
RESID = [s + 1 for s in PROJ]
NORM3 = [s + 2 for s in PROJ]
TURN3 = [s + 3 for s in PROJ]
ROUTE = [1, 8]
TURN_LOGITS, CHOOSE, SPREAD = 9, 10, [11, 12]
UP = [13, 13, 14, 14, 15, 15, 16, 16]
SUMEXP = 18
DOWN = [17, 18, 19, 20, 21, 22, 23]
ROWS_ORDER = [x for s in sorted(set(ROWS_AT) | set(VALUES_AT))
              for x in [("rows",) + r for r in ROWS_AT.get(s, [])] + [("values", v) for v in VALUES_AT.get(s, [])]]
EVACS = len(ROWS_ORDER)


def evac_index(*what):
    return ROWS_ORDER.index(what)


def clips_until(m, half):
    order = [x[1:] for x in ROWS_ORDER if x[0] == "rows"]
    return order.index((m, half)) + 1


def by_scalar_engine(u):
    return u % 3 == 2


RELUS = sum(by_scalar_engine(u) for u in range(SLOTS))


def relus_until(u):
    return sum(by_scalar_engine(v) for v in range(u + 1))


def vit_tower_kernel(nc, x, tok_w, tok_b, ln_w, ln_b, w_qkv, w_proj, b_proj, s_q, s_k, s_v, s_attn,
                     s_after, enc_w, enc_b, sw_w, sw_b, w1, b1, w2, b2, const, out):
    f32, f32r, bf16 = mybir.dt.float32, mybir.dt.float32r, mybir.dt.bfloat16
    u8, i8, f8 = mybir.dt.uint8, mybir.dt.int8, mybir.dt.float8e4
    ALU, ACT, AX = mybir.AluOpType, mybir.ActivationFunctionType, mybir.AxisListType
    ctx = ExitStack()
    with ctx:
        def sb(name, shape, dtype):
            return ctx.enter_context(nc.sbuf_tensor(name, shape, dtype))

        def pb(name, shape):
            return ctx.enter_context(nc.psum_tensor(name, shape, f32))

        def sem(name):
            return ctx.enter_context(nc.semaphore(name))

        const_sb = sb("const_sb", [128, C_ALL], f32)
        we = sb("we", [128, KC, EMBED], f32)
        lnw = sb("lnw", [TT, EMBED], f32)
        lnb = sb("lnb", [TT, EMBED], f32)
        stage_a = sb("stage_a", [128, 576], f32)
        stage_b = sb("stage_b", [128, 576], f32)
        stage_c = sb("stage_c", [128, 576], f32)
        wq_hi_a = sb("wq_hi_a", [128, 576], f32r)
        wq_lo_a = sb("wq_lo_a", [128, 576], f32r)
        wq_hi_b = sb("wq_hi_b", [128, 576], f32r)
        wq_lo_b = sb("wq_lo_b", [128, 576], f32r)
        w1_hi_a = sb("w1_hi_a", [128, FF], f32r)
        w1_lo_a = sb("w1_lo_a", [128, FF], f32r)
        w1_hi_b = sb("w1_hi_b", [128, FF], f32r)
        w1_lo_b = sb("w1_lo_b", [128, FF], f32r)
        wr_hi_a = sb("wr_hi_a", [128, EXPERTS], f32r)
        wr_lo_a = sb("wr_lo_a", [128, EXPERTS], f32r)
        wr_hi_b = sb("wr_hi_b", [128, EXPERTS], f32r)
        wr_lo_b = sb("wr_lo_b", [128, EXPERTS], f32r)
        wr_f = sb("wr_f", [128, 2, EXPERTS], f32)
        encw = sb("encw", [HIDDEN, EMBED + LO], f32)
        encb = sb("encb", [HIDDEN, 1], f32)
        sww = sb("sww", [HIDDEN, EXPERTS], f32)
        swb = sb("swb", [EXPERTS, 1], f32)
        br = sb("br", [EXPERTS, 1], f32)
        w2_sb = sb("w2_sb", [128, FC, EMBED], f32)
        b1_sb = sb("b1_sb", [128, FC], f32)
        wp_a = sb("wp_a", [128, 3, EMBED], bf16)
        wp_b = sb("wp_b", [LO, 3, EMBED], bf16)
        rows24 = sb("rows24", [24, 3, EMBED], bf16)
        parts24 = sb("parts24", [24, 3, 3 * EMBED], bf16)
        first24 = sb("first24", [24, TT], bf16)
        sel = sb("sel", [EXPERTS, FF], bf16)
        ident_b = sb("ident_b", [TT, TT], bf16)
        scal = sb("scal", [128, 5], f32)
        rec = sb("rec", [128, 5], f32)
        inv_rows = sb("inv_rows", [128, 3], f32)
        c_prob = sb("c_prob", [128, 1], f32)
        c_out = sb("c_out", [128, 1], f32)
        tmp1 = sb("tmp1", [128, 2], f32)
        warm = sb("warm", [128, 1], f32)

        x_sb = sb("x_sb", [128, NT, KC, TT], f32)
        st1 = sb("st1", [TT, NT, 6], f32)
        mv1 = sb("mv1", [TT, NT, 2], f32)
        ve1 = sb("ve1", [TT, NT, 1], f32)
        rs1 = sb("rs1", [TT, NT, 1], f32)
        nb1 = sb("nb1", [TT, NT, 1], f32)
        st2 = sb("st2", [TT, NT, 6], f32)
        mv2 = sb("mv2", [TT, NT, 2], f32)
        ve2 = sb("ve2", [TT, NT, 1], f32)
        rs2 = sb("rs2", [TT, NT, 1], f32)
        st3 = sb("st3", [TT, NT, 6], f32)
        mv3 = sb("mv3", [TT, NT, 2], f32)
        ve3 = sb("ve3", [TT, NT, 1], f32)
        rs3 = sb("rs3", [TT, NT, 1], f32)
        y1 = sb("y1", [TT, 2, EMBED], f32)
        n1 = sb("n1", [TT, 2, EMBED], f32)
        m1 = sb("m1", [TT, 2, EMBED], f32)
        h0 = sb("h0", [TT, 2, NT, EMBED], f32)
        h1 = sb("h1", [TT, 2, NT, EMBED], f32)
        xn2 = sb("xn2", [TT, 2, EMBED], f32)
        xn3 = sb("xn3", [TT, 2, EMBED], f32)
        a_hi = sb("a_hi", [128, 2, TOK], f32r)
        a_lo = sb("a_lo", [128, 2, TOK], f32r)
        a_b = sb("a_b", [128, 2, TOK], f32r)
        f_hi = sb("f_hi", [128, 2, TOK], f32r)
        f_lo = sb("f_lo", [128, 2, TOK], f32r)
        f_b = sb("f_b", [128, 2, TOK], f32r)
        rows8 = sb("rows8", [128, 3, TOK], i8)
        q_a = sb("q_a", [128, TOK], bf16)
        q_b = sb("q_b", [LO, TOK], bf16)
        k_a = sb("k_a", [128, 2, TOK], bf16)
        k_b = sb("k_b", [LO, 2, TOK], bf16)
        v8 = sb("v8", [KEYS, GI, 2 * EMBED], i8)
        v_pad = sb("v_pad", [KEYS, 2 * GI, PAIRS, 2, 32], bf16)
        relu8 = sb("relu8", [KEYS, 2, 2 * SEQ], u8)
        prob = sb("prob", [KEYS, 2, 2, 2 * SEQ], u8)
        o8_a = sb("o8_a", [128, TOK], i8)
        o8_b = sb("o8_b", [LO, TOK], i8)
        o_a = sb("o_a", [128, TOK], bf16)
        o_b = sb("o_b", [LO, TOK], bf16)
        logits_t = sb("logits_t", [EXPERTS, TOK], f32)
        logit = sb("logit", [TT, NT, EXPERTS], f32)
        below = sb("below", [TT, NT, EXPERTS], f32)
        econst = sb("econst", [TT, NT, EXPERTS], f32)
        expd = sb("expd", [TT, NT, EXPERTS], f32)
        top = sb("top", [TT, NT], f32)
        score = sb("score", [TT, NT, EXPERTS], f32)
        score2 = sb("score2", [TT, NT, EXPERTS], f32)
        best = sb("best", [TT, NT], f32)
        onehot3 = sb("onehot3", [TT, NT, 24], bf16)
        sume = sb("sume", [TT, NT], f32)
        pmax = sb("pmax", [TT, NT], f32)
        one_t = sb("one_t", [24, TOK], bf16)
        off_t = sb("off_t", [EXPERTS, TOK], bf16)
        hid = sb("hid", [128, FC, TOK], f32)
        out_sb = sb("out_sb", [TT, 2, EMBED], f32)

        scores_ps = pb("scores_ps", [128, 2, 512])
        heads_ps = pb("heads_ps", [128, 512])
        embed_ps = pb("embed_ps", [128, 512])
        turn_ps = pb("turn_ps", [128, 512])
        wide_ps = pb("wide_ps", [128, 512])
        proj_ps = pb("proj_ps", [128, 512])
        route_ps = pb("route_ps", [128, 512])

        loaded = sem("loaded")
        set_dve = sem("set_dve")
        set_pe = sem("set_pe")
        set_pool = sem("set_pool")
        warmed = sem("warmed")
        x_in = [sem(f"x_in{t}") for t in range(NT)]
        embedded = sem("embedded")
        act_y = sem("act_y")
        dve_st1 = sem("dve_st1")
        dve_mv1 = sem("dve_mv1")
        pool_ve1 = sem("pool_ve1")
        pool_rs1 = sem("pool_rs1")
        dve_nb1 = sem("dve_nb1")
        act_n1 = sem("act_n1")
        pool_m1 = sem("pool_m1")
        pool_h0 = sem("pool_h0")
        dve_st2 = sem("dve_st2")
        dve_mv2 = sem("dve_mv2")
        pool_ve2 = sem("pool_ve2")
        pool_rs2 = sem("pool_rs2")
        dve_xn2 = sem("dve_xn2")
        turned = sem("turned")
        act_hi = sem("act_hi")
        dve_lo = sem("dve_lo")
        rows_made = sem("rows_made")
        rows_out = sem("rows_out")
        rows_clip = sem("rows_clip")
        v_clip = sem("v_clip")
        qk_made = sem("qk_made")
        act_relu = sem("act_relu")
        prob_out = sem("prob_out")
        av_made = sem("av_made")
        heads_out = sem("heads_out")
        heads_clip = sem("heads_clip")
        projected = sem("projected")
        dve_h1 = sem("dve_h1")
        dve_st3 = sem("dve_st3")
        dve_mv3 = sem("dve_mv3")
        pool_ve3 = sem("pool_ve3")
        pool_rs3 = sem("pool_rs3")
        dve_xn3 = sem("dve_xn3")
        routed = sem("routed")
        logits_out = sem("logits_out")
        logits_turned = sem("logits_turned")
        choose = sem("choose")
        pool_exp = sem("pool_exp")
        spread = sem("spread")
        spread_out = sem("spread_out")
        up_made = sem("up_made")
        gelu_out = sem("gelu_out")
        dve_sum = sem("dve_sum")
        down_made = sem("down_made")
        result = sem("result")
        stored = [sem(f"stored{p}") for p in range(2)]
        CHOICES = 8

        TURNS = []
        for s in range(SLOTS):
            TURNS += [(1, t) for t in at(TURN2, s)] + [(2, t) for t in at(TURN3, s)]
            TURNS += [(3, t) for t in at(TURN3, s + SLOTS)]

        class Turns:

            def before(self, groups, n):
                return self.value(groups) + sum(groups[TURNS[m][0] - 1] is not None for m in range(n))

            def value(self, groups):
                back, any_ = next((n, g) for n, g in enumerate(groups) if g is not None)
                if not isinstance(any_.loop, int):
                    late = sum(t >= SLOTS for t in TURN3)
                    return (any_.loop + (any_.offset + back)) * (2 * NT) - (NT + late)
                done = 0
                for i in range(any_.offset + back):
                    st = stages(0, i, i % 2)
                    done += sum(st[k - 1] is not None for k, _ in TURNS)
                return done

        turns = Turns()

        block = ctx.enter_context(nc.Block())

        def column(ap, n):
            return ap.rearrange("(a b) -> a b", b=1)

        loads = [
            (const_sb[:, :], const), (we[:, :, :], tok_w),
            (lnw[:, :], ln_w.partition_broadcast(TT)), (lnb[:, :], ln_b.partition_broadcast(TT)),
            (stage_a[:, :], w_qkv[0:128, :]),
            (stage_b[0:LO, :], w_qkv[128:EMBED, :]), (stage_b[LO:128, :], w_qkv[128:EMBED, :]),
            (encw[:, 0:EMBED], enc_w), (encw[:, EMBED:EMBED + LO], enc_w[:, 128:EMBED]),
            (encb[:, :], column(enc_b, HIDDEN)), (sww[:, :], sw_w), (swb[:, :], column(sw_b, EXPERTS)),
            (w2_sb[:, :, :], w2), (b1_sb[:, :], b1),
        ]
        for n, s in enumerate((s_q, s_k, s_v, s_attn, s_after)):
            loads.append((scal[:, n:n + 1], s.partition_broadcast(128)))
        second = [(stage_a[:, 0:FF], w1[0:128, :]),
                  (stage_b[0:LO, 0:FF], w1[128:EMBED, :]), (stage_b[LO:128, 0:FF], w1[128:EMBED, :])]
        third = [(stage_a[:, 0:EMBED], w_proj[0:128, :]), (stage_b[0:LO, 0:EMBED], w_proj[128:EMBED, :])]
        fourth = [(stage_a[8 * j:8 * j + 8, 0:EMBED], b2) for j in range(3)]
        fourth += [(stage_a[0:24, EMBED:2 * EMBED], tok_b.partition_broadcast(24)),
                   (stage_a[0:24, 2 * EMBED:3 * EMBED], b_proj.partition_broadcast(24))]
        L1, L2, L3, L4 = (16 * len(w) for w in (loads, second, third, fourth))
        SET_QKV, SET_W1, SET_PROJ, SET_ALL = 4, 8, 20, 47

        @block.sync
        def _(sync):
            def load_tile(g, t):
                wait(sync, embedded, g.count(NT, t + 1 - NT))
                src = x[g.loop + g.offset, t] if not isinstance(g.loop, int) else x[g.offset, t]
                sync.dma_start(x_sb[:, t], src).then_inc(x_in[t], 16)

            first = Group(0, 0, 0)
            for dst, src in loads[:2]:
                sync.dma_start(dst, src).then_inc(loaded, 16)
            for t in range(2):
                load_tile(first, t)
            for dst, src in loads[2:]:
                sync.dma_start(dst, src).then_inc(loaded, 16)
            for t in range(2, NT):
                load_tile(first, t)
            for free, lot in ((SET_QKV, second), (SET_W1, third), (SET_PROJ, fourth)):
                sync.wait_ge(set_dve, free)
                for dst, src in lot:
                    sync.dma_start(dst, src).then_inc(loaded, 16)

            def body(one, two, three):
                for s in range(SLOTS + 2):
                    if three:
                        for t in at(DOWN, s - 2):
                            sync.wait_ge(result, three.count(NT, t + 1))
                            row = three.loop + three.offset if not isinstance(three.loop, int) else three.offset
                            sync.dma_start(out[row, t], out_sb[:, (three.parity + t) % 2]).then_inc(
                                stored[(three.parity + t) % 2], 16)
                    if one:
                        for t in at(EMBED_END, s - 1):
                            if isinstance(one.loop, int) and one.offset == GROUPS - 1:
                                continue
                            nxt = Group(one.loop, one.offset + 1, 1 - one.parity)
                            load_tile(nxt, t)

            passes(sync, body)
            for p in range(2):
                sync.wait_ge(stored[p], 16 * (GROUPS * NT // 2))

        @block.tensor
        def _(pe):
            ident = const_sb[0:TT, C_IDENT:C_IDENT + TT]

            pe.wait_ge(loaded, L1)
            pe.matmul(proj_ps[:, 0:EXPERTS], encw[:, 0:128], sww[:, :], start=True, stop=True)
            pe.matmul(proj_ps[:, EXPERTS:2 * EXPERTS], encw[:, 128:EMBED + LO], sww[:, :],
                      start=True, stop=True)
            pe.matmul(proj_ps[0:EXPERTS, 2 * EXPERTS:2 * EXPERTS + 1], sww[:, :], encb[:, :],
                      start=True, stop=True).then_inc(set_pe, 1)

            def split_product(dst, hi_a, lo_a, hi_b, lo_b, left, right_hi, right_lo, right_b, moving):
                terms = [(hi_a, right_hi), (hi_a, right_lo), (lo_a, right_hi), (hi_b, right_b),
                         (lo_b[0:LO], right_b[0:LO])]
                for n, (w, a) in enumerate(terms):
                    w, a = w[:, left], a
                    lhs, rhs = (a, w) if moving == "weights" else (w, a)
                    last = pe.matmul(dst, lhs, rhs, start=n == 0, stop=n == 4)
                return last

            def embed(g, t, j):
                dst = embed_ps[0:TT, 0:EMBED]
                if j == 0:
                    pe.wait_ge(x_in[t], g.count(16, 16))
                    wait(pe, act_y, g.count(NT, t))
                    pe.matmul(dst, first24[:, :], rows24[:, 1], start=True, stop=False)
                last = pe.matmul(dst, x_sb[:, t, j], we[:, j], start=False, stop=j == KC - 1)
                if j == KC - 1:
                    last.then_inc(embedded, 1)

            def turn(groups, n):
                k, t = TURNS[n]
                g = groups[k - 1]
                if g is None:
                    return
                src, made = (xn2, dve_xn2) if k == 1 else (xn3, dve_xn3)
                pe.wait_ge(made, g.count(NT, t + 1))
                wait(pe, dve_lo, turns.before(groups, n))
                rows = src[:, (g.parity + t) % 2]
                pe.transpose(turn_ps[:, 0:TT], rows[:, 0:128], ident)
                pe.transpose(turn_ps[0:LO, TT:2 * TT], rows[:, 128:EMBED], ident).then_inc(turned, 1)

            def rows(g, m, half):
                n = evac_index("rows", m, half)
                tiles = 4 if half == 0 else NT
                last_turn = max(i for i, x in enumerate(TURNS) if x[0] == 1 and x[1] < tiles)
                wide_free(g, n)
                need_split(g, last_turn)
                cols = slice(half * HALF, (half + 1) * HALF)
                split_product(wide_ps[:, 0:HALF], wq_hi_a, wq_lo_a, wq_hi_b, wq_lo_b,
                              slice(128 * m, 128 * m + 128), a_hi[:, g.parity, cols],
                              a_lo[:, g.parity, cols], a_b[:, g.parity, cols],
                              "activations").then_inc(rows_made, 1)

            def wide_free(g, n):
                if n > 0:
                    pe.wait_ge(rows_out, g.count(EVACS, n))
                else:
                    wait(pe, rows_out, g.count(EVACS, 0))
                    wait(pe, result, g.count(NT, -NT - 1))

            def need_split(g, last_turn):
                pe.wait_ge(dve_lo, turns.before(stages(g.loop, g.offset, g.parity), last_turn + 1))

            def values(g, n):
                at_n = evac_index("values", n)
                wide_free(g, at_n)
                tiles = 4 if n < 2 else NT
                need_split(g, max(i for i, x in enumerate(TURNS) if x[0] == 1 and x[1] < tiles))
                for c in range(2):
                    cols = slice(n * SEQ + c * KEYS, n * SEQ + (c + 1) * KEYS)
                    last = split_product(wide_ps[0:KEYS, EMBED * c:EMBED * (c + 1)], wq_hi_a, wq_lo_a,
                                         wq_hi_b, wq_lo_b, slice(384, 576), a_hi[:, g.parity, cols],
                                         a_lo[:, g.parity, cols], a_b[:, g.parity, cols], "weights")
                last.then_inc(rows_made, 1)

            def head_rows(pair):
                return ("a", 32 * pair) if pair < 4 else ("b", 32 * (pair - 4))

            def qk(g, u):
                n, pair = divmod(u, PAIRS)
                side, row = head_rows(pair)
                q, k = (q_a, k_a) if side == "a" else (q_b, k_b)
                if pair in (0, 4):
                    m = 1 if side == "a" else 2
                    pe.wait_ge(rows_clip, g.count(6, clips_until(m, n // 2)))
                before = u - 1 if u else SLOTS - 1
                if by_scalar_engine(before):
                    wait(pe, act_relu, g.count(RELUS, relus_until(u - 1) if u else 0))
                else:
                    wait(pe, prob_out, g.count(SLOTS, u))
                queries = q[row:row + 32, n * SEQ:(n + 1) * SEQ]
                for odd in range(2):
                    for c in range(2):
                        keys = k[row:row + 32, odd, n * SEQ + c * KEYS:n * SEQ + (c + 1) * KEYS]
                        last = pe.matmul(scores_ps[0:KEYS, odd, c * SEQ:(c + 1) * SEQ], keys, queries,
                                         start=True, stop=True)
                last.then_inc(qk_made, 1)

            def av_ready(g, u):
                n, pair = divmod(u, PAIRS)
                pe.wait_ge(prob_out, g.count(SLOTS, u + 1))
                if pair == 0:
                    pe.wait_ge(v_clip, g.count(GI, n + 1))
                    wait(pe, heads_out, g.count(GI, n))

            def av(g, u):
                n, pair = divmod(u, PAIRS)
                side, row = head_rows(pair)
                col = 0 if side == "a" else SEQ
                for k in range(4):
                    odd, c = divmod(k, 2)
                    last = pe.matmul(heads_ps[row:row + 32, col:col + SEQ], v_pad[:, 2 * n + c, pair, odd],
                                     prob[:, u % 2, odd, c * SEQ:(c + 1) * SEQ].bitcast(f8),
                                     start=k == 0, stop=k == 3)
                last.then_inc(av_made, 1)

            def project(g, t):
                image = (TT * (t + 1) - 1) // SEQ
                pe.wait_ge(heads_clip, g.count(GI, image + 1))
                wait(pe, dve_h1, g.count(NT, t))
                dst = proj_ps[0:TT, 0:EMBED]
                cols = slice(TT * t, TT * (t + 1))
                pe.matmul(dst, first24[:, :], rows24[:, 2], start=True, stop=False)
                for j in range(3):
                    pe.matmul(dst, o_a[:, cols], wp_a[:, j], start=False, stop=False)
                    last = pe.matmul(dst, o_b[:, cols], wp_b[:, j], start=False, stop=j == 2)
                last.then_inc(projected, 1)

            def route(g, half):
                if half == 0:
                    wait(pe, result, g.count(NT, 0))
                else:
                    pe.wait_ge(logits_out, g.count(2, 1))
                cols = slice(half * HALF, (half + 1) * HALF)
                need_split3(g, 4 if half == 0 else NT)
                split_product(route_ps[0:EXPERTS, 0:HALF], wr_hi_a, wr_lo_a, wr_hi_b, wr_lo_b,
                              slice(0, EXPERTS), f_hi[:, g.parity, cols], f_lo[:, g.parity, cols],
                              f_b[:, g.parity, cols], "activations").then_inc(routed, 1)

            def need_split3(g, tiles):
                this = max([i for i, x in enumerate(TURNS) if x[0] == 3 and x[1] < tiles], default=None)
                if this is None:
                    this = max(i for i, x in enumerate(TURNS) if x[0] == 2 and x[1] < tiles)
                    i = g.offset + 1
                else:
                    i = g.offset + 2
                pe.wait_ge(dve_lo, turns.before(stages(g.loop, i, i % 2), this + 1))

            def turn_logits(g):
                pe.wait_ge(logits_out, g.count(2, 2))
                for t in range(NT):
                    last = pe.matmul(route_ps[0:TT, EXPERTS * t:EXPERTS * (t + 1)],
                                     logits_t[:, TT * t:TT * (t + 1)], ident[0:EXPERTS, 0:EXPERTS],
                                     start=True, stop=True)
                last.then_inc(logits_turned, 1)

            def spread_choice(g, half):
                if half == 0:
                    pe.wait_ge(choose, g.count(CHOICES, CHOICES))
                else:
                    pe.wait_ge(spread_out, g.count(2, 1))
                for n, t in enumerate(range(4) if half == 0 else range(4, NT)):
                    last = pe.matmul(route_ps[0:24, TT * n:TT * (n + 1)], onehot3[:, t], ident_b[:, :],
                                     start=True, stop=True)
                last.then_inc(spread, 1)

            def up(g, n):
                m, half = n // 2, n % 2
                bank = wide_ps if n % 2 == 0 else route_ps
                if n == 0:
                    last_rows = g.count(EVACS, 2 * EVACS)
                    pe.wait_ge(rows_out, min(last_rows, GROUPS * EVACS) if isinstance(last_rows, int) else last_rows)
                    pe.wait_ge(spread_out, g.count(2, 2))
                elif n > 1:
                    pe.wait_ge(gelu_out, g.count(8, n - 1))
                cols = slice(half * HALF, (half + 1) * HALF)
                pe.matmul(bank[:, 0:HALF], sel[:, 128 * m:128 * (m + 1)], off_t[:, cols], start=True, stop=False)
                terms = [(w1_hi_a, f_hi), (w1_hi_a, f_lo), (w1_lo_a, f_hi), (w1_hi_b, f_b)]
                left = slice(128 * m, 128 * (m + 1))
                for w, a in terms:
                    pe.matmul(bank[:, 0:HALF], w[:, left], a[:, g.parity, cols], start=False, stop=False)
                pe.matmul(bank[:, 0:HALF], w1_lo_b[0:LO, left], f_b[0:LO, g.parity, cols],
                          start=False, stop=True).then_inc(up_made, 1)

            def down(g, t):
                if t == 0:
                    pe.wait_ge(gelu_out, g.count(8, 8))
                elif t > 1:
                    pe.wait_ge(result, g.count(NT, t - 1))
                dst = (route_ps if t % 2 == 0 else wide_ps)[0:TT, 0:EMBED]
                cols = slice(TT * t, TT * (t + 1))
                pe.matmul(dst, one_t[:, cols], rows24[:, 0], start=True, stop=False)
                for m in range(FC):
                    last = pe.matmul(dst, hid[:, m, cols], w2_sb[:, m], start=False, stop=m == FC - 1)
                last.then_inc(down_made, 1)

            pe.wait_ge(set_dve, SET_ALL)

            def body(*groups):
                one, two, three = groups
                for s in range(-1, SLOTS):
                    if two:
                        if s >= 0:
                            qk(two, s)
                        for m, half in ROWS_AT.get(s, []):
                            rows(two, m, half)
                        for n in VALUES_AT.get(s, []):
                            values(two, n)
                    for n, (k, t) in enumerate(TURNS):
                        slot = (TURN2 if k == 1 else TURN3)[t] - (SLOTS if k == 3 else 0)
                        if slot == s and k == 1:
                            turn(groups, n)
                    heads = (two, s - 1) if s > 0 else (three, SLOTS - 1)
                    if heads[0] and s >= 0:
                        av_ready(*heads)
                    work = embeds_of(s) if one else []
                    for t, j in work[:1]:
                        embed(one, t, j)
                    if not work and three:
                        for t in at(DOWN, s):
                            down(three, t)
                    if heads[0] and s >= 0:
                        av(*heads)
                    if two:
                        for t in at(PROJ, s):
                            project(two, t)
                    if three:
                        for t in at(PROJ, s + SLOTS):
                            project(three, t)
                        for half in at(ROUTE, s):
                            route(three, half)
                        if s == TURN_LOGITS:
                            turn_logits(three)
                        for half in at(SPREAD, s):
                            spread_choice(three, half)
                        for n in at(UP, s)[:1]:
                            up(three, n)
                    for t, j in work[1:]:
                        embed(one, t, j)
                    if three:
                        for n in at(UP, s)[1:]:
                            up(three, n)
                        for t in at(DOWN, s) if work else []:
                            down(three, t)
                    for n, (k, t) in enumerate(TURNS):
                        slot = (TURN2 if k == 1 else TURN3)[t] - (SLOTS if k == 3 else 0)
                        if slot == s and k != 1:
                            turn(groups, n)

            passes(pe, body)

        def reads_done(eng, g, k):
            if k == 1:
                wait(eng, rows_made, g.count(EVACS, -EVACS))
            else:
                wait(eng, up_made, g.count(8, -8))

        @block.scalar
        def _(act):
            act.wait_ge(set_pool, 1)
            act.activation(warm[:, :], warm[:, :], ACT.Gelu).then_inc(warmed, 1)
            act.wait_ge(set_dve, SET_ALL)

            def embed_evac(g, t):
                act.wait_ge(embedded, g.count(NT, t + 1))
                wait(act, act_n1, g.count(NT, t - 1))
                act.activation(y1[:, (g.parity + t) % 2], embed_ps[0:TT, 0:EMBED],
                               ACT.Copy).then_inc(act_y, 1)

            def norm1(g, t):
                half = (g.parity + t) % 2
                act.wait_ge(dve_nb1, g.count(NT, t + 1))
                wait(act, pool_m1, g.count(NT, t - 1))
                act.activation(n1[:, half], y1[:, half], ACT.Identity,
                               scale=rs1[:, t], bias=nb1[:, t]).then_inc(act_n1, 1)

            def high(groups, n):
                k, t = TURNS[n]
                g = groups[k - 1]
                if g is None:
                    return
                hi, both = (a_hi, a_b) if k == 1 else (f_hi, f_b)
                cols = slice(TT * t, TT * (t + 1))
                act.wait_ge(turned, turns.before(groups, n) + 1)
                if t == 0:
                    reads_done(act, g, k)
                act.activation(hi[:, g.parity, cols], turn_ps[:, 0:TT], ACT.Copy)
                act.activation(both[0:LO, g.parity, cols], turn_ps[0:LO, TT:2 * TT],
                               ACT.Copy).then_inc(act_hi, 1)

            def relu(g, u):
                act.wait_ge(qk_made, g.count(SLOTS, u + 1))
                back = [v for v in range(u) if by_scalar_engine(v)]
                wait(act, prob_out, g.count(SLOTS, back[-1] + 1) if back else g.count(SLOTS, 0))
                act.activation(relu8[:, :, :], scores_ps[0:KEYS, :, 0:2 * SEQ], ACT.Relu,
                               scale=c_prob[0:KEYS, :]).then_inc(act_relu, 1)

            def rows_evac(g, m, half):
                n = evac_index("rows", m, half)
                cols = slice(half * HALF, (half + 1) * HALF)
                act.wait_ge(rows_made, g.count(EVACS, n + 1))
                wait(act, rows_clip, g.count(6, clips_until(m, half) - 6))
                act.activation(rows8[:, m, cols], wide_ps[:, 0:HALF], ACT.Identity,
                               scale=inv_rows[:, m:m + 1]).then_inc(rows_out, 1)

            def values_evac(g, n):
                act.wait_ge(rows_made, g.count(EVACS, evac_index("values", n) + 1))
                wait(act, v_clip, g.count(GI, n + 1 - GI))
                act.activation(v8[:, n], wide_ps[0:KEYS, 0:2 * EMBED], ACT.Identity,
                               scale=rec[0:KEYS, 2:3]).then_inc(rows_out, 1)

            def heads_evac(g, n):
                cols = slice(SEQ * n, SEQ * (n + 1))
                act.wait_ge(av_made, g.count(SLOTS, PAIRS * (n + 1)))
                wait(act, heads_clip, g.count(GI, n + 1 - GI))
                act.activation(o8_a[:, cols], heads_ps[:, 0:SEQ], ACT.Identity, scale=c_out[:, :])
                act.activation(o8_b[:, cols], heads_ps[0:LO, SEQ:2 * SEQ], ACT.Identity,
                               scale=c_out[0:LO, :]).then_inc(heads_out, 1)

            def gelu(g, n):
                m, half = n // 2, n % 2
                bank = wide_ps if n % 2 == 0 else route_ps
                act.wait_ge(up_made, g.count(8, n + 1))
                if n == 0:
                    wait(act, down_made, g.count(NT, 0))
                act.activation(hid[:, m, half * HALF:(half + 1) * HALF], bank[:, 0:HALF], ACT.Gelu,
                               bias=b1_sb[:, m:m + 1]).then_inc(gelu_out, 1)

            def body(*groups):
                one, two, three = groups
                for s in range(-1, SLOTS):
                    if two and s >= 0 and by_scalar_engine(s):
                        relu(two, s)
                    if three and s == 0:
                        heads_evac(three, GI - 1)
                    if two and s in (6, 12, 18):
                        heads_evac(two, s // 6 - 1)
                    if two:
                        for m, half in ROWS_AT.get(s, []):
                            rows_evac(two, m, half)
                        for n in VALUES_AT.get(s, []):
                            values_evac(two, n)
                    for n, (k, t) in enumerate(TURNS):
                        slot = (TURN2 if k == 1 else TURN3)[t] - (SLOTS if k == 3 else 0)
                        if slot == s and k == 1:
                            high(groups, n)
                    if one:
                        for t in at(NORM1, s):
                            norm1(one, t)
                        for t in at(EMBED_END, s):
                            embed_evac(one, t)
                    if three:
                        for n in at(UP, s):
                            gelu(three, n)
                    for n, (k, t) in enumerate(TURNS):
                        slot = (TURN2 if k == 1 else TURN3)[t] - (SLOTS if k == 3 else 0)
                        if slot == s and k != 1:
                            high(groups, n)

            passes(act, body)

        @block.gpsimd
        def _(pool):
            pool.memset(warm[:, :], 0.0).then_inc(set_pool, 1)
            pool.memset(v_pad[:, :, :, :, :], 0.0).then_inc(set_pool, 1)
            pool.wait_ge(loaded, L1)
            pool.wait_ge(set_dve, SET_ALL)

            def rstd(g, t, mv_sem, mv, ve, rs, ve_sem, rs_sem):
                pool.wait_ge(mv_sem, g.count(NT, t + 1))
                pool.tensor_tensor(ve[:, t], mv[:, t, 1:2], const_sb[0:TT, C_EPS:C_EPS + 1],
                                   ALU.add).then_inc(ve_sem, 1)
                pool.wait_ge(ve_sem, g.count(NT, t + 1))
                pool.tensor_tensor(rs[:, t], ve[:, t], const_sb[0:TT, C_HALFNEG:C_HALFNEG + 1],
                                   ALU.pow).then_inc(rs_sem, 1)

            def affine(g, t):
                half = (g.parity + t) % 2
                pool.wait_ge(act_n1, g.count(NT, t + 1))
                pool.tensor_tensor(m1[:, half], n1[:, half], lnw[:, :], ALU.mult).then_inc(pool_m1, 1)
                pool.wait_ge(pool_m1, g.count(NT, t + 1))
                wait(pool, dve_h1, g.count(NT, t + 1 - 2 * NT))
                pool.tensor_tensor(h0[:, g.parity, t], m1[:, half], lnb[:, :], ALU.add).then_inc(pool_h0, 1)

            def body(*groups):
                one, two, three = groups
                for s in range(-1, SLOTS):
                    if one:
                        for t in at(STATS1, s):
                            rstd(one, t, dve_mv1, mv1, ve1, rs1, pool_ve1, pool_rs1)
                        for t in at(NORM1, s):
                            affine(one, t)
                        for t in at(STATS2, s):
                            rstd(one, t, dve_mv2, mv2, ve2, rs2, pool_ve2, pool_rs2)
                    for g, late in ((two, 0), (three, SLOTS)):
                        if g and s >= 0:
                            for t in at(RESID, s + late):
                                rstd(g, t, dve_mv3, mv3, ve3, rs3, pool_ve3, pool_rs3)
                    if three and s == CHOOSE:
                        pool.wait_ge(choose, three.count(CHOICES, 3))
                        wait(pool, dve_sum, three.count(2, 0))
                        pool.tensor_tensor(expd[:, :, :], econst[:, :, :], below[:, :, :],
                                           ALU.pow).then_inc(pool_exp, 1)

            passes(pool, body)

        @block.vector
        def _(dve):
            done = [0]

            def setup(ins):
                done[0] += 1
                ins.then_inc(set_dve, 1)
                dve.wait_ge(set_dve, done[0])

            def split_r(hi, lo, src):
                setup(dve.tensor_copy(hi, src))
                setup(dve.tensor_tensor(lo, src, hi.bitcast(f32), ALU.subtract))

            def split_b(parts, src, rest):
                setup(dve.tensor_copy(parts[0], src))
                setup(dve.tensor_tensor(rest, src, parts[0], ALU.subtract))
                setup(dve.tensor_copy(parts[1], rest))
                setup(dve.tensor_tensor(rest, rest, parts[1], ALU.subtract))
                setup(dve.tensor_copy(parts[2], rest))

            dve.wait_ge(loaded, L1)
            split_r(wq_hi_a[:, :], wq_lo_a[:, :], stage_a[:, :])
            split_r(wq_hi_b[:, :], wq_lo_b[:, :], stage_b[:, :])
            assert done[0] == SET_QKV
            dve.wait_ge(loaded, L1 + L2)
            split_r(w1_hi_a[:, :], w1_lo_a[:, :], stage_a[:, 0:FF])
            split_r(w1_hi_b[:, :], w1_lo_b[:, :], stage_b[:, 0:FF])
            assert done[0] == SET_W1
            dve.wait_ge(loaded, L1 + L2 + L3)
            for parts, src, n in ((wp_a, stage_a, 128), (wp_b, stage_b, LO)):
                scaled, rest = stage_c[0:n, 0:EMBED], stage_c[0:n, EMBED:2 * EMBED]
                setup(dve.tensor_scalar(scaled, src[0:n, 0:EMBED], scal[0:n, 4:5], None, ALU.mult))
                split_b([parts[:, j] for j in range(3)], scaled, rest)
            assert done[0] == SET_PROJ
            dve.wait_ge(loaded, L1 + L2 + L3 + L4)
            bias_parts = [parts24[:, j] for j in range(3)]
            split_b(bias_parts, stage_a[0:24, :], stage_b[0:24, :])
            setup(dve.tensor_scalar(stage_c[0:24, :], bias_parts[0], const_sb[0:24, C_PART:C_PART + 1],
                                    None, ALU.mult))
            for j in (1, 2):
                dst = stage_c[0:24, :] if j == 1 else rows24[:, :, :].rearrange("p a b -> p (a b)")
                setup(dve.scalar_tensor_tensor(dst, bias_parts[j], const_sb[0:24, C_PART + j:C_PART + j + 1],
                                               stage_c[0:24, :], ALU.mult, ALU.add))
            setup(dve.tensor_copy(first24[:, :], const_sb[0:24, C_FIRST:C_FIRST + TT]))
            setup(dve.tensor_copy(sel[:, :], const_sb[0:EXPERTS, C_SEL:C_SEL + FF]))
            setup(dve.tensor_copy(ident_b[:, :], const_sb[0:TT, C_IDENT:C_IDENT + TT]))
            setup(dve.tensor_copy(econst[:, :, :].rearrange("p a b -> p (a b)"),
                                  const_sb[0:TT, C_E:C_E + 1].broadcast_to([TT, NT * EXPERTS])))
            setup(dve.reciprocal(rec[:, :], scal[:, :]))
            setup(dve.tensor_copy(inv_rows[:, 0:2], rec[:, 0:2]))
            setup(dve.tensor_copy(inv_rows[0:64, 2:3], rec[0:64, 0:1]))
            setup(dve.tensor_copy(inv_rows[64:128, 2:3], rec[64:128, 1:2]))
            setup(dve.tensor_scalar(tmp1[:, 0:1], scal[:, 0:1], scal[:, 1:2], DH ** -0.5 / SEQ, ALU.mult, ALU.mult))
            setup(dve.tensor_scalar(c_prob[:, :], tmp1[:, 0:1], rec[:, 3:4], None, ALU.mult))
            setup(dve.tensor_scalar(tmp1[:, 1:2], scal[:, 3:4], scal[:, 2:3], E4_STEP, ALU.mult, ALU.mult))
            setup(dve.tensor_scalar(c_out[:, :], tmp1[:, 1:2], rec[:, 4:5], None, ALU.mult))
            dve.wait_ge(set_pe, 1)
            setup(dve.tensor_copy(wr_f[:, :, :].rearrange("p a b -> p (a b)"), proj_ps[:, 0:2 * EXPERTS]))
            setup(dve.tensor_scalar(br[:, :], proj_ps[0:EXPERTS, 2 * EXPERTS:2 * EXPERTS + 1], swb[:, :],
                                    None, ALU.add))
            split_r(wr_hi_a[:, :], wr_lo_a[:, :], wr_f[:, 0])
            split_r(wr_hi_b[:, :], wr_lo_b[:, :], wr_f[:, 1])
            dve.wait_ge(set_pool, 2)
            setup(dve.memset(tmp1[:, :], 0.0))
            assert done[0] == SET_ALL, done[0]

            def stats1(g, t):
                half = (g.parity + t) % 2
                dve.wait_ge(act_y, g.count(NT, t + 1))
                dve.bn_stats(st1[:, t], y1[:, half]).then_inc(dve_st1, 1)

            def bias1(g, t):
                dve.wait_ge(pool_rs1, g.count(NT, t + 1))
                dve.scalar_tensor_tensor(nb1[:, t], mv1[:, t, 0:1], -1.0, rs1[:, t], ALU.mult,
                                         ALU.mult).then_inc(dve_nb1, 1)

            def stats(g, t, src, src_sem, st, st_sem):
                dve.wait_ge(src_sem, g.count(NT, t + 1))
                dve.bn_stats(st[:, t], src[:, g.parity, t]).then_inc(st_sem, 1)

            def aggregated(groups, s):
                one, two, three = groups
                found = [(one, t, st1, mv1, dve_st1, dve_mv1) for t in at(STATS1, s)]
                found += [(one, t, st2, mv2, dve_st2, dve_mv2) for t in at(STATS2, s)]
                for g, slot in ((two, s), (three, s + SLOTS)):
                    found += [(g, t, st3, mv3, dve_st3, dve_mv3) for t in at(RESID, slot)] if s >= 0 else []
                return [x for x in found if x[0]]

            def norm(groups, g, t, k, src, mv, rs, rs_sem, dst, dst_sem):
                dve.wait_ge(rs_sem, g.count(NT, t + 1))
                wait(dve, turned, before_turn(groups, g, t - 2, k))
                dve.tensor_scalar(dst[:, (g.parity + t) % 2], src[:, g.parity, t], mv[:, t, 0:1], rs[:, t],
                                  ALU.subtract, ALU.mult).then_inc(dst_sem, 1)

            def before_turn(groups, g, t, k):
                back = 0
                if t < 0:
                    back, t = 1, t + NT
                if k == 1:
                    stage = 1
                else:
                    stage = 2 if TURN3[t] < SLOTS else 3
                n = TURNS.index((stage, t))
                i = g.offset + stage - 1 - back
                if isinstance(g.loop, int) and i < 0:
                    return 0
                if isinstance(g.loop, int) and g.offset - back < 0:
                    return 0
                return turns.before(stages(g.loop, i, i % 2), n + 1)

            def low(groups, n):
                k, t = TURNS[n]
                g = groups[k - 1]
                if g is None:
                    return
                hi, lo, both = (a_hi, a_lo, a_b) if k == 1 else (f_hi, f_lo, f_b)
                cols = slice(TT * t, TT * (t + 1))
                dve.wait_ge(act_hi, turns.before(groups, n) + 1)
                dve.tensor_tensor(lo[:, g.parity, cols], turn_ps[:, 0:TT],
                                  hi[:, g.parity, cols].bitcast(f32), ALU.subtract)
                dve.tensor_tensor(both[LO:128, g.parity, cols], turn_ps[0:LO, TT:2 * TT],
                                  both[0:LO, g.parity, cols].bitcast(f32), ALU.subtract).then_inc(dve_lo, 1)

            def quantise(g, u):
                if by_scalar_engine(u):
                    dve.wait_ge(act_relu, g.count(RELUS, relus_until(u)))
                else:
                    dve.wait_ge(qk_made, g.count(SLOTS, u + 1))
                wait(dve, av_made, g.count(SLOTS, u - 1))
                if by_scalar_engine(u):
                    dve.tensor_scalar(prob[:, u % 2], relu8[:, :, :], 7.0, None,
                                      ALU.min).then_inc(prob_out, 1)
                else:
                    dve.tensor_scalar(prob[:, u % 2], scores_ps[0:KEYS, :, 0:2 * SEQ], c_prob[0:KEYS, :],
                                      7.0, ALU.mult, ALU.min).then_inc(prob_out, 1)

            def bounds(n, odd):
                return [const_sb[n, C_BOUND + 2 * odd + b:C_BOUND + 2 * odd + b + 1] for b in range(2)]

            def clip_rows(g, m, half):
                cols = slice(half * HALF, (half + 1) * HALF)
                dve.wait_ge(rows_out, g.count(EVACS, evac_index("rows", m, half) + 1))
                wait(dve, qk_made, g.count(SLOTS, (half + 1) * SLOTS // 2 - SLOTS))
                if m == 0:
                    last = dve.tensor_scalar(q_a[:, cols], rows8[:, 0, cols], -4.0, 3.0, ALU.max, ALU.min)
                elif m == 1:
                    for odd in range(2):
                        low_, high_ = bounds(slice(0, 128), odd)
                        last = dve.tensor_scalar(k_a[:, odd, cols], rows8[:, 1, cols], low_, high_,
                                                 ALU.max, ALU.min)
                else:
                    dve.tensor_scalar(q_b[:, cols], rows8[0:LO, 2, cols], -4.0, 3.0, ALU.max, ALU.min)
                    for odd in range(2):
                        low_, high_ = bounds(slice(LO, 128), odd)
                        last = dve.tensor_scalar(k_b[:, odd, cols], rows8[LO:128, 2, cols], low_, high_,
                                                 ALU.max, ALU.min)
                last.then_inc(rows_clip, 1)

            def clip_values(g, n):
                dve.wait_ge(rows_out, g.count(EVACS, evac_index("values", n) + 1))
                wait(dve, av_made, g.count(SLOTS, PAIRS * (n + 1) - SLOTS))
                flat = v_pad[:, 2 * n:2 * n + 2].rearrange("k c p e d -> k (c p) (e d)")
                for e in range(2):
                    src = v8[:, n].rearrange("k (cp e d) -> k cp e d", e=2, d=DH)[:, :, e]
                    last = dve.tensor_scalar(flat[:, :, 48 * e:48 * e + DH], src, -4.0, 3.0, ALU.max, ALU.min)
                last.then_inc(v_clip, 1)

            def clip_heads(g, n):
                cols = slice(SEQ * n, SEQ * (n + 1))
                dve.wait_ge(heads_out, g.count(GI, n + 1))
                wait(dve, projected, g.count(NT, 0))
                dve.tensor_scalar(o_a[:, cols], o8_a[:, cols], -4.0, 3.0, ALU.max, ALU.min)
                dve.tensor_scalar(o_b[:, cols], o8_b[:, cols], -4.0, 3.0, ALU.max,
                                  ALU.min).then_inc(heads_clip, 1)

            def residual(g, t):
                dve.wait_ge(projected, g.count(NT, t + 1))
                wait(dve, result, g.count(NT, t + 1 - 2 * NT))
                dve.tensor_tensor(h1[:, g.parity, t], proj_ps[0:TT, 0:EMBED], h0[:, g.parity, t],
                                  ALU.add).then_inc(dve_h1, 1)
                stats(g, t, h1, dve_h1, st3, dve_st3)

            def logits_evac(g, half):
                dve.wait_ge(routed, g.count(2, half + 1))
                wait(dve, logits_turned, g.count(1, 0))
                dve.tensor_scalar(logits_t[:, half * HALF:(half + 1) * HALF], route_ps[0:EXPERTS, 0:HALF],
                                  br[:, :], None, ALU.add).then_inc(logits_out, 1)

            def choice(g):
                count = [0]

                def step(ins):
                    count[0] += 1
                    ins.then_inc(choose, 1)
                    dve.wait_ge(choose, g.count(CHOICES, count[0]))

                def wide(ap):
                    return ap.rearrange("p (t e) -> p t e", e=1).broadcast_to([TT, NT, EXPERTS])

                ramp = const_sb[0:TT, C_RAMP:C_RAMP + EXPERTS].rearrange("p (t e) -> p t e", t=1)
                dve.wait_ge(logits_turned, g.count(1, 1))
                step(dve.tensor_copy(logit[:, :, :].rearrange("p t e -> p (t e)"),
                                     route_ps[0:TT, 0:NT * EXPERTS]))
                step(dve.tensor_reduce(top[:, :], logit[:, :, :], AX.X, ALU.max))
                wait(dve, pool_exp, g.count(1, 0))
                step(dve.tensor_tensor(below[:, :, :], logit[:, :, :], wide(top[:, :]), ALU.subtract))
                step(dve.tensor_scalar(score[:, :, :], below[:, :, :], 0.0, None, ALU.is_ge))
                step(dve.tensor_tensor(score2[:, :, :], score[:, :, :],
                                       ramp.broadcast_to([TT, NT, EXPERTS]), ALU.mult))
                step(dve.tensor_reduce(best[:, :], score2[:, :, :], AX.X, ALU.max))
                step(dve.tensor_tensor(score[:, :, :], score2[:, :, :], wide(best[:, :]), ALU.is_equal))
                wait(dve, spread, g.count(2, 0))
                src = score[:, :, :].rearrange("p t (a e) -> p t a e", a=1).broadcast_to([TT, NT, 3, EXPERTS])
                step(dve.tensor_copy(onehot3[:, :, :].rearrange("p t (a e) -> p t a e", a=3), src))
                assert count[0] == CHOICES

            def spread_evac(g, half):
                tiles = 4 if half == 0 else NT - 4
                cols = slice(0, 4 * TT) if half == 0 else slice(4 * TT, TOK)
                dve.wait_ge(spread, g.count(2, half + 1))
                wait(dve, down_made, g.count(NT, 0))
                dve.tensor_copy(one_t[:, cols], route_ps[0:24, 0:tiles * TT])
                dve.tensor_scalar(off_t[:, cols], route_ps[0:EXPERTS, 0:tiles * TT], -1.0, None,
                                  ALU.add).then_inc(spread_out, 1)

            def sum_exp(g):
                dve.wait_ge(pool_exp, g.count(1, 1))
                dve.tensor_reduce(sume[:, :], expd[:, :, :], AX.X, ALU.add).then_inc(dve_sum, 1)
                dve.wait_ge(dve_sum, g.count(2, 1))
                dve.reciprocal(pmax[:, :], sume[:, :]).then_inc(dve_sum, 1)

            def finish(g, t):
                src = (route_ps if t % 2 == 0 else wide_ps)[0:TT, 0:EMBED]
                half = (g.parity + t) % 2
                dve.wait_ge(down_made, g.count(NT, t + 1))
                if t == 0:
                    dve.wait_ge(dve_sum, g.count(2, 2))
                earlier = (NT * g.offset + t) // 2
                value = 16 * earlier if isinstance(g.loop, int) else g.loop * (8 * NT) + 16 * earlier
                wait(dve, stored[half], value)
                dve.scalar_tensor_tensor(out_sb[:, half], src, pmax[:, t:t + 1], h1[:, g.parity, t],
                                         ALU.mult, ALU.add).then_inc(result, 1)

            def body(*groups):
                one, two, three = groups
                for s in range(-1, SLOTS + 1):
                    if one:
                        for t in at(STATS1, s):
                            stats1(one, t)
                        for t in at(STATS2, s):
                            stats(one, t, h0, pool_h0, st2, dve_st2)
                    for g, late in ((two, 0), (three, SLOTS)):
                        if g and 0 <= s < SLOTS:
                            for t in at(RESID, s + late):
                                residual(g, t)
                    for g, t, _, _, st_sem, _ in aggregated(groups, s):
                        dve.wait_ge(st_sem, g.count(NT, t + 1))
                    if two and 0 <= s < SLOTS:
                        quantise(two, s)
                    for g, t, st, mv, _, mv_sem in aggregated(groups, s):
                        dve.bn_aggr(mv[:, t], st[:, t]).then_inc(mv_sem, 1)
                    if two:
                        for m, half in ROWS_AT.get(s, []):
                            clip_rows(two, m, half)
                        for n in VALUES_AT.get(s, []):
                            clip_values(two, n)
                    if three and s == 1:
                        clip_heads(three, GI - 1)
                    if two and s in (7, 13, 19):
                        clip_heads(two, s // 6 - 1)
                    for n, (k, t) in enumerate(TURNS):
                        slot = (TURN2 if k == 1 else TURN3)[t] - (SLOTS if k == 3 else 0)
                        if slot == s and k == 1:
                            low(groups, n)
                    if one:
                        for t in at(NORM1, s):
                            bias1(one, t)
                        for t in at(NORM2, s):
                            norm(groups, one, t, 1, h0, mv2, rs2, pool_rs2, xn2, dve_xn2)
                    for g, late in ((two, 0), (three, SLOTS)):
                        if g and 0 <= s < SLOTS:
                            for t in at(NORM3, s + late):
                                norm(groups, g, t, 2, h1, mv3, rs3, pool_rs3, xn3, dve_xn3)
                    if three:
                        for half in at(ROUTE, s):
                            logits_evac(three, half)
                        if s == CHOOSE:
                            choice(three)
                        for half in at(SPREAD, s):
                            spread_evac(three, half)
                        if s == SUMEXP:
                            sum_exp(three)
                        for t in at(DOWN, s - 1):
                            finish(three, t)
                    for n, (k, t) in enumerate(TURNS):
                        slot = (TURN2 if k == 1 else TURN3)[t] - (SLOTS if k == 3 else 0)
                        if slot == s and k != 1:
                            low(groups, n)

            passes(dve, body)


_INS = ["x", "tok_w", "tok_b", "ln_w", "ln_b", "w_qkv", "w_proj", "b_proj", "s_q", "s_k", "s_v", "s_attn",
        "s_after", "enc_w", "enc_b", "sw_w", "sw_b", "w1", "b1", "w2", "b2", "const"]


def kernel(x, L0_tok_W, L0_tok_b, L0_tok_ln_w, L0_tok_ln_b, L0_attn_Wqkv, L0_attn_Wproj, L0_attn_bproj,
           L0_attn_s_q, L0_attn_s_k, L0_attn_s_v, L0_attn_s_attn, L0_attn_s_after, L0_ffn_enc_w,
           L0_ffn_enc_b, L0_ffn_sw_w, L0_ffn_sw_b, L0_ffn_w1, L0_ffn_b1, L0_ffn_w2, L0_ffn_b2):
    import numpy as _np
    import concourse.bacc as _bacc
    from concourse import mybir as _mybir
    from concourse.bass_utils import run_bass_kernel_spmd as _run

    a = _np.asarray(x).reshape(GROUPS, GI, 3, GRID, PATCH, GRID, PATCH)
    a = a.transpose(0, 1, 3, 5, 2, 4, 6).reshape(GROUPS, NT, TT, KC, 128).transpose(0, 1, 4, 3, 2)
    wq = _np.asarray(L0_attn_Wqkv)
    q, k, v = wq[0:EMBED], wq[EMBED:2 * EMBED], wq[2 * EMBED:]
    rows = _np.concatenate([q[:128], k[:128], q[128:], k[128:], v]).T
    arrays = dict(
        x=a, tok_w=_np.asarray(L0_tok_W).T.reshape(KC, 128, EMBED).transpose(1, 0, 2),
        tok_b=L0_tok_b, ln_w=L0_tok_ln_w, ln_b=L0_tok_ln_b, w_qkv=rows,
        w_proj=_np.asarray(L0_attn_Wproj).T, b_proj=L0_attn_bproj,
        s_q=_np.asarray(L0_attn_s_q).reshape(1), s_k=_np.asarray(L0_attn_s_k).reshape(1),
        s_v=_np.asarray(L0_attn_s_v).reshape(1), s_attn=_np.asarray(L0_attn_s_attn).reshape(1),
        s_after=_np.asarray(L0_attn_s_after).reshape(1),
        enc_w=_np.asarray(L0_ffn_enc_w).T, enc_b=L0_ffn_enc_b, sw_w=L0_ffn_sw_w, sw_b=L0_ffn_sw_b,
        w1=_np.asarray(L0_ffn_w1).transpose(1, 0, 2).reshape(EMBED, FF),
        b1=_np.asarray(L0_ffn_b1).reshape(FC, 128).T,
        w2=_np.asarray(L0_ffn_w2).reshape(FC, 128, EMBED).transpose(1, 0, 2),
        b2=L0_ffn_b2, const=constants())
    nc = _bacc.Bacc("TRN2", target_bir_lowering=False, num_devices=1)
    feeds, args = {}, []
    for name in _INS:
        feed = _np.ascontiguousarray(arrays[name])
        feeds[f"in_{name}"] = feed
        args.append(nc.dram_tensor(f"in_{name}", feed.shape, _mybir.dt.from_np(feed.dtype),
                                   kind="ExternalInput").ap())
    out = nc.dram_tensor("out", (GROUPS, NT, TT, EMBED), _mybir.dt.float32, kind="ExternalOutput").ap()
    vit_tower_kernel(nc, *args, out)
    result = _run(nc, [feeds], core_ids=[0])
    return result.results[0]["out"].reshape(IMAGES, SEQ, EMBED)
```

```python
import numpy as np
import concourse.bass as bass
import concourse.mybir as mybir
from contextlib import ExitStack

IMAGES, PATCH, GRID, EMBED, HEADS, EXPERTS, HIDDEN = 64, 16, 14, 192, 12, 8, 64
SEQ = GRID * GRID
FAN_IN = 3 * PATCH * PATCH
KC = FAN_IN // 128
GI = 4
GROUPS = IMAGES // GI
TOK = GI * SEQ
TT = 112
NT = TOK // TT
HALF = TOK // 2
KEYS = SEQ // 2
DH = EMBED // HEADS
PAIRS = HEADS // 2
SLOTS = GI * PAIRS
LO = EMBED - 128
FF = EXPERTS * HIDDEN
FC = FF // 128
EPS = 1e-5
MASKED = 2.0 ** 60
E4_STEP = 512.0

C_IDENT, C_RAMP, C_SEL = 0, TT, TT + EXPERTS
C_BOUND = C_SEL + FF
C_PART = C_BOUND + 4
C_FIRST = C_PART + 3
C_HALFNEG, C_E, C_EPS = (C_FIRST + TT + n for n in range(3))
C_ALL = C_EPS + 1


def constants():
    c = np.zeros((128, C_ALL), np.float32)
    c[:TT, C_IDENT:C_IDENT + TT] = np.eye(TT)
    c[:, C_RAMP:C_RAMP + EXPERTS] = EXPERTS - np.arange(EXPERTS)
    for e in range(EXPERTS):
        c[e, C_SEL + HIDDEN * e:C_SEL + HIDDEN * (e + 1)] = MASKED
    odd = (np.arange(128) // DH) % 2
    for n, (head, bound) in enumerate(((0, -4), (0, 3), (1, -4), (1, 3))):
        c[:, C_BOUND + n] = np.where(odd == head, bound, 0)
    for j in range(3):
        c[8 * j:8 * j + 8, C_PART + j] = 1
        c[8 * j, C_FIRST:C_FIRST + TT] = 1
    c[:, C_HALFNEG] = -0.5
    c[:, C_E] = np.e
    c[:, C_EPS] = EPS
    return c


class Group:

    def __init__(self, loop, offset, parity):
        self.loop, self.offset, self.parity = loop, offset, parity

    def count(self, per_group, k):
        return self.loop * per_group + (self.offset * per_group + k)


def stages(loop, offset, parity):
    found = []
    for back in range(3):
        n = offset - back
        there = not isinstance(loop, int) or 0 <= n < GROUPS
        found.append(Group(loop, n, (parity + back) % 2) if there else None)
    return found


def wait(eng, sem, value):
    if not isinstance(value, int) or value > 0:
        eng.wait_ge(sem, value)


LOOP_FROM, LOOP_TO = 4, 14


def passes(eng, body):
    for i in range(LOOP_FROM):
        body(*stages(0, i, i % 2))
    with eng.Fori(LOOP_FROM, LOOP_TO, 2) as i:
        body(*stages(i, 0, 0))
        body(*stages(i, 1, 1))
    for i in range(LOOP_TO, GROUPS + 2):
        body(*stages(0, i, i % 2))


EMBED_SPAN = [2, 2, 2, 3, 2, 3, 2]
EMBED_END = [sum(EMBED_SPAN[:t + 1]) - 1 for t in range(NT)]


def embeds_of(slot):
    for t, (span, end) in enumerate(zip(EMBED_SPAN, EMBED_END)):
        step = slot - (end + 1 - span)
        if 0 <= step < span:
            return [(t, j) for j in range(KC) if j * span // KC == step]
    return []


def at(slots, slot):
    return [t for t, s in enumerate(slots) if s == slot]


def odd(slot):
    return slot + 1 - slot % 2


STATS1 = [2, 4, 5, 9, 11, 14, 16]
JOIN1 = [3, 5, 7, 9, 11, 15, 17]
NORM1 = [4, 6, 8, 10, 12, 16, 18]
BIAS1 = [4, 6, 8, 10, 12, 16, 18]
EVAC1 = [1, 3, 5, 8, 10, 13, 15]
STATS2 = [7, 9, 11, 13, 15, 19, 21]
JOIN2 = [7, 9, 11, 13, 15, 19, 21]
NORM2 = [8, 10, 12, 14, 16, 20, 22]
TURN2 = [9, 11, 13, 15, 17, 21, 23]
FIRST_STEPS = {17: ("rows", 0, 0), 18: ("rows", 1, 0), 21: ("rows", 2, 0), 22: ("values", 0), 23: ("values", 1)}
SECOND_STEPS = {0: ("rows", 0, 1), 1: ("rows", 1, 1), 2: ("rows", 2, 1), 5: ("values", 2), 7: ("values", 3)}
DLOG, DSPR, DLOW1 = 0, 0, 0
STEPS = list(FIRST_STEPS.values()) + list(SECOND_STEPS.values())
EVACS = len(STEPS)


def clips_until(m, half):
    return [x[1:] for x in STEPS if x[0] == "rows"].index((m, half)) + 1


DUOS = SLOTS // 2
HEADS_EVAC = [PAIRS * (n + 1) for n in range(GI)]
PROJ = [14, 15, 16, 20, 21, 26, 27]
RESID = [15, 16, 17, 21, 22, 27, 28]
JOIN3 = [15, 17, 17, 21, 23, 27, 29]
NORM3 = [16, 18, 18, 22, 24, 28, 30]
TURN3 = [18, 20, 22, 24, 26, 30, 32]
PARTS = [range(0, 4), range(4, NT)]
ROUTE = [3, 10]
TURN_LOGITS = [4, 11]
CHOOSE = [4, 12]
SPREAD = [5, 13]
UP = [6, 7, 8, 9, 14, 15, 16, 17]
SUMEXP = [7, 17]
DOWN = [10, 11, 12, 13, 18, 19, 22]
CHOICES = 16


def part_cols(part):
    return slice(TT * PARTS[part][0], TT * (PARTS[part][-1] + 1))


def part_of(t):
    return 0 if t in PARTS[0] else 1


def by_scalar_engine(u):
    return u % 2 == 0


def vit_tower_kernel(nc, x, tok_w, tok_b, ln_w, ln_b, w_qkv, w_proj, b_proj, s_q, s_k, s_v, s_attn,
                     s_after, enc_w, enc_b, sw_w, sw_b, w1, b1, w2, b2, const, out):
    f32, f32r, bf16 = mybir.dt.float32, mybir.dt.float32r, mybir.dt.bfloat16
    u8, i8, f8 = mybir.dt.uint8, mybir.dt.int8, mybir.dt.float8e4
    ALU, ACT, AX = mybir.AluOpType, mybir.ActivationFunctionType, mybir.AxisListType
    ctx = ExitStack()
    with ctx:
        def sb(name, shape, dtype):
            return ctx.enter_context(nc.sbuf_tensor(name, shape, dtype))

        def pb(name, shape):
            return ctx.enter_context(nc.psum_tensor(name, shape, f32))

        def sem(name):
            return ctx.enter_context(nc.semaphore(name))

        const_sb = sb("const_sb", [128, C_ALL], f32)
        we = sb("we", [128, KC, EMBED], f32)
        lnw = sb("lnw", [TT, EMBED], f32)
        lnb = sb("lnb", [TT, EMBED], f32)
        raw_q_a = sb("raw_q_a", [128, 3 * EMBED], f32)
        raw_q_b = sb("raw_q_b", [128, 3 * EMBED], f32)
        raw_1_a = sb("raw_1_a", [128, FF], f32)
        raw_1_b = sb("raw_1_b", [128, FF], f32)
        raw_p_a = sb("raw_p_a", [128, EMBED], f32)
        raw_p_b = sb("raw_p_b", [LO + 1, EMBED], f32)
        raw_24 = sb("raw_24", [24, 2 * EMBED], f32)
        scratch_a = sb("scratch_a", [128, 2 * EMBED], f32)
        scratch_b = sb("scratch_b", [128, 2 * EMBED], f32)
        wq_hi_a = sb("wq_hi_a", [128, 576], f32r)
        wq_lo_a = sb("wq_lo_a", [128, 576], f32r)
        wq_hi_b = sb("wq_hi_b", [128, 576], f32r)
        wq_lo_b = sb("wq_lo_b", [128, 576], f32r)
        w1_hi_a = sb("w1_hi_a", [128, FF], f32r)
        w1_lo_a = sb("w1_lo_a", [128, FF], f32r)
        w1_hi_b = sb("w1_hi_b", [128, FF], f32r)
        w1_lo_b = sb("w1_lo_b", [LO + EXPERTS, FF], f32r)
        wr_hi_a = sb("wr_hi_a", [128, EXPERTS], f32r)
        wr_lo_a = sb("wr_lo_a", [128, EXPERTS], f32r)
        wr_hi_b = sb("wr_hi_b", [128, EXPERTS], f32r)
        wr_lo_b = sb("wr_lo_b", [128, EXPERTS], f32r)
        wr_f = sb("wr_f", [128, 2, EXPERTS], f32)
        encw = sb("encw", [HIDDEN, EMBED + LO], f32)
        encb = sb("encb", [HIDDEN, 1], f32)
        sww = sb("sww", [HIDDEN, EXPERTS], f32)
        swb = sb("swb", [EXPERTS, 1], f32)
        br = sb("br", [EXPERTS, 1], f32)
        w2_sb = sb("w2_sb", [128, FC, EMBED], f32)
        b1_sb = sb("b1_sb", [128, FC], f32)
        wp_a = sb("wp_a", [128, 3, EMBED], bf16)
        wp_b = sb("wp_b", [LO + 1, 3, EMBED], bf16)
        rows24 = sb("rows24", [24, 2, EMBED], bf16)
        parts24 = sb("parts24", [24, 3, 2 * EMBED], bf16)
        first24 = sb("first24", [24, TT], bf16)
        ident_b = sb("ident_b", [TT, TT], bf16)
        scal = sb("scal", [128, 5], f32)
        rec = sb("rec", [128, 5], f32)
        inv_rows = sb("inv_rows", [128, 3], f32)
        c_prob = sb("c_prob", [128, 1], f32)
        c_out = sb("c_out", [128, 1], f32)
        proj_scale = sb("proj_scale", [128, 1], f32)
        products = sb("products", [128, 2], f32)
        warm = sb("warm", [128, 1], f32)

        x_sb = sb("x_sb", [128, NT, KC, TT], f32)
        st1 = sb("st1", [TT, NT, 6], f32)
        mv1 = sb("mv1", [TT, NT, 2], f32)
        ve1 = sb("ve1", [TT, NT, 1], f32)
        rs1 = sb("rs1", [TT, NT, 1], f32)
        nb1 = sb("nb1", [TT, NT, 1], f32)
        st2 = sb("st2", [TT, NT, 6], f32)
        mv2 = sb("mv2", [TT, NT, 2], f32)
        ve2 = sb("ve2", [TT, NT, 1], f32)
        rs2 = sb("rs2", [TT, NT, 1], f32)
        st3 = sb("st3", [TT, NT, 6], f32)
        mv3 = sb("mv3", [TT, NT, 2], f32)
        ve3 = sb("ve3", [TT, NT, 1], f32)
        rs3 = sb("rs3", [TT, NT, 1], f32)
        y1 = sb("y1", [TT, 2, EMBED], f32)
        n1 = sb("n1", [TT, 2, EMBED], f32)
        m1 = sb("m1", [TT, 2, EMBED], f32)
        h0 = sb("h0", [TT, 2, NT, EMBED], f32)
        h1 = sb("h1", [TT, 2, NT, EMBED], f32)
        xn2 = sb("xn2", [TT, 2, EMBED], f32)
        xn3 = sb("xn3", [TT, 2, EMBED], f32)
        a_hi = sb("a_hi", [128, 2, TOK], f32r)
        a_lo = sb("a_lo", [128, 2, TOK], f32r)
        a_b = sb("a_b", [128, 2, TOK], f32r)
        f_hi = sb("f_hi", [128, 2, TOK], f32r)
        f_lo = sb("f_lo", [128, 2, TOK], f32r)
        f_b = sb("f_b", [128, 2, TOK], f32r)
        f_c = sb("f_c", [LO + EXPERTS, 2, TOK], f32r)
        rows8 = sb("rows8", [128, 3, TOK], i8)
        q_a = sb("q_a", [128, TOK], bf16)
        q_b = sb("q_b", [LO, TOK], bf16)
        k_a = sb("k_a", [128, 2, TOK], bf16)
        k_b = sb("k_b", [LO, 2, TOK], bf16)
        v8 = sb("v8", [KEYS, GI, 2 * EMBED], i8)
        v_pad = sb("v_pad", [KEYS, 2 * GI, PAIRS, 2, 32], bf16)
        relu8 = sb("relu8", [KEYS, 2, 2, 2 * SEQ], u8)
        prob = sb("prob", [KEYS, 4, 2, 2 * SEQ], u8)
        o8_a = sb("o8_a", [128, TOK], i8)
        o8_b = sb("o8_b", [LO, TOK], i8)
        o_a = sb("o_a", [128, TOK], bf16)
        o_b = sb("o_b", [LO + 1, TOK], bf16)
        logits_t = sb("logits_t", [EXPERTS, TOK], f32)
        logit = sb("logit", [TT, NT, EXPERTS], f32)
        below = sb("below", [TT, NT, EXPERTS], f32)
        econst = sb("econst", [TT, NT, EXPERTS], f32)
        expd = sb("expd", [TT, NT, EXPERTS], f32)
        top = sb("top", [TT, NT], f32)
        score = sb("score", [TT, NT, EXPERTS], f32)
        score2 = sb("score2", [TT, NT, EXPERTS], f32)
        best = sb("best", [TT, NT], f32)
        onehot3 = sb("onehot3", [TT, NT, 24], bf16)
        sume = sb("sume", [TT, NT], f32)
        pmax = sb("pmax", [TT, NT], f32)
        one_t = sb("one_t", [24, TOK], bf16)
        hid = sb("hid", [128, FC, TOK], f32)
        out_sb = sb("out_sb", [TT, 2, EMBED], f32)

        scores_ps = pb("scores_ps", [128, 2, 512])
        heads_ps = pb("heads_ps", [128, 512])
        embed_ps = pb("embed_ps", [128, 512])
        turn_ps = pb("turn_ps", [128, 512])
        wide_ps = pb("wide_ps", [128, 512])
        proj_ps = pb("proj_ps", [128, 512])
        route_ps = pb("route_ps", [128, 512])

        loaded = [sem(f"loaded{n}") for n in range(3)]
        set_dve = sem("set_dve")
        set_pe = sem("set_pe")
        set_pool = sem("set_pool")
        warmed = sem("warmed")
        x_in = [sem(f"x_in{t}") for t in range(NT)]
        embedded = sem("embedded")
        act_y = sem("act_y")
        dve_st1 = sem("dve_st1")
        dve_mv1 = sem("dve_mv1")
        pool_ve1 = sem("pool_ve1")
        pool_rs1 = sem("pool_rs1")
        dve_nb1 = sem("dve_nb1")
        act_n1 = sem("act_n1")
        pool_m1 = sem("pool_m1")
        pool_h0 = sem("pool_h0")
        dve_st2 = sem("dve_st2")
        dve_mv2 = sem("dve_mv2")
        pool_ve2 = sem("pool_ve2")
        pool_rs2 = sem("pool_rs2")
        dve_xn2 = sem("dve_xn2")
        turned = sem("turned")
        act_hi = sem("act_hi")
        dve_lo = sem("dve_lo")
        rows_made = sem("rows_made")
        rows_out = sem("rows_out")
        rows_clip = sem("rows_clip")
        v_clip = sem("v_clip")
        qk_made = sem("qk_made")
        act_relu = sem("act_relu")
        prob_out = sem("prob_out")
        av_made = sem("av_made")
        heads_out = sem("heads_out")
        heads_clip = sem("heads_clip")
        projected = sem("projected")
        dve_h1 = sem("dve_h1")
        dve_st3 = sem("dve_st3")
        dve_mv3 = sem("dve_mv3")
        pool_ve3 = sem("pool_ve3")
        pool_rs3 = sem("pool_rs3")
        dve_xn3 = sem("dve_xn3")
        routed = sem("routed")
        logits_out = sem("logits_out")
        logits_turned = sem("logits_turned")
        choose = sem("choose")
        pool_exp = sem("pool_exp")
        spread = sem("spread")
        spread_out = sem("spread_out")
        up_made = sem("up_made")
        gelu_out = sem("gelu_out")
        dve_sum = sem("dve_sum")
        down_made = sem("down_made")
        result = sem("result")
        stored = [sem(f"stored{p}") for p in range(2)]

        TURNS = []
        for s in range(SLOTS):
            TURNS += [(1, t) for t in at(TURN2, s)] + [(2, t) for t in at(TURN3, s)]
            TURNS += [(3, t) for t in at(TURN3, s + SLOTS)]

        class Turns:

            def before(self, groups, n):
                return self.value(groups) + sum(groups[TURNS[m][0] - 1] is not None for m in range(n))

            def value(self, groups):
                back, any_ = next((n, g) for n, g in enumerate(groups) if g is not None)
                if not isinstance(any_.loop, int):
                    late = sum(t >= SLOTS for t in TURN3)
                    return (any_.loop + (any_.offset + back)) * (2 * NT) - (NT + late)
                done = 0
                for i in range(any_.offset + back):
                    st = stages(0, i, i % 2)
                    done += sum(st[k - 1] is not None for k, _ in TURNS)
                return done

        turns = Turns()

        WIDE = [(s, 1, rows_out, EVACS, STEPS.index(x) + 1) for s, x in FIRST_STEPS.items()]
        WIDE += [(s, 2, rows_out, EVACS, STEPS.index(x) + 1) for s, x in SECOND_STEPS.items()]
        WIDE += [(s, 3, gelu_out, 8, n + 1) for n, s in enumerate(UP) if n % 2 == 0]
        WIDE += [(s, 3, result, NT, t + 1) for t, s in enumerate(DOWN) if t % 2]
        PROJECTED = [(s, 2, dve_h1, NT, t + 1) for t, s in enumerate(PROJ) if s < SLOTS]
        PROJECTED += [(s - SLOTS, 3, dve_h1, NT, t + 1) for t, s in enumerate(PROJ) if s >= SLOTS]
        PROJECTED += [(s, 3, result, NT, t + 1) for t, s in enumerate(DOWN) if t % 2 == 0]
        ROUTED = [(s, 3, logits_out, 2, n + 1) for n, s in enumerate(ROUTE)]
        ROUTED += [(s, 3, choose, CHOICES, 8 * n + 1) for n, s in enumerate(TURN_LOGITS)]
        ROUTED += [(s, 3, spread_out, 2, n + 1) for n, s in enumerate(SPREAD)]
        ROUTED += [(s, 3, gelu_out, 8, n + 1) for n, s in enumerate(UP) if n % 2]

        def empty(eng, users, groups, slot):
            users = sorted(users, key=lambda x: x[0])
            assert len({x[0] for x in users}) == len(users)
            back, g = next((n, g) for n, g in enumerate(groups) if g is not None)
            number, loop = g.offset + back, g.loop
            n = [x[0] for x in users].index(slot)
            while True:
                n -= 1
                if n < 0:
                    n, number = len(users) - 1, number - 1
                    groups = stages(loop, number, number % 2)
                    if isinstance(loop, int) and number < 0:
                        return
                _, stage, signal, per_group, k = users[n]
                if groups[stage - 1] is not None:
                    return wait(eng, signal, groups[stage - 1].count(per_group, k))

        block = ctx.enter_context(nc.Block())

        def column(ap, n):
            return ap.rearrange("(a b) -> a b", b=1)

        embed_loads = [(const_sb[:, :], const)]
        embed_loads += [(raw_24[8 * j:8 * j + 8, 0:EMBED], b2) for j in range(3)]
        embed_loads += [(raw_24[:, EMBED:2 * EMBED], tok_b.partition_broadcast(24)), (we[:, :, :], tok_w),
                        (lnw[:, :], ln_w.partition_broadcast(TT)), (lnb[:, :], ln_b.partition_broadcast(TT))]
        attention_loads = [(scal[:, n:n + 1], s.partition_broadcast(128))
                           for n, s in enumerate((s_q, s_k, s_v, s_attn, s_after))]
        attention_loads += [
            (raw_q_a[:, :], w_qkv[0:128, :]),
            (raw_q_b[0:LO, :], w_qkv[128:EMBED, :]), (raw_q_b[LO:128, :], w_qkv[128:EMBED, :]),
            (raw_p_a[:, :], w_proj[0:128, :]), (raw_p_b[0:LO, :], w_proj[128:EMBED, :]),
            (raw_p_b[LO:LO + 1, :], b_proj.rearrange("(a b) -> a b", a=1)),
        ]
        expert_loads = [
            (encw[:, 0:EMBED], enc_w), (encw[:, EMBED:EMBED + LO], enc_w[:, 128:EMBED]),
            (encb[:, :], column(enc_b, HIDDEN)), (sww[:, :], sw_w), (swb[:, :], column(sw_b, EXPERTS)),
            (raw_1_a[:, :], w1[0:128, :]),
            (raw_1_b[0:LO, :], w1[128:EMBED, :]), (raw_1_b[LO:128, :], w1[128:EMBED, :]),
            (w2_sb[:, :, :], w2), (b1_sb[:, :], b1),
        ]
        all_loads = [embed_loads, attention_loads, expert_loads]
        SET_EMBED, SET_ALL = 9, 49
        ROUTER_PRODUCT, SET_ATTENTION, SET_PROJECTION, SET_EXPERTS = 6, 3, 7, 12

        def everything_loaded(eng):
            for signal, lot in zip(loaded, all_loads):
                eng.wait_ge(signal, 16 * len(lot))

        def is_first(g):
            return isinstance(g.loop, int) and g.offset == 0

        @block.sync
        def _(sync):
            def load_tile(g, t):
                wait(sync, embedded, g.count(NT, t + 1 - NT))
                src = x[g.loop + g.offset, t] if not isinstance(g.loop, int) else x[g.offset, t]
                sync.dma_start(x_sb[:, t], src).then_inc(x_in[t], 16)

            first = Group(0, 0, 0)
            for dst, src in embed_loads[:5]:
                sync.dma_start(dst, src).then_inc(loaded[0], 16)
            load_tile(first, 0)
            for dst, src in embed_loads[5:]:
                sync.dma_start(dst, src).then_inc(loaded[0], 16)
            for t in range(1, 4):
                load_tile(first, t)
            for dst, src in attention_loads:
                sync.dma_start(dst, src).then_inc(loaded[1], 16)
            for t in range(4, NT):
                load_tile(first, t)
            for dst, src in expert_loads:
                sync.dma_start(dst, src).then_inc(loaded[2], 16)

            def body(one, two, three):
                for s in range(SLOTS + 2):
                    if three:
                        for t in at(DOWN, s - 2):
                            sync.wait_ge(result, three.count(NT, t + 1))
                            row = three.loop + three.offset if not isinstance(three.loop, int) else three.offset
                            sync.dma_start(out[row, t], out_sb[:, (three.parity + t) % 2]).then_inc(
                                stored[(three.parity + t) % 2], 16)
                    if one:
                        for t in at(EMBED_END, s - 1):
                            if isinstance(one.loop, int) and one.offset == GROUPS - 1:
                                continue
                            nxt = Group(one.loop, one.offset + 1, 1 - one.parity)
                            load_tile(nxt, t)

            passes(sync, body)
            for p in range(2):
                sync.wait_ge(stored[p], 16 * (GROUPS * NT // 2))

        @block.tensor
        def _(pe):
            ident = const_sb[0:TT, C_IDENT:C_IDENT + TT]

            def router_product():
                pe.wait_ge(loaded[2], 16 * len(expert_loads))
                pe.matmul(proj_ps[:, 0:EXPERTS], encw[:, 0:128], sww[:, :], start=True, stop=True)
                pe.matmul(proj_ps[:, EXPERTS:2 * EXPERTS], encw[:, 128:EMBED + LO], sww[:, :],
                          start=True, stop=True)
                pe.matmul(proj_ps[0:EXPERTS, 2 * EXPERTS:2 * EXPERTS + 1], sww[:, :], encb[:, :],
                          start=True, stop=True).then_inc(set_pe, 1)

            def split_product(dst, hi_a, lo_a, hi_b, lo_b, left, right_hi, right_lo, right_b, moving):
                terms = [(hi_a, right_hi), (hi_a, right_lo), (lo_a, right_hi), (hi_b, right_b),
                         (lo_b[0:LO], right_b[0:LO])]
                for n, (w, a) in enumerate(terms):
                    w, a = w[:, left], a
                    lhs, rhs = (a, w) if moving == "weights" else (w, a)
                    last = pe.matmul(dst, lhs, rhs, start=n == 0, stop=n == 4)
                return last

            def embed(g, t, j):
                dst = embed_ps[0:TT, 0:EMBED]
                if j == 0:
                    pe.wait_ge(x_in[t], g.count(16, 16))
                    wait(pe, act_y, g.count(NT, t))
                    pe.matmul(dst, first24[:, :], rows24[:, 1], start=True, stop=False)
                last = pe.matmul(dst, x_sb[:, t, j], we[:, j], start=False, stop=j == KC - 1)
                if j == KC - 1:
                    last.then_inc(embedded, 1)

            def turn(groups, n):
                k, t = TURNS[n]
                g = groups[k - 1]
                if g is None:
                    return
                src, made = (xn2, dve_xn2) if k == 1 else (xn3, dve_xn3)
                pe.wait_ge(made, g.count(NT, t + 1))
                wait(pe, dve_lo, turns.before(groups, n))
                rows = src[:, (g.parity + t) % 2]
                pe.transpose(turn_ps[:, 0:TT], rows[:, 0:128], ident)
                pe.transpose(turn_ps[0:LO, TT:2 * TT], rows[:, 128:EMBED], ident).then_inc(turned, 1)

            def rows(g, m, half):
                tiles = 4 if half == 0 else NT
                last_turn = max(i for i, x in enumerate(TURNS) if x[0] == 1 and x[1] < tiles)
                need_split(g, last_turn)
                cols = slice(half * HALF, (half + 1) * HALF)
                split_product(wide_ps[:, 0:HALF], wq_hi_a, wq_lo_a, wq_hi_b, wq_lo_b,
                              slice(128 * m, 128 * m + 128), a_hi[:, g.parity, cols],
                              a_lo[:, g.parity, cols], a_b[:, g.parity, cols],
                              "activations").then_inc(rows_made, 1)

            def need_split(g, last_turn):
                pe.wait_ge(dve_lo, turns.before(stages(g.loop, g.offset, g.parity), last_turn + 1))

            def values(g, n):
                tiles = 4 if n < 2 else NT
                need_split(g, max(i for i, x in enumerate(TURNS) if x[0] == 1 and x[1] < tiles))
                for c in range(2):
                    cols = slice(n * SEQ + c * KEYS, n * SEQ + (c + 1) * KEYS)
                    last = split_product(wide_ps[0:KEYS, EMBED * c:EMBED * (c + 1)], wq_hi_a, wq_lo_a,
                                         wq_hi_b, wq_lo_b, slice(384, 576), a_hi[:, g.parity, cols],
                                         a_lo[:, g.parity, cols], a_b[:, g.parity, cols], "weights")
                last.then_inc(rows_made, 1)

            def step(groups, g, slot, what):
                empty(pe, WIDE, groups, slot)
                if what[0] == "rows":
                    rows(g, *what[1:])
                else:
                    values(g, what[1])

            def head_rows(pair):
                return ("a", 32 * pair) if pair < 4 else ("b", 32 * (pair - 4))

            def qk(g, u):
                n, place = divmod(u, PAIRS)
                pair, odd = place - place % 2, place % 2
                side, row = head_rows(pair)
                q, k = (q_a, k_a) if side == "a" else (q_b, k_b)
                if pair in (0, 4) and odd == 0:
                    m = 1 if side == "a" else 2
                    pe.wait_ge(rows_clip, g.count(6, clips_until(m, n // 2)))
                before = u - 1 if u else SLOTS - 1
                if by_scalar_engine(before):
                    wait(pe, act_relu, g.count(DUOS, (u + 1) // 2))
                else:
                    wait(pe, prob_out, g.count(SLOTS, u))
                for c in range(2):
                    for side in range(2):
                        rows = slice(row + 32 * side, row + 32 * side + 32)
                        keys = k[rows, odd, n * SEQ + c * KEYS:n * SEQ + (c + 1) * KEYS]
                        last = pe.matmul(scores_ps[0:KEYS, side, c * SEQ:(c + 1) * SEQ], keys,
                                         q[rows, n * SEQ:(n + 1) * SEQ], start=True, stop=True)
                last.then_inc(qk_made, 1)

            def av_ready(g, duo):
                n, first = divmod(2 * duo, PAIRS)
                pe.wait_ge(prob_out, g.count(SLOTS, 2 * duo + 2))
                if first == 0:
                    pe.wait_ge(v_clip, g.count(GI, n + 1))
                    wait(pe, heads_out, g.count(GI, n))

            def av(g, duo):
                for k in range(4):
                    odd, c = divmod(k, 2)
                    for side_ in range(2):
                        u = 2 * duo + odd
                        n, pair = divmod(2 * duo + side_, PAIRS)
                        side, row = head_rows(pair)
                        col = 0 if side == "a" else SEQ
                        last = pe.matmul(heads_ps[row:row + 32, col:col + SEQ],
                                         v_pad[:, 2 * n + c, pair, odd],
                                         prob[:, u % 4, side_, c * SEQ:(c + 1) * SEQ].bitcast(f8),
                                         start=k == 0, stop=k == 3)
                last.then_inc(av_made, 1)

            def project(groups, g, t):
                image = (TT * (t + 1) - 1) // SEQ
                pe.wait_ge(heads_clip, g.count(GI, image + 1))
                empty(pe, PROJECTED, groups, PROJ[t] % SLOTS)
                dst = proj_ps[0:TT, 0:EMBED]
                cols = slice(TT * t, TT * (t + 1))
                for j in range(3):
                    pe.matmul(dst, o_a[:, cols], wp_a[:, j], start=j == 0, stop=False)
                    last = pe.matmul(dst, o_b[:, cols], wp_b[:, j], start=False, stop=j == 2)
                last.then_inc(projected, 1)

            def route(groups, g, part):
                cols = part_cols(part)
                empty(pe, ROUTED, groups, ROUTE[part])
                need_split3(g, PARTS[part][-1] + 1)
                split_product(route_ps[0:EXPERTS, 0:cols.stop - cols.start], wr_hi_a, wr_lo_a, wr_hi_b,
                              wr_lo_b, slice(0, EXPERTS), f_hi[:, g.parity, cols],
                              f_lo[:, g.parity, cols], f_b[:, g.parity, cols],
                              "activations").then_inc(routed, 1)

            def need_split3(g, tiles):
                this = max([i for i, x in enumerate(TURNS) if x[0] == 3 and x[1] < tiles], default=None)
                if this is None:
                    this = max(i for i, x in enumerate(TURNS) if x[0] == 2 and x[1] < tiles)
                    i = g.offset + 1
                else:
                    i = g.offset + 2
                pe.wait_ge(dve_lo, turns.before(stages(g.loop, i, i % 2), this + 1))

            def turn_logits(groups, g, part):
                empty(pe, ROUTED, groups, TURN_LOGITS[part])
                for n, t in enumerate(PARTS[part]):
                    last = pe.matmul(route_ps[0:TT, EXPERTS * n:EXPERTS * (n + 1)],
                                     logits_t[:, TT * t:TT * (t + 1)], ident[0:EXPERTS, 0:EXPERTS],
                                     start=True, stop=True)
                last.then_inc(logits_turned, 1)

            def spread_choice(g, part):
                pe.wait_ge(choose, g.count(CHOICES, 8 * (part + 1)))
                for n, t in enumerate(PARTS[part]):
                    last = pe.matmul(route_ps[0:24, TT * n:TT * (n + 1)], onehot3[:, t], ident_b[:, :],
                                     start=True, stop=True)
                last.then_inc(spread, 1)

            def up(groups, g, n):
                part, m = divmod(n, FC)
                bank, users = (wide_ps, WIDE) if n % 2 == 0 else (route_ps, ROUTED)
                empty(pe, users, groups, UP[n])
                if m == 0:
                    pe.wait_ge(spread_out, g.count(2, part + 1))
                cols, left = part_cols(part), slice(128 * m, 128 * (m + 1))
                dst = bank[:, 0:cols.stop - cols.start]
                terms = [(w1_hi_a, f_hi), (w1_hi_a, f_lo), (w1_lo_a, f_hi), (w1_hi_b, f_b), (w1_lo_b, f_c)]
                for k, (w, a) in enumerate(terms):
                    last = pe.matmul(dst, w[:, left], a[:, g.parity, cols], start=k == 0, stop=k == 4)
                last.then_inc(up_made, 1)

            def down(groups, g, t):
                pe.wait_ge(gelu_out, g.count(8, 4 * (part_of(t) + 1)))
                bank, users = (proj_ps, PROJECTED) if t % 2 == 0 else (wide_ps, WIDE)
                empty(pe, users, groups, DOWN[t])
                dst, cols = bank[0:TT, 0:EMBED], slice(TT * t, TT * (t + 1))
                pe.matmul(dst, one_t[:, cols], rows24[:, 0], start=True, stop=False)
                for m in range(FC):
                    last = pe.matmul(dst, hid[:, m, cols], w2_sb[:, m], start=False, stop=m == FC - 1)
                last.then_inc(down_made, 1)

            pe.wait_ge(set_dve, SET_EMBED)

            def body(*groups):
                one, two, three = groups
                for s in range(SLOTS):
                    if one and is_first(one):
                        if s == ROUTER_PRODUCT:
                            router_product()
                        if s == min(FIRST_STEPS):
                            pe.wait_ge(set_dve, SET_ALL)
                    if two:
                        qk(two, s)
                    for n, (k, t) in enumerate(TURNS):
                        if k == 1 and TURN2[t] == s:
                            turn(groups, n)
                    heads, duo = (two, s // 2 - 1) if s > 0 else (three, DUOS - 1)
                    if heads and s % 2 == 0:
                        av_ready(heads, duo)
                    if one and s in FIRST_STEPS:
                        step(groups, one, s, FIRST_STEPS[s])
                    work = embeds_of(s) if one else []
                    for t, j in work[:1]:
                        embed(one, t, j)
                    if three and s > EMBED_END[-1]:
                        for n in at(UP, s):
                            up(groups, three, n)
                    for g, late in ((two, 0), (three, SLOTS)):
                        if g:
                            for t in at(PROJ, s + late):
                                project(groups, g, t)
                    if heads and s % 2 == 0:
                        av(heads, duo)
                    if two and s in SECOND_STEPS:
                        step(groups, two, s, SECOND_STEPS[s])
                    if three:
                        for part in at(ROUTE, s):
                            route(groups, three, part)
                    if three:
                        for part in at(TURN_LOGITS, s):
                            turn_logits(groups, three, part)
                    if three:
                        for part in at(SPREAD, s):
                            spread_choice(three, part)
                    if three and s <= EMBED_END[-1]:
                        for n in at(UP, s):
                            up(groups, three, n)
                    for t, j in work[1:]:
                        embed(one, t, j)
                    if three and s <= EMBED_END[-1]:
                        for t in at(DOWN, s):
                            down(groups, three, t)
                    for n, (k, t) in enumerate(TURNS):
                        if k != 1 and TURN3[t] % SLOTS == s:
                            turn(groups, n)
                    if three and s > EMBED_END[-1]:
                        for t in at(DOWN, s):
                            down(groups, three, t)

            passes(pe, body)

        def reads_done(eng, g, k):
            if k == 1:
                wait(eng, rows_made, g.count(EVACS, -EVACS))
            else:
                wait(eng, up_made, g.count(8, -8))

        @block.scalar
        def _(act):
            act.wait_ge(set_pool, 1)
            act.activation(warm[:, :], warm[:, :], ACT.Gelu).then_inc(warmed, 1)

            def embed_evac(g, t):
                act.wait_ge(embedded, g.count(NT, t + 1))
                wait(act, act_n1, g.count(NT, t - 1))
                act.activation(y1[:, (g.parity + t) % 2], embed_ps[0:TT, 0:EMBED],
                               ACT.Copy).then_inc(act_y, 1)

            def norm1(g, t):
                half = (g.parity + t) % 2
                act.wait_ge(dve_nb1, g.count(NT, t + 1))
                wait(act, pool_m1, g.count(NT, t - 1))
                act.activation(n1[:, half], y1[:, half], ACT.Identity,
                               scale=rs1[:, t], bias=nb1[:, t]).then_inc(act_n1, 1)

            def high(groups, n):
                k, t = TURNS[n]
                g = groups[k - 1]
                if g is None:
                    return
                hi, both = (a_hi, a_b) if k == 1 else (f_hi, f_b)
                cols = slice(TT * t, TT * (t + 1))
                act.wait_ge(turned, turns.before(groups, n) + 1)
                if t == 0:
                    reads_done(act, g, k)
                act.activation(hi[:, g.parity, cols], turn_ps[:, 0:TT], ACT.Copy)
                last = act.activation(both[0:LO, g.parity, cols], turn_ps[0:LO, TT:2 * TT], ACT.Copy)
                if k != 1:
                    last = act.activation(f_c[0:LO, g.parity, cols], turn_ps[0:LO, TT:2 * TT], ACT.Copy)
                last.then_inc(act_hi, 1)

            def relu(g, u):
                act.wait_ge(qk_made, g.count(SLOTS, u + 1))
                wait(act, prob_out, g.count(SLOTS, u - 3))
                act.activation(relu8[:, u // 2 % 2], scores_ps[0:KEYS, :, 0:2 * SEQ], ACT.Relu,
                               scale=c_prob[0:KEYS, :]).then_inc(act_relu, 1)

            def step_evac(g, what):
                act.wait_ge(rows_made, g.count(EVACS, STEPS.index(what) + 1))
                if what[0] == "rows":
                    m, half = what[1:]
                    wait(act, rows_clip, g.count(6, clips_until(m, half) - 6))
                    act.activation(rows8[:, m, half * HALF:(half + 1) * HALF], wide_ps[:, 0:HALF],
                                   ACT.Identity, scale=inv_rows[:, m:m + 1]).then_inc(rows_out, 1)
                else:
                    n = what[1]
                    wait(act, v_clip, g.count(GI, n + 1 - GI))
                    act.activation(v8[:, n], wide_ps[0:KEYS, 0:2 * EMBED], ACT.Identity,
                                   scale=rec[0:KEYS, 2:3]).then_inc(rows_out, 1)

            def heads_evac(g, n):
                cols = slice(SEQ * n, SEQ * (n + 1))
                act.wait_ge(av_made, g.count(DUOS, PAIRS // 2 * (n + 1)))
                wait(act, heads_clip, g.count(GI, n + 1 - GI))
                act.activation(o8_a[:, cols], heads_ps[:, 0:SEQ], ACT.Identity, scale=c_out[:, :])
                act.activation(o8_b[:, cols], heads_ps[0:LO, SEQ:2 * SEQ], ACT.Identity,
                               scale=c_out[0:LO, :]).then_inc(heads_out, 1)

            def gelu(g, n):
                part, m = divmod(n, FC)
                bank = wide_ps if n % 2 == 0 else route_ps
                cols = part_cols(part)
                act.wait_ge(up_made, g.count(8, n + 1))
                if n == 0:
                    wait(act, down_made, g.count(NT, 0))
                act.activation(hid[:, m, cols], bank[:, 0:cols.stop - cols.start], ACT.Gelu,
                               bias=b1_sb[:, m:m + 1]).then_inc(gelu_out, 1)

            def body(*groups):
                one, two, three = groups
                for s in range(SLOTS):
                    if one and is_first(one) and s == min(FIRST_STEPS):
                        everything_loaded(act)
                        act.wait_ge(set_dve, SET_ALL)
                    if two and by_scalar_engine(s):
                        relu(two, s)
                    for n, (k, t) in enumerate(TURNS):
                        if k == 1 and TURN2[t] == s:
                            high(groups, n)
                    if one:
                        for t in at(NORM1, s):
                            norm1(one, t)
                    if two and s in SECOND_STEPS:
                        step_evac(two, SECOND_STEPS[s])
                    if three:
                        for n in at(UP, s):
                            gelu(three, n)
                    if one and s in FIRST_STEPS:
                        step_evac(one, FIRST_STEPS[s])
                    if one:
                        for t in at(EVAC1, s):
                            embed_evac(one, t)
                    for n, (k, t) in enumerate(TURNS):
                        if k != 1 and TURN3[t] % SLOTS == s:
                            high(groups, n)
                    for g, late in ((two, 0), (three, SLOTS)):
                        if g:
                            for n in at(HEADS_EVAC, s + late):
                                heads_evac(g, n)

            passes(act, body)

        @block.gpsimd
        def _(pool):
            pool.memset(warm[:, :], 0.0).then_inc(set_pool, 1)
            pool.memset(v_pad[:, :, :, :, :], 0.0).then_inc(set_pool, 1)
            pool.wait_ge(loaded[0], 16 * len(embed_loads))

            def rstd(g, t, mv_sem, mv, ve, rs, ve_sem, rs_sem):
                pool.wait_ge(mv_sem, g.count(NT, t + 1))
                pool.tensor_tensor(ve[:, t], mv[:, t, 1:2], const_sb[0:TT, C_EPS:C_EPS + 1],
                                   ALU.add).then_inc(ve_sem, 1)
                pool.wait_ge(ve_sem, g.count(NT, t + 1))
                pool.tensor_tensor(rs[:, t], ve[:, t], const_sb[0:TT, C_HALFNEG:C_HALFNEG + 1],
                                   ALU.pow).then_inc(rs_sem, 1)

            def affine(g, t):
                half = (g.parity + t) % 2
                pool.wait_ge(act_n1, g.count(NT, t + 1))
                pool.tensor_tensor(m1[:, half], n1[:, half], lnw[:, :], ALU.mult).then_inc(pool_m1, 1)
                pool.wait_ge(pool_m1, g.count(NT, t + 1))
                wait(pool, dve_h1, g.count(NT, t + 1 - 2 * NT))
                pool.tensor_tensor(h0[:, g.parity, t], m1[:, half], lnb[:, :], ALU.add).then_inc(pool_h0, 1)

            def body(*groups):
                one, two, three = groups
                for s in range(SLOTS):
                    if one and is_first(one) and s == SLOTS - 1:
                        pool.wait_ge(set_dve, SET_ALL)
                    if one:
                        for t in at(NORM1, s):
                            affine(one, t)
                    for part in at(CHOOSE, s) if three else []:
                        pool.wait_ge(choose, three.count(CHOICES, 8 * part + 3))
                        wait(pool, dve_sum, three.count(4, 2 * part - 2))
                        tiles = slice(PARTS[part][0], PARTS[part][-1] + 1)
                        pool.tensor_tensor(expd[:, tiles], econst[:, tiles], below[:, tiles],
                                           ALU.pow).then_inc(pool_exp, 1)
                    if one:
                        for t in at(JOIN1, s):
                            rstd(one, t, dve_mv1, mv1, ve1, rs1, pool_ve1, pool_rs1)
                    for g, late in ((two, 0), (three, SLOTS)):
                        if g:
                            for t in at(JOIN3, s + late):
                                rstd(g, t, dve_mv3, mv3, ve3, rs3, pool_ve3, pool_rs3)
                    if one:
                        for t in at(JOIN2, s):
                            rstd(one, t, dve_mv2, mv2, ve2, rs2, pool_ve2, pool_rs2)

            passes(pool, body)

        @block.vector
        def _(dve):
            done = [0]

            def setup(ins):
                done[0] += 1
                ins.then_inc(set_dve, 1)
                dve.wait_ge(set_dve, done[0])

            def split_r(hi, lo, src):
                setup(dve.tensor_copy(hi, src))
                setup(dve.tensor_tensor(lo, src[0:lo.shape[0]], hi[0:lo.shape[0]].bitcast(f32), ALU.subtract))

            def split_b(parts, src, rest):
                setup(dve.tensor_copy(parts[0], src))
                setup(dve.tensor_tensor(rest, src, parts[0], ALU.subtract))
                setup(dve.tensor_copy(parts[1], rest))
                setup(dve.tensor_tensor(rest, rest, parts[1], ALU.subtract))
                setup(dve.tensor_copy(parts[2], rest))

            def set_embedding():
                dve.wait_ge(loaded[0], 16 * len(embed_loads))
                bias_parts = [parts24[:, j] for j in range(3)]
                split_b(bias_parts, raw_24[:, :], scratch_a[0:24, :])
                setup(dve.tensor_scalar(scratch_b[0:24, :], bias_parts[0], const_sb[0:24, C_PART:C_PART + 1],
                                        None, ALU.mult))
                for j in (1, 2):
                    dst = scratch_b[0:24, :] if j == 1 else rows24[:, :, :].rearrange("p a b -> p (a b)")
                    setup(dve.scalar_tensor_tensor(dst, bias_parts[j], const_sb[0:24, C_PART + j:C_PART + j + 1],
                                                   scratch_b[0:24, :], ALU.mult, ALU.add))
                setup(dve.tensor_copy(first24[:, :], const_sb[0:24, C_FIRST:C_FIRST + TT]))

            def set_attention():
                dve.wait_ge(loaded[1], 16 * len(attention_loads))
                split_r(wq_hi_a[:, :], wq_lo_a[:, :], raw_q_a[:, :])
                split_r(wq_hi_b[:, :], wq_lo_b[:, :], raw_q_b[:, :])
                setup(dve.reciprocal(rec[:, :], scal[:, :]))
                setup(dve.tensor_copy(inv_rows[:, 0:2], rec[:, 0:2]))
                setup(dve.tensor_copy(inv_rows[0:LO, 2:3], rec[0:LO, 0:1]))
                setup(dve.tensor_copy(inv_rows[LO:128, 2:3], rec[LO:128, 1:2]))
                setup(dve.tensor_scalar(products[:, 0:1], scal[:, 0:1], scal[:, 1:2], DH ** -0.5 / SEQ,
                                        ALU.mult, ALU.mult))
                setup(dve.tensor_scalar(c_prob[:, :], products[:, 0:1], rec[:, 3:4], None, ALU.mult))
                setup(dve.tensor_scalar(products[:, 1:2], scal[:, 3:4], scal[:, 2:3], E4_STEP,
                                        ALU.mult, ALU.mult))
                setup(dve.tensor_scalar(c_out[:, :], products[:, 1:2], rec[:, 4:5], None, ALU.mult))

            def set_projection():
                setup(dve.tensor_copy(proj_scale[:, :], scal[:, 4:5]))
                setup(dve.memset(proj_scale[LO:LO + 1, :], 1.0))
                setup(dve.memset(o_b[LO:LO + 1, :], 1.0))
                for parts, src, scale in ((wp_a, raw_p_a, scal[:, 4:5]), (wp_b, raw_p_b, proj_scale[0:LO + 1])):
                    n = src.shape[0]
                    scaled, rest = scratch_a[0:n, 0:EMBED], scratch_b[0:n, 0:EMBED]
                    setup(dve.tensor_scalar(scaled, src[:, :], scale, None, ALU.mult))
                    split_b([parts[:, j] for j in range(3)], scaled, rest)

            def set_experts():
                dve.wait_ge(loaded[2], 16 * len(expert_loads))
                split_r(w1_hi_a[:, :], w1_lo_a[:, :], raw_1_a[:, :])
                split_r(w1_hi_b[:, :], w1_lo_b[0:LO, :], raw_1_b[:, :])
                setup(dve.tensor_copy(w1_lo_b[LO:LO + EXPERTS, :], const_sb[0:EXPERTS, C_SEL:C_SEL + FF]))
                setup(dve.tensor_copy(ident_b[:, :], const_sb[0:TT, C_IDENT:C_IDENT + TT]))
                setup(dve.tensor_copy(econst[:, :, :].rearrange("p a b -> p (a b)"),
                                      const_sb[0:TT, C_E:C_E + 1].broadcast_to([TT, NT * EXPERTS])))
                dve.wait_ge(set_pe, 1)
                setup(dve.tensor_copy(wr_f[:, :, :].rearrange("p a b -> p (a b)"), proj_ps[:, 0:2 * EXPERTS]))
                setup(dve.tensor_scalar(br[:, :], proj_ps[0:EXPERTS, 2 * EXPERTS:2 * EXPERTS + 1], swb[:, :],
                                        None, ALU.add))
                split_r(wr_hi_a[:, :], wr_lo_a[:, :], wr_f[:, 0])
                split_r(wr_hi_b[:, :], wr_lo_b[:, :], wr_f[:, 1])
                dve.wait_ge(set_pool, 2)
                assert done[0] == SET_ALL, done[0]

            set_embedding()
            assert done[0] == SET_EMBED

            def stats1(g, t):
                half = (g.parity + t) % 2
                dve.wait_ge(act_y, g.count(NT, t + 1))
                dve.bn_stats(st1[:, t], y1[:, half]).then_inc(dve_st1, 1)

            def bias1(g, t):
                dve.wait_ge(pool_rs1, g.count(NT, t + 1))
                dve.scalar_tensor_tensor(nb1[:, t], mv1[:, t, 0:1], -1.0, rs1[:, t], ALU.mult,
                                         ALU.mult).then_inc(dve_nb1, 1)

            def stats(g, t, src, src_sem, st, st_sem):
                dve.wait_ge(src_sem, g.count(NT, t + 1))
                dve.bn_stats(st[:, t], src[:, g.parity, t]).then_inc(st_sem, 1)

            def aggregated(groups, s):
                one, two, three = groups
                found = [(one, t, st1, mv1, dve_st1, dve_mv1) for t in at(JOIN1, s)]
                found += [(one, t, st2, mv2, dve_st2, dve_mv2) for t in at(JOIN2, s)]
                for g, slot in ((two, s), (three, s + SLOTS)):
                    found += [(g, t, st3, mv3, dve_st3, dve_mv3) for t in at(JOIN3, slot)]
                return [x for x in found if x[0]]

            def norm(groups, g, t, k, src, mv, rs, rs_sem, dst, dst_sem):
                dve.wait_ge(rs_sem, g.count(NT, t + 1))
                wait(dve, turned, before_turn(groups, g, t - 2, k))
                dve.tensor_scalar(dst[:, (g.parity + t) % 2], src[:, g.parity, t], mv[:, t, 0:1], rs[:, t],
                                  ALU.subtract, ALU.mult).then_inc(dst_sem, 1)

            def before_turn(groups, g, t, k):
                back = 0
                if t < 0:
                    back, t = 1, t + NT
                if k == 1:
                    stage = 1
                else:
                    stage = 2 if TURN3[t] < SLOTS else 3
                n = TURNS.index((stage, t))
                i = g.offset + stage - 1 - back
                if isinstance(g.loop, int) and i < 0:
                    return 0
                if isinstance(g.loop, int) and g.offset - back < 0:
                    return 0
                return turns.before(stages(g.loop, i, i % 2), n + 1)

            def low(groups, n):
                k, t = TURNS[n]
                g = groups[k - 1]
                if g is None:
                    return
                hi, lo, both = (a_hi, a_lo, a_b) if k == 1 else (f_hi, f_lo, f_b)
                cols = slice(TT * t, TT * (t + 1))
                dve.wait_ge(act_hi, turns.before(groups, n) + 1)
                dve.tensor_tensor(lo[:, g.parity, cols], turn_ps[:, 0:TT],
                                  hi[:, g.parity, cols].bitcast(f32), ALU.subtract)
                dve.tensor_tensor(both[LO:128, g.parity, cols], turn_ps[0:LO, TT:2 * TT],
                                  both[0:LO, g.parity, cols].bitcast(f32), ALU.subtract).then_inc(dve_lo, 1)

            def quantise(g, u):
                wait(dve, av_made, g.count(DUOS, (u - 4) // 2 + 1))
                if by_scalar_engine(u):
                    dve.wait_ge(act_relu, g.count(DUOS, u // 2 + 1))
                    dve.tensor_scalar(prob[:, u % 4], relu8[:, u // 2 % 2], 7.0, None,
                                      ALU.min).then_inc(prob_out, 1)
                else:
                    dve.wait_ge(qk_made, g.count(SLOTS, u + 1))
                    dve.tensor_scalar(prob[:, u % 4], scores_ps[0:KEYS, :, 0:2 * SEQ], c_prob[0:KEYS, :],
                                      7.0, ALU.mult, ALU.min).then_inc(prob_out, 1)

            def bounds(n, odd):
                return [const_sb[n, C_BOUND + 2 * odd + b:C_BOUND + 2 * odd + b + 1] for b in range(2)]

            def clip_rows(g, m, half):
                cols = slice(half * HALF, (half + 1) * HALF)
                dve.wait_ge(rows_out, g.count(EVACS, STEPS.index(("rows", m, half)) + 1))
                wait(dve, qk_made, g.count(SLOTS, (half + 1) * SLOTS // 2 - SLOTS))
                if m == 0:
                    last = dve.tensor_scalar(q_a[:, cols], rows8[:, 0, cols], -4.0, 3.0, ALU.max, ALU.min)
                elif m == 1:
                    for odd in range(2):
                        low_, high_ = bounds(slice(0, 128), odd)
                        last = dve.tensor_scalar(k_a[:, odd, cols], rows8[:, 1, cols], low_, high_,
                                                 ALU.max, ALU.min)
                else:
                    dve.tensor_scalar(q_b[:, cols], rows8[0:LO, 2, cols], -4.0, 3.0, ALU.max, ALU.min)
                    for odd in range(2):
                        low_, high_ = bounds(slice(LO, 128), odd)
                        last = dve.tensor_scalar(k_b[:, odd, cols], rows8[LO:128, 2, cols], low_, high_,
                                                 ALU.max, ALU.min)
                last.then_inc(rows_clip, 1)

            def clip_values(g, n):
                dve.wait_ge(rows_out, g.count(EVACS, STEPS.index(("values", n)) + 1))
                wait(dve, av_made, g.count(DUOS, PAIRS // 2 * (n + 1) - DUOS))
                flat = v_pad[:, 2 * n:2 * n + 2].rearrange("k c p e d -> k (c p) (e d)")
                for e in range(2):
                    src = v8[:, n].rearrange("k (cp e d) -> k cp e d", e=2, d=DH)[:, :, e]
                    last = dve.tensor_scalar(flat[:, :, 48 * e:48 * e + DH], src, -4.0, 3.0, ALU.max, ALU.min)
                last.then_inc(v_clip, 1)

            def clip(g, what):
                if what[0] == "rows":
                    clip_rows(g, *what[1:])
                else:
                    clip_values(g, what[1])

            def clip_heads(g, n):
                cols = slice(SEQ * n, SEQ * (n + 1))
                dve.wait_ge(heads_out, g.count(GI, n + 1))
                wait(dve, projected, g.count(NT, 0))
                dve.tensor_scalar(o_a[:, cols], o8_a[:, cols], -4.0, 3.0, ALU.max, ALU.min)
                dve.tensor_scalar(o_b[0:LO, cols], o8_b[:, cols], -4.0, 3.0, ALU.max,
                                  ALU.min).then_inc(heads_clip, 1)

            def residual(g, t):
                dve.wait_ge(projected, g.count(NT, t + 1))
                wait(dve, result, g.count(NT, t + 1 - 2 * NT))
                dve.tensor_tensor(h1[:, g.parity, t], proj_ps[0:TT, 0:EMBED], h0[:, g.parity, t],
                                  ALU.add).then_inc(dve_h1, 1)
                stats(g, t, h1, dve_h1, st3, dve_st3)

            def logits_evac(g, part):
                cols = part_cols(part)
                dve.wait_ge(routed, g.count(2, part + 1))
                wait(dve, logits_turned, g.count(2, part - 1))
                dve.tensor_scalar(logits_t[:, cols], route_ps[0:EXPERTS, 0:cols.stop - cols.start],
                                  br[:, :], None, ALU.add).then_inc(logits_out, 1)

            def choice(g, part):
                count = [8 * part]
                n, tiles = len(PARTS[part]), slice(PARTS[part][0], PARTS[part][-1] + 1)

                def step(ins):
                    count[0] += 1
                    ins.then_inc(choose, 1)
                    dve.wait_ge(choose, g.count(CHOICES, count[0]))

                def wide(ap):
                    return ap.rearrange("p (t e) -> p t e", e=1).broadcast_to([TT, n, EXPERTS])

                ramp = const_sb[0:TT, C_RAMP:C_RAMP + EXPERTS].rearrange("p (t e) -> p t e", t=1)
                dve.wait_ge(logits_turned, g.count(2, part + 1))
                step(dve.tensor_copy(logit[:, tiles].rearrange("p t e -> p (t e)"),
                                     route_ps[0:TT, 0:n * EXPERTS]))
                step(dve.tensor_reduce(top[:, tiles], logit[:, tiles], AX.X, ALU.max))
                wait(dve, pool_exp, g.count(2, part - 1))
                step(dve.tensor_tensor(below[:, tiles], logit[:, tiles], wide(top[:, tiles]), ALU.subtract))
                step(dve.tensor_scalar(score[:, tiles], below[:, tiles], 0.0, None, ALU.is_ge))
                step(dve.tensor_tensor(score2[:, tiles], score[:, tiles],
                                       ramp.broadcast_to([TT, n, EXPERTS]), ALU.mult))
                step(dve.tensor_reduce(best[:, tiles], score2[:, tiles], AX.X, ALU.max))
                step(dve.tensor_tensor(score[:, tiles], score2[:, tiles], wide(best[:, tiles]),
                                       ALU.is_equal))
                wait(dve, spread, g.count(2, part - 1))
                src = score[:, tiles].rearrange("p t (a e) -> p t a e", a=1).broadcast_to([TT, n, 3, EXPERTS])
                step(dve.tensor_copy(onehot3[:, tiles].rearrange("p t (a e) -> p t a e", a=3), src))
                assert count[0] == 8 * (part + 1)

            def spread_evac(g, part):
                cols = part_cols(part)
                width = cols.stop - cols.start
                dve.wait_ge(spread, g.count(2, part + 1))
                wait(dve, down_made, g.count(NT, 0))
                dve.tensor_copy(one_t[:, cols], route_ps[0:24, 0:width])
                dve.tensor_scalar(f_c[LO:LO + EXPERTS, g.parity, cols], route_ps[0:EXPERTS, 0:width], -1.0,
                                  None, ALU.add).then_inc(spread_out, 1)

            def sum_exp(g, part):
                tiles = slice(PARTS[part][0], PARTS[part][-1] + 1)
                dve.wait_ge(pool_exp, g.count(2, part + 1))
                dve.tensor_reduce(sume[:, tiles], expd[:, tiles], AX.X, ALU.add).then_inc(dve_sum, 1)
                dve.wait_ge(dve_sum, g.count(4, 2 * part + 1))
                dve.reciprocal(pmax[:, tiles], sume[:, tiles]).then_inc(dve_sum, 1)

            def finish(g, t):
                src = (proj_ps if t % 2 == 0 else wide_ps)[0:TT, 0:EMBED]
                half = (g.parity + t) % 2
                dve.wait_ge(down_made, g.count(NT, t + 1))
                if t == PARTS[part_of(t)][0]:
                    dve.wait_ge(dve_sum, g.count(4, 2 * part_of(t) + 2))
                earlier = (NT * g.offset + t) // 2
                value = 16 * earlier if isinstance(g.loop, int) else g.loop * (8 * NT) + 16 * earlier
                wait(dve, stored[half], value)
                dve.scalar_tensor_tensor(out_sb[:, half], src, pmax[:, t:t + 1], h1[:, g.parity, t],
                                         ALU.mult, ALU.add).then_inc(result, 1)

            def body(*groups):
                one, two, three = groups
                for s in range(SLOTS + 1):
                    if one and is_first(one):
                        for step, slot in ((set_attention, SET_ATTENTION), (set_projection, SET_PROJECTION),
                                           (set_experts, SET_EXPERTS)):
                            if s == slot:
                                step()
                    if two and 0 < s < SLOTS and by_scalar_engine(s - 1):
                        quantise(two, s - 1)
                    for n, (k, t) in enumerate(TURNS):
                        if k != 1 and TURN3[t] % SLOTS == s - 1:
                            low(groups, n)
                    if one:
                        for t in at(STATS2, s):
                            stats(one, t, h0, pool_h0, st2, dve_st2)
                    for g, late in ((two, 0), (three, SLOTS)):
                        if g and s < SLOTS:
                            for t in at(RESID, s + late):
                                residual(g, t)
                    if one:
                        for t in at(STATS1, s):
                            stats1(one, t)
                    if s < SLOTS:
                        for g, t, _, _, st_sem, _ in aggregated(groups, s):
                            dve.wait_ge(st_sem, g.count(NT, t + 1))
                        if two and not by_scalar_engine(s):
                            quantise(two, s)
                        for g, t, st, mv, _, mv_sem in aggregated(groups, s):
                            dve.bn_aggr(mv[:, t], st[:, t]).then_inc(mv_sem, 1)
                    for t in at(DOWN, s - 1) if three else []:
                        finish(three, t)
                    if one and s - 1 in FIRST_STEPS:
                        clip(one, FIRST_STEPS[s - 1])
                    if one:
                        for t in at(BIAS1, s):
                            bias1(one, t)
                    if one:
                        for t in at(NORM2, s):
                            norm(groups, one, t, 1, h0, mv2, rs2, pool_rs2, xn2, dve_xn2)
                    for g, late in ((two, 0), (three, SLOTS)):
                        if g and s < SLOTS:
                            for t in at(NORM3, s + late):
                                norm(groups, g, t, 2, h1, mv3, rs3, pool_rs3, xn3, dve_xn3)
                    if three:
                        for part in at(SUMEXP, s):
                            sum_exp(three, part)
                    if two and s - 1 in SECOND_STEPS:
                        clip(two, SECOND_STEPS[s - 1])
                    if three:
                        for part in at(CHOOSE, s):
                            choice(three, part)
                    if three:
                        for part in at(SPREAD, s - DSPR):
                            spread_evac(three, part)
                    for g, late in ((two, 0), (three, SLOTS)):
                        if g and s < SLOTS:
                            for n in at(HEADS_EVAC, s + late - 1):
                                clip_heads(g, n)
                    if three:
                        for part in at(ROUTE, s - DLOG):
                            logits_evac(three, part)
                    for n, (k, t) in enumerate(TURNS):
                        if k == 1 and TURN2[t] == s - DLOW1:
                            low(groups, n)

            passes(dve, body)


_INS = ["x", "tok_w", "tok_b", "ln_w", "ln_b", "w_qkv", "w_proj", "b_proj", "s_q", "s_k", "s_v", "s_attn",
        "s_after", "enc_w", "enc_b", "sw_w", "sw_b", "w1", "b1", "w2", "b2", "const"]


def kernel(x, L0_tok_W, L0_tok_b, L0_tok_ln_w, L0_tok_ln_b, L0_attn_Wqkv, L0_attn_Wproj, L0_attn_bproj,
           L0_attn_s_q, L0_attn_s_k, L0_attn_s_v, L0_attn_s_attn, L0_attn_s_after, L0_ffn_enc_w,
           L0_ffn_enc_b, L0_ffn_sw_w, L0_ffn_sw_b, L0_ffn_w1, L0_ffn_b1, L0_ffn_w2, L0_ffn_b2):
    import numpy as _np
    import concourse.bacc as _bacc
    from concourse import mybir as _mybir
    from concourse.bass_utils import run_bass_kernel_spmd as _run

    a = _np.asarray(x).reshape(GROUPS, GI, 3, GRID, PATCH, GRID, PATCH)
    a = a.transpose(0, 1, 3, 5, 2, 4, 6).reshape(GROUPS, NT, TT, KC, 128).transpose(0, 1, 4, 3, 2)
    wq = _np.asarray(L0_attn_Wqkv)
    q, k, v = wq[0:EMBED], wq[EMBED:2 * EMBED], wq[2 * EMBED:]
    rows = _np.concatenate([q[:128], k[:128], q[128:], k[128:], v]).T
    arrays = dict(
        x=a, tok_w=_np.asarray(L0_tok_W).T.reshape(KC, 128, EMBED).transpose(1, 0, 2),
        tok_b=L0_tok_b, ln_w=L0_tok_ln_w, ln_b=L0_tok_ln_b, w_qkv=rows,
        w_proj=_np.asarray(L0_attn_Wproj).T, b_proj=L0_attn_bproj,
        s_q=_np.asarray(L0_attn_s_q).reshape(1), s_k=_np.asarray(L0_attn_s_k).reshape(1),
        s_v=_np.asarray(L0_attn_s_v).reshape(1), s_attn=_np.asarray(L0_attn_s_attn).reshape(1),
        s_after=_np.asarray(L0_attn_s_after).reshape(1),
        enc_w=_np.asarray(L0_ffn_enc_w).T, enc_b=L0_ffn_enc_b, sw_w=L0_ffn_sw_w, sw_b=L0_ffn_sw_b,
        w1=_np.asarray(L0_ffn_w1).transpose(1, 0, 2).reshape(EMBED, FF),
        b1=_np.asarray(L0_ffn_b1).reshape(FC, 128).T,
        w2=_np.asarray(L0_ffn_w2).reshape(FC, 128, EMBED).transpose(1, 0, 2),
        b2=L0_ffn_b2, const=constants())
    nc = _bacc.Bacc("TRN2", target_bir_lowering=False, num_devices=1)
    feeds, args = {}, []
    for name in _INS:
        feed = _np.ascontiguousarray(arrays[name])
        feeds[f"in_{name}"] = feed
        args.append(nc.dram_tensor(f"in_{name}", feed.shape, _mybir.dt.from_np(feed.dtype),
                                   kind="ExternalInput").ap())
    out = nc.dram_tensor("out", (GROUPS, NT, TT, EMBED), _mybir.dt.float32, kind="ExternalOutput").ap()
    vit_tower_kernel(nc, *args, out)
    result = _run(nc, [feeds], core_ids=[0])
    return result.results[0]["out"].reshape(IMAGES, SEQ, EMBED)
```

```python
import numpy as np
import concourse.bass as bass
import concourse.mybir as mybir
from contextlib import ExitStack

IMAGES, PATCH, GRID, EMBED, HEADS, EXPERTS, HIDDEN = 64, 16, 14, 192, 12, 8, 64
SEQ = GRID * GRID
FAN_IN = 3 * PATCH * PATCH
KC = FAN_IN // 128
GI = 4
GROUPS = IMAGES // GI
TOK = GI * SEQ
TT = 112
NT = TOK // TT
HALF = TOK // 2
KEYS = SEQ // 2
DH = EMBED // HEADS
PAIRS = HEADS // 2
SLOTS = GI * PAIRS
LO = EMBED - 128
FF = EXPERTS * HIDDEN
FC = FF // 128
EPS = 1e-5
MASKED = 2.0 ** 60
E4_STEP = 512.0

C_IDENT, C_RAMP, C_SEL = 0, TT, TT + EXPERTS
C_BOUND = C_SEL + FF
C_PART = C_BOUND + 4
C_FIRST = C_PART + 3
C_HALFNEG, C_E, C_EPS = (C_FIRST + TT + n for n in range(3))
C_ALL = C_EPS + 1


def constants():
    c = np.zeros((128, C_ALL), np.float32)
    c[:TT, C_IDENT:C_IDENT + TT] = np.eye(TT)
    c[:, C_RAMP:C_RAMP + EXPERTS] = EXPERTS - np.arange(EXPERTS)
    for e in range(EXPERTS):
        c[e, C_SEL + HIDDEN * e:C_SEL + HIDDEN * (e + 1)] = MASKED
    odd = (np.arange(128) // DH) % 2
    for n, (head, bound) in enumerate(((0, -4), (0, 3), (1, -4), (1, 3))):
        c[:, C_BOUND + n] = np.where(odd == head, bound, 0)
    for j in range(3):
        c[8 * j:8 * j + 8, C_PART + j] = 1
        c[8 * j, C_FIRST:C_FIRST + TT] = 1
    c[:, C_HALFNEG] = -0.5
    c[:, C_E] = np.e
    c[:, C_EPS] = EPS
    return c


class Group:

    def __init__(self, loop, offset, parity):
        self.loop, self.offset, self.parity = loop, offset, parity

    def count(self, per_group, k):
        return self.loop * per_group + (self.offset * per_group + k)


def stages(loop, offset, parity):
    found = []
    for back in range(3):
        n = offset - back
        there = not isinstance(loop, int) or 0 <= n < GROUPS
        found.append(Group(loop, n, (parity + back) % 2) if there else None)
    return found


def wait(eng, sem, value):
    if not isinstance(value, int) or value > 0:
        eng.wait_ge(sem, value)


LOOP_FROM, LOOP_TO = 4, 14


def passes(eng, body):
    for i in range(LOOP_FROM):
        body(*stages(0, i, i % 2))
    with eng.Fori(LOOP_FROM, LOOP_TO, 2) as i:
        body(*stages(i, 0, 0))
        body(*stages(i, 1, 1))
    for i in range(LOOP_TO, GROUPS + 2):
        body(*stages(0, i, i % 2))


EMBED_SPAN = [2, 2, 2, 3, 2, 3, 2]
EMBED_END = [sum(EMBED_SPAN[:t + 1]) - 1 for t in range(NT)]


def embeds_of(slot):
    for t, (span, end) in enumerate(zip(EMBED_SPAN, EMBED_END)):
        step = slot - (end + 1 - span)
        if 0 <= step < span:
            return [(t, j) for j in range(KC) if j * span // KC == step]
    return []


def at(slots, slot):
    return [t for t, s in enumerate(slots) if s == slot]


EVAC1 = [1, 3, 5, 8, 10, 13, 15]
STATS1 = [2, 4, 5, 9, 11, 15, 17]
JOIN1 = [3, 5, 7, 9, 11, 15, 17]
BIAS1 = [4, 6, 8, 10, 12, 16, 18]
NORM1 = [4, 7, 8, 10, 12, 16, 18]
STATS2 = [7, 9, 11, 13, 15, 19, 21]
JOIN2 = [7, 9, 11, 13, 15, 19, 21]
NORM2 = [8, 10, 12, 14, 16, 20, 22]
TURN2 = [10, 11, 13, 15, 17, 21, 23]
FIRST_STEPS = {
    17: ("rows", 0, 0), 18: ("rows", 1, 0), 21: ("rows", 2, 0),
    22: ("values", 0), 23: ("values", 1),
}
SECOND_STEPS = {
    0: ("rows", 0, 1), 1: ("rows", 1, 1), 2: ("rows", 2, 1),
    4: ("values", 2), 7: ("values", 3),
}
STEPS = list(FIRST_STEPS.values()) + list(SECOND_STEPS.values())
EVACS = len(STEPS)


def clips_until(m, half):
    return [x[1:] for x in STEPS if x[0] == "rows"].index((m, half)) + 1


AV_PAIRS = [range(0, 4), range(4, PAIRS)]
AVS = len(AV_PAIRS)
AV = [PAIRS * n + pairs[-1] + 2 for n in range(GI) for pairs in AV_PAIRS]
HEADS_EVAC = AV[AVS - 1::AVS]
RING = 8
PROJ = [14, 15, 16, 20, 21, 27, 29]
RESID = [15, 16, 17, 21, 22, 28, 29]
JOIN3 = [15, 17, 17, 21, 23, 29, 29]
NORM3 = [16, 18, 18, 22, 25, 30, 30]
TURN3 = [18, 20, 22, 24, 26, 30, 32]
PARTS = [range(0, 4), range(4, NT)]
ROUTE = [2, 10]
TURN_LOGITS = [4, 11]
CHOOSE = [4, 11]
SPREAD = [5, 12]
EXP = [4, 5, 6, 7, 12, 13, 14]
SUMEXP = [8, 17]
UP = [6, 6, 8, 9, 14, 15, 16, 17]
DOWN = [10, 11, 12, 13, 18, 19, 22]
CHOICES = 16


def part_cols(part):
    return slice(TT * PARTS[part][0], TT * (PARTS[part][-1] + 1))


def part_of(t):
    return 0 if t in PARTS[0] else 1


def vit_tower_kernel(nc, x, tok_w, tok_b, ln_w, ln_b, w_qkv, w_proj, b_proj, s_q, s_k, s_v, s_attn,
                     s_after, enc_w, enc_b, sw_w, sw_b, w1, b1, w2, b2, const, out):
    f32, f32r, bf16 = mybir.dt.float32, mybir.dt.float32r, mybir.dt.bfloat16
    u8, i8, f8 = mybir.dt.uint8, mybir.dt.int8, mybir.dt.float8e4
    ALU, ACT, AX = mybir.AluOpType, mybir.ActivationFunctionType, mybir.AxisListType
    ctx = ExitStack()
    with ctx:
        def sb(name, shape, dtype):
            return ctx.enter_context(nc.sbuf_tensor(name, shape, dtype))

        def pb(name, shape):
            return ctx.enter_context(nc.psum_tensor(name, shape, f32))

        def sem(name):
            return ctx.enter_context(nc.semaphore(name))

        const_sb = sb("const_sb", [128, C_ALL], f32)
        we = sb("we", [128, KC, EMBED], f32)
        lnw = sb("lnw", [TT, EMBED], f32)
        lnb = sb("lnb", [TT, EMBED], f32)
        raw_q_a = sb("raw_q_a", [128, 3 * EMBED], f32)
        raw_q_b = sb("raw_q_b", [128, 3 * EMBED], f32)
        raw_1_a = sb("raw_1_a", [128, FF], f32)
        raw_1_b = sb("raw_1_b", [128, FF], f32)
        raw_p_a = sb("raw_p_a", [128, EMBED], f32)
        raw_p_b = sb("raw_p_b", [LO + 1, EMBED], f32)
        raw_24 = sb("raw_24", [24, 2 * EMBED], f32)
        scratch_a = sb("scratch_a", [128, 2 * EMBED], f32)
        scratch_b = sb("scratch_b", [128, 2 * EMBED], f32)
        wq_hi_a = sb("wq_hi_a", [128, 576], f32r)
        wq_lo_a = sb("wq_lo_a", [128, 576], f32r)
        wq_hi_b = sb("wq_hi_b", [128, 576], f32r)
        wq_lo_b = sb("wq_lo_b", [128, 576], f32r)
        w1_hi_a = sb("w1_hi_a", [128, FF], f32r)
        w1_lo_a = sb("w1_lo_a", [128, FF], f32r)
        w1_hi_b = sb("w1_hi_b", [128, FF], f32r)
        w1_lo_b = sb("w1_lo_b", [LO + EXPERTS, FF], f32r)
        wr_hi_a = sb("wr_hi_a", [128, EXPERTS], f32r)
        wr_lo_a = sb("wr_lo_a", [128, EXPERTS], f32r)
        wr_hi_b = sb("wr_hi_b", [128, EXPERTS], f32r)
        wr_lo_b = sb("wr_lo_b", [128, EXPERTS], f32r)
        wr_f = sb("wr_f", [128, 2, EXPERTS], f32)
        encw = sb("encw", [HIDDEN, EMBED + LO], f32)
        encb = sb("encb", [HIDDEN, 1], f32)
        sww = sb("sww", [HIDDEN, EXPERTS], f32)
        swb = sb("swb", [EXPERTS, 1], f32)
        br = sb("br", [EXPERTS, 1], f32)
        w2_sb = sb("w2_sb", [128, FC, EMBED], f32)
        b1_sb = sb("b1_sb", [128, FC], f32)
        wp_a = sb("wp_a", [128, 3, EMBED], bf16)
        wp_b = sb("wp_b", [LO + 1, 3, EMBED], bf16)
        rows24 = sb("rows24", [24, 2, EMBED], bf16)
        parts24 = sb("parts24", [24, 3, 2 * EMBED], bf16)
        first24 = sb("first24", [24, TT], bf16)
        ident_b = sb("ident_b", [TT, TT], bf16)
        scal = sb("scal", [128, 5], f32)
        rec = sb("rec", [128, 5], f32)
        inv_rows = sb("inv_rows", [128, 3], f32)
        c_prob = sb("c_prob", [128, 1], f32)
        c_out = sb("c_out", [128, 1], f32)
        proj_scale = sb("proj_scale", [128, 1], f32)
        products = sb("products", [128, 2], f32)
        warm = sb("warm", [128, 1], f32)

        x_sb = sb("x_sb", [128, NT, KC, TT], f32)
        st1 = sb("st1", [TT, NT, 6], f32)
        mv1 = sb("mv1", [TT, NT, 2], f32)
        ve1 = sb("ve1", [TT, NT, 1], f32)
        rs1 = sb("rs1", [TT, NT, 1], f32)
        nb1 = sb("nb1", [TT, NT, 1], f32)
        st2 = sb("st2", [TT, NT, 6], f32)
        mv2 = sb("mv2", [TT, NT, 2], f32)
        ve2 = sb("ve2", [TT, NT, 1], f32)
        rs2 = sb("rs2", [TT, NT, 1], f32)
        st3 = sb("st3", [TT, NT, 6], f32)
        mv3 = sb("mv3", [TT, NT, 2], f32)
        ve3 = sb("ve3", [TT, NT, 1], f32)
        rs3 = sb("rs3", [TT, NT, 1], f32)
        y1 = sb("y1", [TT, 2, EMBED], f32)
        n1 = sb("n1", [TT, 2, EMBED], f32)
        m1 = sb("m1", [TT, 2, EMBED], f32)
        h0 = sb("h0", [TT, 2, NT, EMBED], f32)
        h1 = sb("h1", [TT, 2, NT, EMBED], f32)
        xn2 = sb("xn2", [TT, 2, EMBED], f32)
        xn3 = sb("xn3", [TT, 2, EMBED], f32)
        a_hi = sb("a_hi", [128, 2, TOK], f32r)
        a_lo = sb("a_lo", [128, 2, TOK], f32r)
        a_b = sb("a_b", [128, 2, TOK], f32r)
        f_hi = sb("f_hi", [128, 2, TOK], f32r)
        f_lo = sb("f_lo", [128, 2, TOK], f32r)
        f_b = sb("f_b", [128, 2, TOK], f32r)
        f_c = sb("f_c", [LO + EXPERTS, 2, TOK], f32r)
        rows8 = sb("rows8", [128, 3, TOK], i8)
        q_a = sb("q_a", [128, TOK], bf16)
        q_b = sb("q_b", [LO, TOK], bf16)
        k_a = sb("k_a", [128, 2, TOK], bf16)
        k_b = sb("k_b", [LO, 2, TOK], bf16)
        v8 = sb("v8", [KEYS, GI, 2 * EMBED], i8)
        v_pad = sb("v_pad", [KEYS, 2 * GI, PAIRS, 2, 32], bf16)
        relu8 = sb("relu8", [KEYS, 2, 2, 2 * SEQ], u8)
        prob = sb("prob", [KEYS, RING, 2, 2 * SEQ], u8)
        o8_a = sb("o8_a", [128, TOK], i8)
        o8_b = sb("o8_b", [LO, TOK], i8)
        o_a = sb("o_a", [128, TOK], bf16)
        o_b = sb("o_b", [LO + 1, TOK], bf16)
        logits_t = sb("logits_t", [EXPERTS, TOK], f32)
        logit = sb("logit", [TT, NT, EXPERTS], f32)
        below = sb("below", [TT, NT, EXPERTS], f32)
        econst = sb("econst", [TT, NT, EXPERTS], f32)
        expd = sb("expd", [TT, NT, EXPERTS], f32)
        top = sb("top", [TT, NT], f32)
        score = sb("score", [TT, NT, EXPERTS], f32)
        score2 = sb("score2", [TT, NT, EXPERTS], f32)
        best = sb("best", [TT, NT], f32)
        onehot3 = sb("onehot3", [TT, NT, 24], bf16)
        sume = sb("sume", [TT, NT], f32)
        pmax = sb("pmax", [TT, NT], f32)
        one_t = sb("one_t", [24, TOK], bf16)
        hid = sb("hid", [128, FC, TOK], f32)
        out_sb = sb("out_sb", [TT, 2, EMBED], f32)

        scores_ps = pb("scores_ps", [128, 2, 512])
        heads_ps = pb("heads_ps", [128, 512])
        embed_ps = pb("embed_ps", [128, 512])
        turn_ps = pb("turn_ps", [128, 512])
        wide_ps = pb("wide_ps", [128, 512])
        proj_ps = pb("proj_ps", [128, 512])
        route_ps = pb("route_ps", [128, 512])

        loaded = [sem(f"loaded{n}") for n in range(4)]
        set_dve = sem("set_dve")
        set_pe = sem("set_pe")
        set_pool = sem("set_pool")
        warmed = sem("warmed")
        x_in = [sem(f"x_in{t}") for t in range(NT)]
        embedded = sem("embedded")
        act_y = sem("act_y")
        dve_st1 = sem("dve_st1")
        dve_mv1 = sem("dve_mv1")
        pool_ve1 = sem("pool_ve1")
        pool_rs1 = sem("pool_rs1")
        dve_nb1 = sem("dve_nb1")
        act_n1 = sem("act_n1")
        pool_m1 = sem("pool_m1")
        pool_h0 = sem("pool_h0")
        dve_st2 = sem("dve_st2")
        dve_mv2 = sem("dve_mv2")
        pool_ve2 = sem("pool_ve2")
        pool_rs2 = sem("pool_rs2")
        dve_xn2 = sem("dve_xn2")
        turned = sem("turned")
        act_hi = sem("act_hi")
        dve_lo = sem("dve_lo")
        rows_made = sem("rows_made")
        rows_out = sem("rows_out")
        rows_clip = sem("rows_clip")
        v_clip = sem("v_clip")
        qk_made = sem("qk_made")
        act_relu = sem("act_relu")
        prob_out = sem("prob_out")
        av_made = sem("av_made")
        heads_out = sem("heads_out")
        heads_clip = sem("heads_clip")
        projected = sem("projected")
        dve_h1 = sem("dve_h1")
        dve_st3 = sem("dve_st3")
        dve_mv3 = sem("dve_mv3")
        pool_ve3 = sem("pool_ve3")
        pool_rs3 = sem("pool_rs3")
        dve_xn3 = sem("dve_xn3")
        routed = sem("routed")
        logits_out = sem("logits_out")
        logits_turned = sem("logits_turned")
        choose = sem("choose")
        pool_exp = sem("pool_exp")
        spread = sem("spread")
        spread_out = sem("spread_out")
        up_made = sem("up_made")
        gelu_out = sem("gelu_out")
        dve_sum = sem("dve_sum")
        down_made = sem("down_made")
        result = sem("result")
        stored = [sem(f"stored{p}") for p in range(2)]

        TURNS = []
        for s in range(SLOTS):
            TURNS += [(1, t) for t in at(TURN2, s)] + [(2, t) for t in at(TURN3, s)]
            TURNS += [(3, t) for t in at(TURN3, s + SLOTS)]

        class Turns:

            def before(self, groups, n):
                return self.value(groups) + sum(groups[TURNS[m][0] - 1] is not None for m in range(n))

            def value(self, groups):
                back, any_ = next((n, g) for n, g in enumerate(groups) if g is not None)
                if not isinstance(any_.loop, int):
                    late = sum(t >= SLOTS for t in TURN3)
                    return (any_.loop + (any_.offset + back)) * (2 * NT) - (NT + late)
                done = 0
                for i in range(any_.offset + back):
                    st = stages(0, i, i % 2)
                    done += sum(st[k - 1] is not None for k, _ in TURNS)
                return done

        turns = Turns()

        WIDE = [(s, 1, rows_out, EVACS, STEPS.index(x) + 1) for s, x in FIRST_STEPS.items()]
        WIDE += [(s, 2, rows_out, EVACS, STEPS.index(x) + 1) for s, x in SECOND_STEPS.items()]
        WIDE += [(s, 3, gelu_out, 8, n + 1) for n, s in enumerate(UP) if n % 2 == 0]
        WIDE += [(s, 3, result, NT, t + 1) for t, s in enumerate(DOWN) if t % 2]
        PROJECTED = [(s, 2, dve_h1, NT, t + 1) for t, s in enumerate(PROJ) if s < SLOTS]
        PROJECTED += [(s - SLOTS, 3, dve_h1, NT, t + 1) for t, s in enumerate(PROJ) if s >= SLOTS]
        PROJECTED += [(s, 3, result, NT, t + 1) for t, s in enumerate(DOWN) if t % 2 == 0]
        ROUTED = [(s, 3, logits_out, 2, n + 1) for n, s in enumerate(ROUTE)]
        ROUTED += [(s, 3, choose, CHOICES, 8 * n + 1) for n, s in enumerate(TURN_LOGITS)]
        ROUTED += [(s, 3, spread_out, 2, n + 1) for n, s in enumerate(SPREAD)]
        ROUTED += [(s, 3, gelu_out, 8, n + 1) for n, s in enumerate(UP) if n % 2]

        def empty(eng, users, groups, slot):
            users = sorted(users, key=lambda x: x[0])
            assert len({x[0] for x in users}) == len(users)
            back, g = next((n, g) for n, g in enumerate(groups) if g is not None)
            number, loop = g.offset + back, g.loop
            n = [x[0] for x in users].index(slot)
            while True:
                n -= 1
                if n < 0:
                    n, number = len(users) - 1, number - 1
                    groups = stages(loop, number, number % 2)
                    if isinstance(loop, int) and number < 0:
                        return
                _, stage, signal, per_group, k = users[n]
                if groups[stage - 1] is not None:
                    return wait(eng, signal, groups[stage - 1].count(per_group, k))

        block = ctx.enter_context(nc.Block())

        def column(ap, n):
            return ap.rearrange("(a b) -> a b", b=1)

        bias_loads = [(const_sb[:, :], const)]
        bias_loads += [(raw_24[8 * j:8 * j + 8, 0:EMBED], b2) for j in range(3)]
        bias_loads += [(raw_24[:, EMBED:2 * EMBED], tok_b.partition_broadcast(24))]
        embed_loads = [(we[:, :, :], tok_w),
                       (lnw[:, :], ln_w.partition_broadcast(TT)), (lnb[:, :], ln_b.partition_broadcast(TT))]
        attention_loads = [(scal[:, n:n + 1], s.partition_broadcast(128))
                           for n, s in enumerate((s_q, s_k, s_v, s_attn, s_after))]
        attention_loads += [
            (raw_q_a[:, :], w_qkv[0:128, :]),
            (raw_q_b[0:LO, :], w_qkv[128:EMBED, :]), (raw_q_b[LO:128, :], w_qkv[128:EMBED, :]),
            (raw_p_a[:, :], w_proj[0:128, :]), (raw_p_b[0:LO, :], w_proj[128:EMBED, :]),
            (raw_p_b[LO:LO + 1, :], b_proj.rearrange("(a b) -> a b", a=1)),
        ]
        expert_loads = [
            (encw[:, 0:EMBED], enc_w), (encw[:, EMBED:EMBED + LO], enc_w[:, 128:EMBED]),
            (encb[:, :], column(enc_b, HIDDEN)), (sww[:, :], sw_w), (swb[:, :], column(sw_b, EXPERTS)),
            (raw_1_a[:, :], w1[0:128, :]),
            (raw_1_b[0:LO, :], w1[128:EMBED, :]), (raw_1_b[LO:128, :], w1[128:EMBED, :]),
            (w2_sb[:, :, :], w2), (b1_sb[:, :], b1),
        ]
        all_loads = [bias_loads, embed_loads, attention_loads, expert_loads]
        SET_EMBED, SET_ATTENTION, SET_ALL = 9, 21, 49
        ROUTER_PRODUCT, PREPARE_PROJECTION, PREPARE_EXPERTS = 4, 4, 7

        def come(eng, *which):
            for n in which:
                eng.wait_ge(loaded[n], 16 * len(all_loads[n]))

        def is_first(g):
            return isinstance(g.loop, int) and g.offset == 0

        @block.sync
        def _(sync):
            def load_tile(g, t):
                wait(sync, embedded, g.count(NT, t + 1 - NT))
                src = x[g.loop + g.offset, t] if not isinstance(g.loop, int) else x[g.offset, t]
                sync.dma_start(x_sb[:, t], src).then_inc(x_in[t], 16)

            first = Group(0, 0, 0)
            def load(which, lot):
                for dst, src in lot:
                    sync.dma_start(dst, src).then_inc(loaded[which], 16)

            load_tile(first, 0)
            load(1, embed_loads[:1])
            load(0, bias_loads)
            load_tile(first, 1)
            load(1, embed_loads[1:])
            load(2, attention_loads)
            for t in range(2, NT):
                load_tile(first, t)
            load(3, expert_loads)

            def body(one, two, three):
                for s in range(SLOTS + 2):
                    if three:
                        for t in at(DOWN, s - 2):
                            sync.wait_ge(result, three.count(NT, t + 1))
                            row = three.loop + three.offset if not isinstance(three.loop, int) else three.offset
                            sync.dma_start(out[row, t], out_sb[:, (three.parity + t) % 2]).then_inc(
                                stored[(three.parity + t) % 2], 16)
                    if one:
                        for t in at(EMBED_END, s - 1):
                            if isinstance(one.loop, int) and one.offset == GROUPS - 1:
                                continue
                            nxt = Group(one.loop, one.offset + 1, 1 - one.parity)
                            load_tile(nxt, t)

            passes(sync, body)
            for p in range(2):
                sync.wait_ge(stored[p], 16 * (GROUPS * NT // 2))

        @block.tensor
        def _(pe):
            ident = const_sb[0:TT, C_IDENT:C_IDENT + TT]

            def router_product():
                come(pe, 3)
                pe.matmul(proj_ps[:, 0:EXPERTS], encw[:, 0:128], sww[:, :], start=True, stop=True)
                pe.matmul(proj_ps[:, EXPERTS:2 * EXPERTS], encw[:, 128:EMBED + LO], sww[:, :],
                          start=True, stop=True)
                pe.matmul(proj_ps[0:EXPERTS, 2 * EXPERTS:2 * EXPERTS + 1], sww[:, :], encb[:, :],
                          start=True, stop=True).then_inc(set_pe, 1)

            def split_product(dst, hi_a, lo_a, hi_b, lo_b, left, right_hi, right_lo, right_b, moving):
                terms = [(hi_a, right_hi), (hi_a, right_lo), (lo_a, right_hi), (hi_b, right_b),
                         (lo_b[0:LO], right_b[0:LO])]
                for n, (w, a) in enumerate(terms):
                    w, a = w[:, left], a
                    lhs, rhs = (a, w) if moving == "weights" else (w, a)
                    last = pe.matmul(dst, lhs, rhs, start=n == 0, stop=n == 4)
                return last

            def embed(g, t, j):
                dst = embed_ps[0:TT, 0:EMBED]
                if j == 0:
                    pe.wait_ge(x_in[t], g.count(16, 16))
                    wait(pe, act_y, g.count(NT, t))
                pe.matmul(dst, x_sb[:, t, j], we[:, j], start=j == 0, stop=False)
                if j == KC - 1:
                    if is_first(g) and t == 0:
                        pe.wait_ge(set_dve, SET_EMBED)
                    pe.matmul(dst, first24[:, :], rows24[:, 1], start=False, stop=True).then_inc(embedded, 1)

            def turn(groups, n):
                k, t = TURNS[n]
                g = groups[k - 1]
                if g is None:
                    return
                src, made = (xn2, dve_xn2) if k == 1 else (xn3, dve_xn3)
                pe.wait_ge(made, g.count(NT, t + 1))
                wait(pe, dve_lo, turns.before(groups, n))
                rows = src[:, (g.parity + t) % 2]
                pe.transpose(turn_ps[:, 0:TT], rows[:, 0:128], ident)
                pe.transpose(turn_ps[0:LO, TT:2 * TT], rows[:, 128:EMBED], ident).then_inc(turned, 1)

            def rows(g, m, half):
                tiles = 4 if half == 0 else NT
                last_turn = max(i for i, x in enumerate(TURNS) if x[0] == 1 and x[1] < tiles)
                need_split(g, last_turn)
                cols = slice(half * HALF, (half + 1) * HALF)
                split_product(wide_ps[:, 0:HALF], wq_hi_a, wq_lo_a, wq_hi_b, wq_lo_b,
                              slice(128 * m, 128 * m + 128), a_hi[:, g.parity, cols],
                              a_lo[:, g.parity, cols], a_b[:, g.parity, cols],
                              "activations").then_inc(rows_made, 1)

            def need_split(g, last_turn):
                pe.wait_ge(dve_lo, turns.before(stages(g.loop, g.offset, g.parity), last_turn + 1))

            def values(g, n):
                tiles = 4 if n < 2 else NT
                need_split(g, max(i for i, x in enumerate(TURNS) if x[0] == 1 and x[1] < tiles))
                for c in range(2):
                    cols = slice(n * SEQ + c * KEYS, n * SEQ + (c + 1) * KEYS)
                    last = split_product(wide_ps[0:KEYS, EMBED * c:EMBED * (c + 1)], wq_hi_a, wq_lo_a,
                                         wq_hi_b, wq_lo_b, slice(384, 576), a_hi[:, g.parity, cols],
                                         a_lo[:, g.parity, cols], a_b[:, g.parity, cols], "weights")
                last.then_inc(rows_made, 1)

            def step(groups, g, slot, what):
                empty(pe, WIDE, groups, slot)
                if what[0] == "rows":
                    rows(g, *what[1:])
                else:
                    values(g, what[1])

            def head_rows(pair):
                return ("a", 32 * pair) if pair < 4 else ("b", 32 * (pair - 4))

            def qk(g, u):
                n, place = divmod(u, PAIRS)
                pair, odd = place - place % 2, place % 2
                side, row = head_rows(pair)
                q, k = (q_a, k_a) if side == "a" else (q_b, k_b)
                if pair in (0, 4) and odd == 0:
                    m = 1 if side == "a" else 2
                    pe.wait_ge(rows_clip, g.count(6, clips_until(m, n // 2)))
                wait(pe, act_relu, g.count(SLOTS, u))
                for c in range(2):
                    for which in range(2):
                        rows = slice(row + 32 * which, row + 32 * which + 32)
                        keys = k[rows, odd, n * SEQ + c * KEYS:n * SEQ + (c + 1) * KEYS]
                        last = pe.matmul(scores_ps[0:KEYS, which, c * SEQ:(c + 1) * SEQ], keys,
                                         q[rows, n * SEQ:(n + 1) * SEQ], start=True, stop=True)
                last.then_inc(qk_made, 1)

            def av_ready(g, k):
                n, group = divmod(k, AVS)
                pe.wait_ge(prob_out, g.count(SLOTS, PAIRS * n + AV_PAIRS[group][-1] + 1))
                if group == 0:
                    pe.wait_ge(v_clip, g.count(GI, n + 1))
                    wait(pe, heads_out, g.count(GI, n))

            def av(g, k):
                n, group = divmod(k, AVS)
                for step in range(4):
                    odd, c = divmod(step, 2)
                    for pair in AV_PAIRS[group]:
                        side, row = head_rows(pair)
                        col = 0 if side == "a" else SEQ
                        u = PAIRS * n + pair - pair % 2 + odd
                        last = pe.matmul(heads_ps[row:row + 32, col:col + SEQ],
                                         v_pad[:, 2 * n + c, pair, odd],
                                         prob[:, u % RING, pair % 2, c * SEQ:(c + 1) * SEQ].bitcast(f8),
                                         start=step == 0, stop=step == 3)
                last.then_inc(av_made, 1)

            def project(groups, g, t):
                image = (TT * (t + 1) - 1) // SEQ
                pe.wait_ge(heads_clip, g.count(GI, image + 1))
                empty(pe, PROJECTED, groups, PROJ[t] % SLOTS)
                dst = proj_ps[0:TT, 0:EMBED]
                cols = slice(TT * t, TT * (t + 1))
                for j in range(3):
                    pe.matmul(dst, o_a[:, cols], wp_a[:, j], start=j == 0, stop=False)
                    last = pe.matmul(dst, o_b[:, cols], wp_b[:, j], start=False, stop=j == 2)
                last.then_inc(projected, 1)

            def route(groups, g, part):
                cols = part_cols(part)
                empty(pe, ROUTED, groups, ROUTE[part])
                need_split3(g, PARTS[part][-1] + 1)
                split_product(route_ps[0:EXPERTS, 0:cols.stop - cols.start], wr_hi_a, wr_lo_a, wr_hi_b,
                              wr_lo_b, slice(0, EXPERTS), f_hi[:, g.parity, cols],
                              f_lo[:, g.parity, cols], f_b[:, g.parity, cols],
                              "activations").then_inc(routed, 1)

            def need_split3(g, tiles):
                this = max([i for i, x in enumerate(TURNS) if x[0] == 3 and x[1] < tiles], default=None)
                if this is None:
                    this = max(i for i, x in enumerate(TURNS) if x[0] == 2 and x[1] < tiles)
                    i = g.offset + 1
                else:
                    i = g.offset + 2
                pe.wait_ge(dve_lo, turns.before(stages(g.loop, i, i % 2), this + 1))

            def turn_logits(groups, g, part):
                empty(pe, ROUTED, groups, TURN_LOGITS[part])
                for n, t in enumerate(PARTS[part]):
                    last = pe.matmul(route_ps[0:TT, EXPERTS * n:EXPERTS * (n + 1)],
                                     logits_t[:, TT * t:TT * (t + 1)], ident[0:EXPERTS, 0:EXPERTS],
                                     start=True, stop=True)
                last.then_inc(logits_turned, 1)

            def spread_choice(g, part):
                pe.wait_ge(choose, g.count(CHOICES, 8 * (part + 1)))
                for n, t in enumerate(PARTS[part]):
                    last = pe.matmul(route_ps[0:24, TT * n:TT * (n + 1)], onehot3[:, t], ident_b[:, :],
                                     start=True, stop=True)
                last.then_inc(spread, 1)

            def up(groups, g, n):
                part, m = divmod(n, FC)
                bank, users = (wide_ps, WIDE) if n % 2 == 0 else (route_ps, ROUTED)
                empty(pe, users, groups, UP[n])
                if m == 0:
                    pe.wait_ge(spread_out, g.count(2, part + 1))
                cols, left = part_cols(part), slice(128 * m, 128 * (m + 1))
                dst = bank[:, 0:cols.stop - cols.start]
                terms = [(w1_hi_a, f_hi), (w1_hi_a, f_lo), (w1_lo_a, f_hi), (w1_hi_b, f_b), (w1_lo_b, f_c)]
                for k, (w, a) in enumerate(terms):
                    last = pe.matmul(dst, w[:, left], a[:, g.parity, cols], start=k == 0, stop=k == 4)
                last.then_inc(up_made, 1)

            def down(groups, g, t):
                pe.wait_ge(gelu_out, g.count(8, 4 * (part_of(t) + 1)))
                bank, users = (proj_ps, PROJECTED) if t % 2 == 0 else (wide_ps, WIDE)
                empty(pe, users, groups, DOWN[t])
                dst, cols = bank[0:TT, 0:EMBED], slice(TT * t, TT * (t + 1))
                pe.matmul(dst, one_t[:, cols], rows24[:, 0], start=True, stop=False)
                for m in range(FC):
                    last = pe.matmul(dst, hid[:, m, cols], w2_sb[:, m], start=False, stop=m == FC - 1)
                last.then_inc(down_made, 1)

            come(pe, 0, 1)

            def body(*groups):
                one, two, three = groups
                for s in range(SLOTS):
                    if one and is_first(one) and s == min(FIRST_STEPS):
                        pe.wait_ge(set_dve, SET_ATTENTION)
                    if two and is_first(two) and s == ROUTER_PRODUCT:
                        router_product()
                    if two and is_first(two) and s == min(PROJ):
                        pe.wait_ge(set_dve, SET_ALL)
                    for g, late in ((two, 0), (three, SLOTS)):
                        if g:
                            for k in at(AV, s + late):
                                av_ready(g, k)
                    if two:
                        qk(two, s)
                    if three and s <= EMBED_END[-1]:
                        for n in at(UP, s):
                            up(groups, three, n)
                    for n, (k, t) in enumerate(TURNS):
                        if k != 1 and TURN3[t] % SLOTS == s:
                            turn(groups, n)
                    for n, (k, t) in enumerate(TURNS):
                        if k == 1 and TURN2[t] == s:
                            turn(groups, n)
                    if three:
                        for part in at(TURN_LOGITS, s):
                            turn_logits(groups, three, part)
                    if one and s in FIRST_STEPS:
                        step(groups, one, s, FIRST_STEPS[s])
                    work = embeds_of(s) if one else []
                    for t, j in work[:1]:
                        embed(one, t, j)
                    if three and s > EMBED_END[-1]:
                        for n in at(UP, s):
                            up(groups, three, n)
                    if three:
                        for part in at(ROUTE, s):
                            route(groups, three, part)
                    if two and s in SECOND_STEPS:
                        step(groups, two, s, SECOND_STEPS[s])
                    if three and s > EMBED_END[-1]:
                        for t in at(DOWN, s):
                            down(groups, three, t)
                    if three:
                        for part in at(SPREAD, s):
                            spread_choice(three, part)
                    for g, late in ((two, 0), (three, SLOTS)):
                        if g:
                            for t in at(PROJ, s + late):
                                project(groups, g, t)
                    for t, j in work[1:]:
                        embed(one, t, j)
                    for g, late in ((two, 0), (three, SLOTS)):
                        if g:
                            for k in at(AV, s + late):
                                av(g, k)
                    if three and s <= EMBED_END[-1]:
                        for t in at(DOWN, s):
                            down(groups, three, t)

            passes(pe, body)

        def reads_done(eng, g, k):
            if k == 1:
                wait(eng, rows_made, g.count(EVACS, -EVACS))
            else:
                wait(eng, up_made, g.count(8, -8))

        @block.scalar
        def _(act):
            act.wait_ge(set_pool, 1)
            act.activation(warm[:, :], warm[:, :], ACT.Gelu).then_inc(warmed, 1)

            def embed_evac(g, t):
                act.wait_ge(embedded, g.count(NT, t + 1))
                wait(act, act_n1, g.count(NT, t - 1))
                act.activation(y1[:, (g.parity + t) % 2], embed_ps[0:TT, 0:EMBED],
                               ACT.Copy).then_inc(act_y, 1)

            def norm1(g, t):
                half = (g.parity + t) % 2
                act.wait_ge(dve_nb1, g.count(NT, t + 1))
                wait(act, pool_m1, g.count(NT, t - 1))
                act.activation(n1[:, half], y1[:, half], ACT.Identity,
                               scale=rs1[:, t], bias=nb1[:, t]).then_inc(act_n1, 1)

            def high(groups, n):
                k, t = TURNS[n]
                g = groups[k - 1]
                if g is None:
                    return
                hi, both = (a_hi, a_b) if k == 1 else (f_hi, f_b)
                cols = slice(TT * t, TT * (t + 1))
                act.wait_ge(turned, turns.before(groups, n) + 1)
                if t == 0:
                    reads_done(act, g, k)
                act.activation(hi[:, g.parity, cols], turn_ps[:, 0:TT], ACT.Copy)
                last = act.activation(both[0:LO, g.parity, cols], turn_ps[0:LO, TT:2 * TT], ACT.Copy)
                if k != 1:
                    last = act.activation(f_c[0:LO, g.parity, cols], turn_ps[0:LO, TT:2 * TT], ACT.Copy)
                last.then_inc(act_hi, 1)

            def relu(g, u):
                act.wait_ge(qk_made, g.count(SLOTS, u + 1))
                wait(act, prob_out, g.count(SLOTS, u - 1))
                act.activation(relu8[:, u % 2], scores_ps[0:KEYS, :, 0:2 * SEQ], ACT.Relu,
                               scale=c_prob[0:KEYS, :]).then_inc(act_relu, 1)

            def step_evac(g, what):
                act.wait_ge(rows_made, g.count(EVACS, STEPS.index(what) + 1))
                if what[0] == "rows":
                    m, half = what[1:]
                    wait(act, rows_clip, g.count(6, clips_until(m, half) - 6))
                    act.activation(rows8[:, m, half * HALF:(half + 1) * HALF], wide_ps[:, 0:HALF],
                                   ACT.Identity, scale=inv_rows[:, m:m + 1]).then_inc(rows_out, 1)
                else:
                    n = what[1]
                    wait(act, v_clip, g.count(GI, n + 1 - GI))
                    act.activation(v8[:, n], wide_ps[0:KEYS, 0:2 * EMBED], ACT.Identity,
                                   scale=rec[0:KEYS, 2:3]).then_inc(rows_out, 1)

            def heads_evac(g, n):
                cols = slice(SEQ * n, SEQ * (n + 1))
                act.wait_ge(av_made, g.count(GI * AVS, AVS * (n + 1)))
                wait(act, heads_clip, g.count(GI, n + 1 - GI))
                act.activation(o8_a[:, cols], heads_ps[:, 0:SEQ], ACT.Identity, scale=c_out[:, :])
                act.activation(o8_b[:, cols], heads_ps[0:LO, SEQ:2 * SEQ], ACT.Identity,
                               scale=c_out[0:LO, :]).then_inc(heads_out, 1)

            def gelu(g, n):
                part, m = divmod(n, FC)
                bank = wide_ps if n % 2 == 0 else route_ps
                cols = part_cols(part)
                act.wait_ge(up_made, g.count(8, n + 1))
                if n == 0:
                    wait(act, down_made, g.count(NT, 0))
                act.activation(hid[:, m, cols], bank[:, 0:cols.stop - cols.start], ACT.Gelu,
                               bias=b1_sb[:, m:m + 1]).then_inc(gelu_out, 1)

            def body(*groups):
                one, two, three = groups
                for s in range(SLOTS):
                    for n, (k, t) in enumerate(TURNS):
                        if k == 1 and TURN2[t] == s:
                            high(groups, n)
                    if two:
                        relu(two, s)
                    if three:
                        for n in at(UP, s):
                            gelu(three, n)
                    if one:
                        for t in at(NORM1, s):
                            norm1(one, t)
                    if one and is_first(one) and s == min(FIRST_STEPS):
                        act.wait_ge(set_dve, SET_ATTENTION)
                    if two and is_first(two) and s == min(PROJ):
                        come(act, 3)
                    for n, (k, t) in enumerate(TURNS):
                        if k != 1 and TURN3[t] % SLOTS == s:
                            high(groups, n)
                    if one:
                        for t in at(EVAC1, s):
                            embed_evac(one, t)
                    if two and s in SECOND_STEPS:
                        step_evac(two, SECOND_STEPS[s])
                    if one and s in FIRST_STEPS:
                        step_evac(one, FIRST_STEPS[s])
                    for g, late in ((two, 0), (three, SLOTS)):
                        if g:
                            for n in at(HEADS_EVAC, s + late):
                                heads_evac(g, n)

            passes(act, body)

        @block.gpsimd
        def _(pool):
            pool.memset(warm[:, :], 0.0).then_inc(set_pool, 1)
            pool.memset(v_pad[:, :, :, :, :], 0.0).then_inc(set_pool, 1)
            come(pool, 0, 1)

            def rstd(g, t, mv_sem, mv, ve, rs, ve_sem, rs_sem):
                pool.wait_ge(mv_sem, g.count(NT, t + 1))
                pool.tensor_tensor(ve[:, t], mv[:, t, 1:2], const_sb[0:TT, C_EPS:C_EPS + 1],
                                   ALU.add).then_inc(ve_sem, 1)
                pool.wait_ge(ve_sem, g.count(NT, t + 1))
                pool.tensor_tensor(rs[:, t], ve[:, t], const_sb[0:TT, C_HALFNEG:C_HALFNEG + 1],
                                   ALU.pow).then_inc(rs_sem, 1)

            def power(g, t):
                part = part_of(t)
                if t == PARTS[part][0]:
                    pool.wait_ge(choose, g.count(CHOICES, 8 * part + 3))
                    wait(pool, dve_sum, g.count(4, 2 * part - 2))
                pool.tensor_tensor(expd[:, t], econst[:, t], below[:, t], ALU.pow).then_inc(pool_exp, 1)

            def affine(g, t):
                half = (g.parity + t) % 2
                pool.wait_ge(act_n1, g.count(NT, t + 1))
                pool.tensor_tensor(m1[:, half], n1[:, half], lnw[:, :], ALU.mult).then_inc(pool_m1, 1)
                pool.wait_ge(pool_m1, g.count(NT, t + 1))
                wait(pool, dve_h1, g.count(NT, t + 1 - 2 * NT))
                pool.tensor_tensor(h0[:, g.parity, t], m1[:, half], lnb[:, :], ALU.add).then_inc(pool_h0, 1)

            def body(*groups):
                one, two, three = groups
                for s in range(SLOTS):
                    if three:
                        for t in at(EXP, s):
                            power(three, t)
                    if two and is_first(two) and s == min(PROJ):
                        pool.wait_ge(set_dve, SET_ALL)
                    if one:
                        for t in at(JOIN1, s):
                            rstd(one, t, dve_mv1, mv1, ve1, rs1, pool_ve1, pool_rs1)
                    if one:
                        for t in at(JOIN2, s):
                            rstd(one, t, dve_mv2, mv2, ve2, rs2, pool_ve2, pool_rs2)
                    for g, late in ((two, 0), (three, SLOTS)):
                        if g:
                            for t in at(JOIN3, s + late):
                                rstd(g, t, dve_mv3, mv3, ve3, rs3, pool_ve3, pool_rs3)
                    if one:
                        for t in at(NORM1, s):
                            affine(one, t)

            passes(pool, body)

        @block.vector
        def _(dve):
            done = [0]

            def setup(ins):
                done[0] += 1
                ins.then_inc(set_dve, 1)
                dve.wait_ge(set_dve, done[0])

            def split_r(hi, lo, src):
                setup(dve.tensor_copy(hi, src))
                setup(dve.tensor_tensor(lo, src[0:lo.shape[0]], hi[0:lo.shape[0]].bitcast(f32), ALU.subtract))

            def split_b(parts, src, rest):
                setup(dve.tensor_copy(parts[0], src))
                setup(dve.tensor_tensor(rest, src, parts[0], ALU.subtract))
                setup(dve.tensor_copy(parts[1], rest))
                setup(dve.tensor_tensor(rest, rest, parts[1], ALU.subtract))
                setup(dve.tensor_copy(parts[2], rest))

            def set_embedding():
                come(dve, 0)
                bias_parts = [parts24[:, j] for j in range(3)]
                split_b(bias_parts, raw_24[:, :], scratch_a[0:24, :])
                setup(dve.tensor_scalar(scratch_b[0:24, :], bias_parts[0], const_sb[0:24, C_PART:C_PART + 1],
                                        None, ALU.mult))
                for j in (1, 2):
                    dst = scratch_b[0:24, :] if j == 1 else rows24[:, :, :].rearrange("p a b -> p (a b)")
                    setup(dve.scalar_tensor_tensor(dst, bias_parts[j],
                                                   const_sb[0:24, C_PART + j:C_PART + j + 1],
                                                   scratch_b[0:24, :], ALU.mult, ALU.add))
                setup(dve.tensor_copy(first24[:, :], const_sb[0:24, C_FIRST:C_FIRST + TT]))

            def set_attention():
                come(dve, 2)
                split_r(wq_hi_a[:, :], wq_lo_a[:, :], raw_q_a[:, :])
                split_r(wq_hi_b[:, :], wq_lo_b[:, :], raw_q_b[:, :])
                setup(dve.reciprocal(rec[:, :], scal[:, :]))
                setup(dve.tensor_copy(inv_rows[:, 0:2], rec[:, 0:2]))
                setup(dve.tensor_copy(inv_rows[0:LO, 2:3], rec[0:LO, 0:1]))
                setup(dve.tensor_copy(inv_rows[LO:128, 2:3], rec[LO:128, 1:2]))
                setup(dve.tensor_scalar(products[:, 0:1], scal[:, 0:1], scal[:, 1:2], DH ** -0.5 / SEQ,
                                        ALU.mult, ALU.mult))
                setup(dve.tensor_scalar(c_prob[:, :], products[:, 0:1], rec[:, 3:4], None, ALU.mult))
                setup(dve.tensor_scalar(products[:, 1:2], scal[:, 3:4], scal[:, 2:3], E4_STEP,
                                        ALU.mult, ALU.mult))
                setup(dve.tensor_scalar(c_out[:, :], products[:, 1:2], rec[:, 4:5], None, ALU.mult))

            def set_projection():
                setup(dve.tensor_copy(proj_scale[:, :], scal[:, 4:5]))
                setup(dve.memset(proj_scale[LO:LO + 1, :], 1.0))
                setup(dve.memset(o_b[LO:LO + 1, :], 1.0))
                for parts, src, scale in ((wp_a, raw_p_a, scal[:, 4:5]), (wp_b, raw_p_b, proj_scale[0:LO + 1])):
                    n = src.shape[0]
                    scaled, rest = scratch_a[0:n, 0:EMBED], scratch_b[0:n, 0:EMBED]
                    setup(dve.tensor_scalar(scaled, src[:, :], scale, None, ALU.mult))
                    split_b([parts[:, j] for j in range(3)], scaled, rest)

            def set_experts():
                come(dve, 3)
                split_r(w1_hi_a[:, :], w1_lo_a[:, :], raw_1_a[:, :])
                split_r(w1_hi_b[:, :], w1_lo_b[0:LO, :], raw_1_b[:, :])
                setup(dve.tensor_copy(w1_lo_b[LO:LO + EXPERTS, :], const_sb[0:EXPERTS, C_SEL:C_SEL + FF]))
                setup(dve.tensor_copy(ident_b[:, :], const_sb[0:TT, C_IDENT:C_IDENT + TT]))
                setup(dve.tensor_copy(econst[:, :, :].rearrange("p a b -> p (a b)"),
                                      const_sb[0:TT, C_E:C_E + 1].broadcast_to([TT, NT * EXPERTS])))
                dve.wait_ge(set_pe, 1)
                setup(dve.tensor_copy(wr_f[:, :, :].rearrange("p a b -> p (a b)"), proj_ps[:, 0:2 * EXPERTS]))
                setup(dve.tensor_scalar(br[:, :], proj_ps[0:EXPERTS, 2 * EXPERTS:2 * EXPERTS + 1], swb[:, :],
                                        None, ALU.add))
                split_r(wr_hi_a[:, :], wr_lo_a[:, :], wr_f[:, 0])
                split_r(wr_hi_b[:, :], wr_lo_b[:, :], wr_f[:, 1])
                assert done[0] == SET_ALL

            set_embedding()
            assert done[0] == SET_EMBED
            set_attention()
            assert done[0] == SET_ATTENTION
            dve.wait_ge(set_pool, 2)

            def stats1(g, t):
                half = (g.parity + t) % 2
                dve.wait_ge(act_y, g.count(NT, t + 1))
                dve.bn_stats(st1[:, t], y1[:, half]).then_inc(dve_st1, 1)

            def bias1(g, t):
                dve.wait_ge(pool_rs1, g.count(NT, t + 1))
                dve.scalar_tensor_tensor(nb1[:, t], mv1[:, t, 0:1], -1.0, rs1[:, t], ALU.mult,
                                         ALU.mult).then_inc(dve_nb1, 1)

            def stats(g, t, src, src_sem, st, st_sem):
                dve.wait_ge(src_sem, g.count(NT, t + 1))
                dve.bn_stats(st[:, t], src[:, g.parity, t]).then_inc(st_sem, 1)

            def aggregated(groups, s):
                one, two, three = groups
                found = [(one, t, st1, mv1, dve_st1, dve_mv1) for t in at(JOIN1, s)]
                found += [(one, t, st2, mv2, dve_st2, dve_mv2) for t in at(JOIN2, s)]
                for g, slot in ((two, s), (three, s + SLOTS)):
                    found += [(g, t, st3, mv3, dve_st3, dve_mv3) for t in at(JOIN3, slot)]
                return [x for x in found if x[0]]

            def norm(groups, g, t, k, src, mv, rs, rs_sem, dst, dst_sem):
                dve.wait_ge(rs_sem, g.count(NT, t + 1))
                wait(dve, turned, before_turn(groups, g, t - 2, k))
                dve.tensor_scalar(dst[:, (g.parity + t) % 2], src[:, g.parity, t], mv[:, t, 0:1], rs[:, t],
                                  ALU.subtract, ALU.mult).then_inc(dst_sem, 1)

            def before_turn(groups, g, t, k):
                back = 0
                if t < 0:
                    back, t = 1, t + NT
                if k == 1:
                    stage = 1
                else:
                    stage = 2 if TURN3[t] < SLOTS else 3
                n = TURNS.index((stage, t))
                i = g.offset + stage - 1 - back
                if isinstance(g.loop, int) and i < 0:
                    return 0
                if isinstance(g.loop, int) and g.offset - back < 0:
                    return 0
                return turns.before(stages(g.loop, i, i % 2), n + 1)

            def low(groups, n):
                k, t = TURNS[n]
                g = groups[k - 1]
                if g is None:
                    return
                hi, lo, both = (a_hi, a_lo, a_b) if k == 1 else (f_hi, f_lo, f_b)
                cols = slice(TT * t, TT * (t + 1))
                dve.wait_ge(act_hi, turns.before(groups, n) + 1)
                dve.tensor_tensor(lo[:, g.parity, cols], turn_ps[:, 0:TT],
                                  hi[:, g.parity, cols].bitcast(f32), ALU.subtract)
                dve.tensor_tensor(both[LO:128, g.parity, cols], turn_ps[0:LO, TT:2 * TT],
                                  both[0:LO, g.parity, cols].bitcast(f32), ALU.subtract).then_inc(dve_lo, 1)

            def quantise(g, u):
                image, pair = divmod(u - RING, PAIRS)
                wait(dve, av_made, g.count(GI * AVS, AVS * image + 1 + (pair not in AV_PAIRS[0])))
                dve.wait_ge(act_relu, g.count(SLOTS, u + 1))
                dve.tensor_scalar(prob[:, u % RING], relu8[:, u % 2], 7.0, None, ALU.min).then_inc(prob_out, 1)

            def bounds(n, odd):
                return [const_sb[n, C_BOUND + 2 * odd + b:C_BOUND + 2 * odd + b + 1] for b in range(2)]

            def clip_rows(g, m, half):
                cols = slice(half * HALF, (half + 1) * HALF)
                dve.wait_ge(rows_out, g.count(EVACS, STEPS.index(("rows", m, half)) + 1))
                wait(dve, qk_made, g.count(SLOTS, (half + 1) * SLOTS // 2 - SLOTS))
                if m == 0:
                    last = dve.tensor_scalar(q_a[:, cols], rows8[:, 0, cols], -4.0, 3.0, ALU.max, ALU.min)
                elif m == 1:
                    for odd in range(2):
                        low_, high_ = bounds(slice(0, 128), odd)
                        last = dve.tensor_scalar(k_a[:, odd, cols], rows8[:, 1, cols], low_, high_,
                                                 ALU.max, ALU.min)
                else:
                    dve.tensor_scalar(q_b[:, cols], rows8[0:LO, 2, cols], -4.0, 3.0, ALU.max, ALU.min)
                    for odd in range(2):
                        low_, high_ = bounds(slice(LO, 128), odd)
                        last = dve.tensor_scalar(k_b[:, odd, cols], rows8[LO:128, 2, cols], low_, high_,
                                                 ALU.max, ALU.min)
                last.then_inc(rows_clip, 1)

            def clip_values(g, n):
                dve.wait_ge(rows_out, g.count(EVACS, STEPS.index(("values", n)) + 1))
                wait(dve, av_made, g.count(GI * AVS, AVS * (n + 1 - GI)))
                flat = v_pad[:, 2 * n:2 * n + 2].rearrange("k c p e d -> k (c p) (e d)")
                for e in range(2):
                    src = v8[:, n].rearrange("k (cp e d) -> k cp e d", e=2, d=DH)[:, :, e]
                    last = dve.tensor_scalar(flat[:, :, 48 * e:48 * e + DH], src, -4.0, 3.0, ALU.max, ALU.min)
                last.then_inc(v_clip, 1)

            def clip(g, what):
                if what[0] == "rows":
                    clip_rows(g, *what[1:])
                else:
                    clip_values(g, what[1])

            def clip_heads(g, n):
                cols = slice(SEQ * n, SEQ * (n + 1))
                dve.wait_ge(heads_out, g.count(GI, n + 1))
                wait(dve, projected, g.count(NT, 0))
                dve.tensor_scalar(o_a[:, cols], o8_a[:, cols], -4.0, 3.0, ALU.max, ALU.min)
                dve.tensor_scalar(o_b[0:LO, cols], o8_b[:, cols], -4.0, 3.0, ALU.max,
                                  ALU.min).then_inc(heads_clip, 1)

            def residual(g, t):
                dve.wait_ge(projected, g.count(NT, t + 1))
                wait(dve, result, g.count(NT, t + 1 - 2 * NT))
                dve.tensor_tensor(h1[:, g.parity, t], proj_ps[0:TT, 0:EMBED], h0[:, g.parity, t],
                                  ALU.add).then_inc(dve_h1, 1)
                stats(g, t, h1, dve_h1, st3, dve_st3)

            def logits_evac(g, part):
                cols = part_cols(part)
                dve.wait_ge(routed, g.count(2, part + 1))
                wait(dve, logits_turned, g.count(2, part - 1))
                dve.tensor_scalar(logits_t[:, cols], route_ps[0:EXPERTS, 0:cols.stop - cols.start],
                                  br[:, :], None, ALU.add).then_inc(logits_out, 1)

            def choice(g, part):
                count = [8 * part]
                n, tiles = len(PARTS[part]), slice(PARTS[part][0], PARTS[part][-1] + 1)

                def step(ins):
                    count[0] += 1
                    ins.then_inc(choose, 1)
                    dve.wait_ge(choose, g.count(CHOICES, count[0]))

                def wide(ap):
                    return ap.rearrange("p (t e) -> p t e", e=1).broadcast_to([TT, n, EXPERTS])

                ramp = const_sb[0:TT, C_RAMP:C_RAMP + EXPERTS].rearrange("p (t e) -> p t e", t=1)
                dve.wait_ge(logits_turned, g.count(2, part + 1))
                step(dve.tensor_copy(logit[:, tiles].rearrange("p t e -> p (t e)"),
                                     route_ps[0:TT, 0:n * EXPERTS]))
                step(dve.tensor_reduce(top[:, tiles], logit[:, tiles], AX.X, ALU.max))
                wait(dve, pool_exp, g.count(NT, PARTS[part][-1] + 1 - NT))
                step(dve.tensor_tensor(below[:, tiles], logit[:, tiles], wide(top[:, tiles]), ALU.subtract))
                step(dve.tensor_scalar(score[:, tiles], below[:, tiles], 0.0, None, ALU.is_ge))
                step(dve.tensor_tensor(score2[:, tiles], score[:, tiles],
                                       ramp.broadcast_to([TT, n, EXPERTS]), ALU.mult))
                step(dve.tensor_reduce(best[:, tiles], score2[:, tiles], AX.X, ALU.max))
                step(dve.tensor_tensor(score[:, tiles], score2[:, tiles], wide(best[:, tiles]),
                                       ALU.is_equal))
                wait(dve, spread, g.count(2, part - 1))
                src = score[:, tiles].rearrange("p t (a e) -> p t a e", a=1).broadcast_to([TT, n, 3, EXPERTS])
                step(dve.tensor_copy(onehot3[:, tiles].rearrange("p t (a e) -> p t a e", a=3), src))
                assert count[0] == 8 * (part + 1)

            def spread_evac(g, part):
                cols = part_cols(part)
                width = cols.stop - cols.start
                dve.wait_ge(spread, g.count(2, part + 1))
                wait(dve, down_made, g.count(NT, 0))
                dve.tensor_copy(one_t[:, cols], route_ps[0:24, 0:width])
                dve.tensor_scalar(f_c[LO:LO + EXPERTS, g.parity, cols], route_ps[0:EXPERTS, 0:width], -1.0,
                                  None, ALU.add).then_inc(spread_out, 1)

            def sum_exp(g, part):
                tiles = slice(PARTS[part][0], PARTS[part][-1] + 1)
                dve.wait_ge(pool_exp, g.count(NT, PARTS[part][-1] + 1))
                dve.tensor_reduce(sume[:, tiles], expd[:, tiles], AX.X, ALU.add).then_inc(dve_sum, 1)
                dve.wait_ge(dve_sum, g.count(4, 2 * part + 1))
                dve.reciprocal(pmax[:, tiles], sume[:, tiles]).then_inc(dve_sum, 1)

            def finish(g, t):
                src = (proj_ps if t % 2 == 0 else wide_ps)[0:TT, 0:EMBED]
                half = (g.parity + t) % 2
                dve.wait_ge(down_made, g.count(NT, t + 1))
                if t == PARTS[part_of(t)][0]:
                    dve.wait_ge(dve_sum, g.count(4, 2 * part_of(t) + 2))
                earlier = (NT * g.offset + t) // 2
                value = 16 * earlier if isinstance(g.loop, int) else g.loop * (8 * NT) + 16 * earlier
                wait(dve, stored[half], value)
                dve.scalar_tensor_tensor(out_sb[:, half], src, pmax[:, t:t + 1], h1[:, g.parity, t],
                                         ALU.mult, ALU.add).then_inc(result, 1)

            def body(*groups):
                one, two, three = groups
                for s in range(SLOTS + 1):
                    for t in at(DOWN, s - 1) if three else []:
                        finish(three, t)
                    if one:
                        for t in at(STATS2, s):
                            stats(one, t, h0, pool_h0, st2, dve_st2)
                    if three:
                        for part in at(SPREAD, s):
                            spread_evac(three, part)
                    for n, (k, t) in enumerate(TURNS):
                        if k != 1 and TURN3[t] % SLOTS == s - 1:
                            low(groups, n)
                    for g, late in ((two, 0), (three, SLOTS)):
                        if g and s < SLOTS:
                            for t in at(RESID, s + late):
                                residual(g, t)
                    if one:
                        for t in at(STATS1, s):
                            stats1(one, t)
                    if three:
                        for part in at(SUMEXP, s):
                            sum_exp(three, part)
                    joined = aggregated(groups, s)
                    for n, (g, t, _, _, st_sem, _) in enumerate(joined):
                        if all(later[4] is not st_sem for later in joined[n + 1:]):
                            dve.wait_ge(st_sem, g.count(NT, t + 1))
                    if two and s > 0:
                        quantise(two, s - 1)
                    for g, t, st, mv, _, mv_sem in joined:
                        dve.bn_aggr(mv[:, t], st[:, t]).then_inc(mv_sem, 1)
                    if one:
                        for t in at(BIAS1, s):
                            bias1(one, t)
                    if three:
                        for part in at(CHOOSE, s):
                            choice(three, part)
                    if two and s - 1 in SECOND_STEPS:
                        clip(two, SECOND_STEPS[s - 1])
                    if two and is_first(two) and s == PREPARE_PROJECTION:
                        set_projection()
                    if two and is_first(two) and s == PREPARE_EXPERTS:
                        set_experts()
                    for g, late in ((two, 0), (three, SLOTS)):
                        if g and s < SLOTS:
                            for n in at(HEADS_EVAC, s + late - 1):
                                clip_heads(g, n)
                    if one:
                        for t in at(NORM2, s):
                            norm(groups, one, t, 1, h0, mv2, rs2, pool_rs2, xn2, dve_xn2)
                    if three:
                        for part in at(ROUTE, s):
                            logits_evac(three, part)
                    if one and s - 1 in FIRST_STEPS:
                        clip(one, FIRST_STEPS[s - 1])
                    for g, late in ((two, 0), (three, SLOTS)):
                        if g and s < SLOTS:
                            for t in at(NORM3, s + late):
                                norm(groups, g, t, 2, h1, mv3, rs3, pool_rs3, xn3, dve_xn3)
                    for n, (k, t) in enumerate(TURNS):
                        if k == 1 and TURN2[t] == s:
                            low(groups, n)

            passes(dve, body)


_INS = ["x", "tok_w", "tok_b", "ln_w", "ln_b", "w_qkv", "w_proj", "b_proj", "s_q", "s_k", "s_v", "s_attn",
        "s_after", "enc_w", "enc_b", "sw_w", "sw_b", "w1", "b1", "w2", "b2", "const"]


def kernel(x, L0_tok_W, L0_tok_b, L0_tok_ln_w, L0_tok_ln_b, L0_attn_Wqkv, L0_attn_Wproj, L0_attn_bproj,
           L0_attn_s_q, L0_attn_s_k, L0_attn_s_v, L0_attn_s_attn, L0_attn_s_after, L0_ffn_enc_w,
           L0_ffn_enc_b, L0_ffn_sw_w, L0_ffn_sw_b, L0_ffn_w1, L0_ffn_b1, L0_ffn_w2, L0_ffn_b2):
    import numpy as _np
    import concourse.bacc as _bacc
    from concourse import mybir as _mybir
    from concourse.bass_utils import run_bass_kernel_spmd as _run

    a = _np.asarray(x).reshape(GROUPS, GI, 3, GRID, PATCH, GRID, PATCH)
    a = a.transpose(0, 1, 3, 5, 2, 4, 6).reshape(GROUPS, NT, TT, KC, 128).transpose(0, 1, 4, 3, 2)
    wq = _np.asarray(L0_attn_Wqkv)
    q, k, v = wq[0:EMBED], wq[EMBED:2 * EMBED], wq[2 * EMBED:]
    rows = _np.concatenate([q[:128], k[:128], q[128:], k[128:], v]).T
    arrays = dict(
        x=a, tok_w=_np.asarray(L0_tok_W).T.reshape(KC, 128, EMBED).transpose(1, 0, 2),
        tok_b=L0_tok_b, ln_w=L0_tok_ln_w, ln_b=L0_tok_ln_b, w_qkv=rows,
        w_proj=_np.asarray(L0_attn_Wproj).T, b_proj=L0_attn_bproj,
        s_q=_np.asarray(L0_attn_s_q).reshape(1), s_k=_np.asarray(L0_attn_s_k).reshape(1),
        s_v=_np.asarray(L0_attn_s_v).reshape(1), s_attn=_np.asarray(L0_attn_s_attn).reshape(1),
        s_after=_np.asarray(L0_attn_s_after).reshape(1),
        enc_w=_np.asarray(L0_ffn_enc_w).T, enc_b=L0_ffn_enc_b, sw_w=L0_ffn_sw_w, sw_b=L0_ffn_sw_b,
        w1=_np.asarray(L0_ffn_w1).transpose(1, 0, 2).reshape(EMBED, FF),
        b1=_np.asarray(L0_ffn_b1).reshape(FC, 128).T,
        w2=_np.asarray(L0_ffn_w2).reshape(FC, 128, EMBED).transpose(1, 0, 2),
        b2=L0_ffn_b2, const=constants())
    nc = _bacc.Bacc("TRN2", target_bir_lowering=False, num_devices=1)
    feeds, args = {}, []
    for name in _INS:
        feed = _np.ascontiguousarray(arrays[name])
        feeds[f"in_{name}"] = feed
        args.append(nc.dram_tensor(f"in_{name}", feed.shape, _mybir.dt.from_np(feed.dtype),
                                   kind="ExternalInput").ap())
    out = nc.dram_tensor("out", (GROUPS, NT, TT, EMBED), _mybir.dt.float32, kind="ExternalOutput").ap()
    vit_tower_kernel(nc, *args, out)
    result = _run(nc, [feeds], core_ids=[0])
    return result.results[0]["out"].reshape(IMAGES, SEQ, EMBED)
```
